# Optimizing a Trainium2 kernel written in Bass

```python
import numpy as np
import jax
import jax.numpy as jnp

def _softmax(x, axis=-1):
    return jax.nn.softmax(x, axis=axis)

def _gelu(x):
    return jax.nn.gelu(x, approximate=True)

def _silu(x):
    return jax.nn.silu(x)

def _sigmoid(x):
    return jax.nn.sigmoid(x)

def _layernorm(x, axis=-1, eps=1e-05):
    m = jnp.mean(x, axis=axis, keepdims=True)
    v = jnp.var(x, axis=axis, keepdims=True)
    return (x - m) / jnp.sqrt(v + eps)

def _scatter_add(tgt, idx, src, axis=0):
    return tgt.at[idx].add(src)

def _segment_sum(src, seg, n):
    return jax.ops.segment_sum(src, seg, n)
kernel_name = 'mk_macaron_d1_jaxref_r8_0fd1e1'

def setup_inputs(seed: int=0):
    np.random.seed(seed)
    _w = jnp.asarray

    def _L0_attn_setup():
        import jax, jax.numpy as jnp
        import numpy as np
        D_MODEL = 128
        N_HEADS = 16
        D_K = D_MODEL // N_HEADS
        key = jax.random.key(seed)
        ks = jax.random.split(key, 9)
        s = 1.0 / np.sqrt(D_MODEL)
        return {'x': jax.random.normal(ks[0], (4, 256, D_MODEL), dtype=jnp.float32), 'Wq': jax.random.normal(ks[1], (D_MODEL, D_MODEL), dtype=jnp.float32) * s, 'bq': jax.random.normal(ks[2], (D_MODEL,), dtype=jnp.float32) * 0.01, 'Wk': jax.random.normal(ks[3], (D_MODEL, D_MODEL), dtype=jnp.float32) * s, 'bk': jax.random.normal(ks[4], (D_MODEL,), dtype=jnp.float32) * 0.01, 'Wv': jax.random.normal(ks[5], (D_MODEL, D_MODEL), dtype=jnp.float32) * s, 'bv': jax.random.normal(ks[6], (D_MODEL,), dtype=jnp.float32) * 0.01, 'Wo': jax.random.normal(ks[7], (D_MODEL, D_MODEL), dtype=jnp.float32) * s, 'bo': jax.random.normal(ks[8], (D_MODEL,), dtype=jnp.float32) * 0.01}
    _L0_attn_in = _L0_attn_setup()

    def _L0_ffn_setup():
        import jax, jax.numpy as jnp
        import numpy as np
        E, D, H = (8, 128, 512)
        B, S = (4, 512)
        TEMPERATURE = 1.0
        key = jax.random.key(seed)
        ks = jax.random.split(key, 7)
        sc = 0.02
        return {'x': jax.random.normal(ks[0], (B, S, D), dtype=jnp.float32), 'W1': jax.random.normal(ks[1], (E, D, H), dtype=jnp.float32) * sc, 'b1': jax.random.normal(ks[2], (E, H), dtype=jnp.float32) * sc, 'W2': jax.random.normal(ks[3], (E, H, D), dtype=jnp.float32) * sc, 'b2': jax.random.normal(ks[4], (E, D), dtype=jnp.float32) * sc, 'Wr': jax.random.normal(ks[5], (D, E), dtype=jnp.float32) * sc, 'br': jax.random.normal(ks[6], (E,), dtype=jnp.float32) * sc}
    _L0_ffn_in = _L0_ffn_setup()
    _d = {'L0_attn_x': _L0_attn_in['x'], 'L0_attn_Wq': _L0_attn_in['Wq'], 'L0_attn_bq': _L0_attn_in['bq'], 'L0_attn_Wk': _L0_attn_in['Wk'], 'L0_attn_bk': _L0_attn_in['bk'], 'L0_attn_Wv': _L0_attn_in['Wv'], 'L0_attn_bv': _L0_attn_in['bv'], 'L0_attn_Wo': _L0_attn_in['Wo'], 'L0_attn_bo': _L0_attn_in['bo'], 'L0_ffn_W1': _L0_ffn_in['W1'], 'L0_ffn_b1': _L0_ffn_in['b1'], 'L0_ffn_W2': _L0_ffn_in['W2'], 'L0_ffn_b2': _L0_ffn_in['b2'], 'L0_ffn_Wr': _L0_ffn_in['Wr'], 'L0_ffn_br': _L0_ffn_in['br']}
    _x0 = _d['L0_attn_x']
    _d['L0_attn_x'] = jax.random.normal(jax.random.fold_in(jax.random.key(seed), 1), (4, 1024, 128), dtype=_x0.dtype)
    del _x0
    return _d

def reference(L0_attn_x, L0_attn_Wq, L0_attn_bq, L0_attn_Wk, L0_attn_bk, L0_attn_Wv, L0_attn_bv, L0_attn_Wo, L0_attn_bo, L0_ffn_W1, L0_ffn_b1, L0_ffn_W2, L0_ffn_b2, L0_ffn_Wr, L0_ffn_br):

    def _L0_attn_ref(x, Wq, bq, Wk, bk, Wv, bv, Wo, bo):
        import jax, jax.numpy as jnp
        import numpy as np
        D_MODEL = 128
        N_HEADS = 16
        D_K = D_MODEL // N_HEADS
        B, S, _ = x.shape
        q = (x @ Wq + bq).reshape(B, S, N_HEADS, D_K).transpose(0, 2, 1, 3)
        k = (x @ Wk + bk).reshape(B, S, N_HEADS, D_K).transpose(0, 2, 1, 3)
        v = (x @ Wv + bv).reshape(B, S, N_HEADS, D_K).transpose(0, 2, 1, 3)
        scale = 1.0 / np.sqrt(D_K).astype(np.float32)
        scores = jnp.einsum('bhsd,bhtd->bhst', q, k) * scale
        attn = jax.nn.softmax(scores, axis=-1)
        ctx = jnp.einsum('bhst,bhtd->bhsd', attn, v)
        ctx = ctx.transpose(0, 2, 1, 3).reshape(B, S, D_MODEL)
        return ctx @ Wo + bo

    def _L0_ffn_ref(x, W1, b1, W2, b2, Wr, br):
        import jax, jax.numpy as jnp
        import numpy as np
        E, D, H = (8, 128, 512)
        B, S = (4, 512)
        TEMPERATURE = 1.0
        routing_logits = (x @ Wr + br) / TEMPERATURE
        routing_probs = jax.nn.softmax(routing_logits, axis=-1)
        indices = jnp.argmax(routing_probs, axis=-1)
        out = jnp.zeros_like(x)
        num_experts = W1.shape[0]
        for i in range(num_experts):
            mask = (indices == i).astype(x.dtype)[..., None]
            xi = x * mask
            h = jax.nn.relu(xi @ W1[i] + b1[i])
            out = out + (h @ W2[i] + b2[i])
        return out
    x = L0_attn_x
    x = x + 0.5 * _L0_ffn_ref(_layernorm(x, axis=-1), L0_ffn_W1, L0_ffn_b1, L0_ffn_W2, L0_ffn_b2, L0_ffn_Wr, L0_ffn_br)
    x = x + _L0_attn_ref(_layernorm(x, axis=-1), L0_attn_Wq, L0_attn_bq, L0_attn_Wk, L0_attn_bk, L0_attn_Wv, L0_attn_bv, L0_attn_Wo, L0_attn_bo)
    x = x + 0.5 * _L0_ffn_ref(_layernorm(x, axis=-1), L0_ffn_W1, L0_ffn_b1, L0_ffn_W2, L0_ffn_b2, L0_ffn_Wr, L0_ffn_br)
    return x

_drawn_inputs = setup_inputs


def setup_inputs(seed=0):
    import zlib

    import numpy as np

    out = dict(_drawn_inputs(seed))
    spreads = {}
    factors = {'L0_attn_bq': 50.721,
     'L0_attn_bk': 64.0,
     'L0_attn_bv': 4.553,
     'L0_attn_bo': 5.256,
     'L0_ffn_b1': 3.297,
     'L0_ffn_br': 2.786}
    for name, (base, spread) in spreads.items():
        noise = np.random.default_rng([zlib.crc32(name.encode()), seed]).standard_normal(out[name].shape)
        drawn = base * np.exp(spread * noise) if base else spread * noise
        out[name] = jnp.asarray(drawn.astype(out[name].dtype))
    for name, factor in factors.items():
        out[name] = (out[name] * factor).astype(out[name].dtype)
    return out
```

```python
import concourse.bass as bass
from concourse import mybir
from contextlib import ExitStack

F32 = mybir.dt.float32
BF16 = mybir.dt.bfloat16
I32 = mybir.dt.int32
U32 = mybir.dt.uint32
ALU = mybir.AluOpType
ACT = mybir.ActivationFunctionType
AX = mybir.AxisListType

P = 128
BATCH, SEQ, D = 4, 1024, 128
TILES = BATCH * SEQ // P
QUAD = 4
QUADS = TILES // QUAD
HEADS, DK = 16, 8
EXPERTS, HID = 8, 512
HC = HID // P
SORTED = TILES + EXPERTS
PAIRS = SORTED // 2
EPS = 1e-5

GH = 4
GROUPS = BATCH * HEADS // GH
GPB = HEADS // GH
KT = SEQ // P
HALF = 512
PARTS = 3
ROWS = PARTS * PARTS * DK
MROWS = 2 * 2 * DK
STEPS = 2 * KT
P1_UNITS = 32
SCALE = float(DK) ** -0.5


def wait_unless_zero(engine, semaphore, count):
    if not (isinstance(count, int) and count == 0):
        engine.wait_ge(semaphore, count)


def layernorm(nc, dve, act, x_sb, xn_sb, stats, mv, rt, done, vsem, asem, half):
    if half == "act":
        act.wait_ge(vsem, 3)
        nc.scalar.activation(rt[:, 0, :], rt[:, 1, :], ACT.Sqrt).then_inc(asem, 1)
        return
    for t in range(TILES):
        last = nc.vector.bn_stats(stats[:, t, :], x_sb[:, t, :])
    last.then_inc(vsem, 1)
    dve.wait_ge(vsem, 1)
    for t in range(TILES):
        last = nc.vector.bn_aggr(mv[:, t, :], stats[:, t, :])
    last.then_inc(vsem, 1)
    dve.wait_ge(vsem, 2)
    nc.vector.tensor_scalar(rt[:, 1, :], mv[:, :, 1], EPS, None, ALU.add).then_inc(vsem, 1)
    dve.wait_ge(asem, 1)
    nc.vector.reciprocal(rt[:, 2, :], rt[:, 0, :]).then_inc(vsem, 1)
    dve.wait_ge(vsem, 4)
    nc.vector.tensor_tensor(rt[:, 3, :], rt[:, 2, :], rt[:, 2, :], ALU.mult).then_inc(vsem, 1)
    dve.wait_ge(vsem, 5)
    nc.vector.tensor_tensor(rt[:, 4, :], rt[:, 3, :], rt[:, 1, :], ALU.mult).then_inc(vsem, 1)
    dve.wait_ge(vsem, 6)
    nc.vector.tensor_scalar(rt[:, 5, :], rt[:, 4, :], -0.5, 1.5, ALU.mult, ALU.add).then_inc(vsem, 1)
    dve.wait_ge(vsem, 7)
    nc.vector.tensor_tensor(rt[:, 6, :], rt[:, 5, :], rt[:, 2, :], ALU.mult).then_inc(vsem, 1)
    dve.wait_ge(vsem, 8)
    for t in range(TILES):
        ins = nc.vector.tensor_scalar(xn_sb[:, t, :], x_sb[:, t, :], mv[:, t, 0:1], rt[:, 6, t:t + 1],
                                      ALU.subtract, ALU.mult)
        if t % QUAD == QUAD - 1:
            ins.then_inc(done, 1)


def constants(nc, w, dram):
    with ExitStack() as ctx:
        def sb(name, shape, dt):
            return ctx.enter_context(nc.sbuf_tensor(name, shape, dt))

        def sem(name):
            return ctx.enter_context(nc.semaphore(name))

        b1_rows = sb("b1_rows", [EXPERTS * HC, P], F32)
        b2_all = sb("b2_all", [P, EXPERTS, D], F32)
        relu_b1 = sb("relu_b1", [P, EXPERTS, HC], F32)
        idle = sb("idle", [P, EXPERTS, D], F32)
        total = sb("total", [P, D], F32)
        iota_i = sb("iota_i", [P, SORTED], I32)
        zeros = sb("zeros", [P, D], F32)
        ps_b1 = ctx.enter_context(nc.psum_tensor("ps_b1", [P, HALF], F32))
        ps_idle = ctx.enter_context(nc.psum_tensor("ps_idle", [P, EXPERTS, D], F32))
        small, big, xload, b1load, zeroed = sem("small"), sem("big"), sem("xload"), sem("b1load"), sem("zeroed")
        pool_step, dve_step, b1_t, idle_done = sem("pool_step"), sem("dve_step"), sem("b1_t"), sem("idle_done")

        with nc.Block() as block:
            @block.sync
            def _(sp):
                sp.dma_start(b1_rows[:, :], dram["L0_ffn_b1"].rearrange("e (c p) -> (e c) p", p=P)).then_inc(b1load, 16)
                sp.dma_start(w["x"][:, :, :], dram["L0_attn_x"].rearrange("b (t p) d -> p (b t) d", p=P)).then_inc(xload, 16)
                sp.dma_start(w["W2"][:, :, :, :], dram["L0_ffn_W2"].rearrange("e (c p) d -> p e c d", p=P)).then_inc(big, 16)
                sp.dma_start(w["W1"][:, :, :], dram["L0_ffn_W1"].rearrange("e d h -> d e h")).then_inc(big, 16)
                sp.wait_ge(dve_step, 1)
                sp.dma_start(dram["sorted_x"].rearrange("(t p) d -> p t d", p=P),
                             zeros[:, :].unsqueeze(1).to_broadcast([P, SORTED, D])).then_inc(zeroed, 16)
                sp.wait_ge(xload, 16)
                sp.wait_ge(zeroed, 16)

            @block.scalar
            def _(act):
                act.dma_start(b2_all[:, :, :], dram["L0_ffn_b2"].partition_broadcast(P)).then_inc(small, 16)
                for name, key in (("Wr", "L0_ffn_Wr"), ("Wq", "L0_attn_Wq"), ("Wk", "L0_attn_Wk"),
                                  ("Wv", "L0_attn_Wv"), ("Wo", "L0_attn_Wo")):
                    act.dma_start(w[name][:, :], dram[key]).then_inc(small, 16)
                for name, key in (("br", "L0_ffn_br"), ("bv", "L0_attn_bv"), ("bo", "L0_attn_bo")):
                    act.dma_start(w[name][:, :], dram[key].partition_broadcast(P)).then_inc(small, 16)
                for name, key in (("bq", "L0_attn_bq"), ("bk", "L0_attn_bk")):
                    act.dma_start(w[name][:, :], dram[key].rearrange("(p a) -> p a", a=1)).then_inc(small, 16)
                act.wait_ge(small, 16 * 11)

            @block.gpsimd
            def _(pool):
                nc.gpsimd.memset(w["ident"][:, :], 0.0).then_inc(pool_step, 1)
                nc.gpsimd.memset(w["before"][:, :], 0.0).then_inc(pool_step, 1)
                nc.gpsimd.memset(w["ones"][:, :], 1.0).then_inc(pool_step, 1)
                nc.gpsimd.iota(iota_i[:, :], [[1, SORTED]], base=0, channel_multiplier=0).then_inc(pool_step, 1)
                pool.wait_ge(pool_step, 4)
                nc.gpsimd.affine_select(out=w["ident"][:, :], in_=w["ident"][:, :], compare_op=ALU.not_equal, fill=1.0,
                                        base=0, pattern=[[-1, P]], channel_multiplier=1).then_inc(pool_step, 1)
                nc.gpsimd.affine_select(out=w["before"][:, :], in_=w["before"][:, :], compare_op=ALU.is_ge, fill=1.0,
                                        base=0, pattern=[[-1, P]], channel_multiplier=1).then_inc(pool_step, 1)

            @block.tensor
            def _(pe):
                pe.wait_ge(b1load, 16)
                pe.wait_ge(pool_step, 6)
                nc.tensor.transpose(ps_b1[:, 0:EXPERTS * HC], b1_rows[:, :],
                                    w["ident"][0:EXPERTS * HC, 0:EXPERTS * HC]).then_inc(b1_t, 1)
                pe.wait_ge(big, 32)
                pe.wait_ge(dve_step, 3)
                for e in range(EXPERTS):
                    for c in range(HC):
                        last = nc.tensor.matmul(ps_idle[:, e, :], relu_b1[:, e, c:c + 1].to_broadcast([P, P]),
                                                w["W2"][:, e, c, :], start=(c == 0), stop=(c == HC - 1))
                last.then_inc(idle_done, 1)

            @block.vector
            def _(dve):
                nc.vector.memset(zeros[:, :], 0.0).then_inc(dve_step, 1)
                dve.wait_ge(b1_t, 1)
                nc.vector.tensor_copy(w["b1T"][:, :, :].rearrange("p e c -> p (e c)"), ps_b1[:, 0:EXPERTS * HC]).then_inc(dve_step, 1)
                nc.vector.tensor_scalar(relu_b1[:, :, :].rearrange("p e c -> p (e c)"), ps_b1[:, 0:EXPERTS * HC],
                                        0.0, None, ALU.max).then_inc(dve_step, 1)
                dve.wait_ge(pool_step, 6)
                nc.vector.tensor_copy(w["iota"][:, :], iota_i[:, :])
                nc.vector.memset(w["seg"][:, :, :], 1.0).then_inc(dve_step, 1)
                dve.wait_ge(dve_step, 4)
                nc.vector.memset(w["seg"][:, :, 0:1], 0.0)
                nc.vector.tensor_scalar(w["rank8"][:, :], w["iota"][:, 0:EXPERTS], -1.0, float(EXPERTS), ALU.mult, ALU.add)
                dve.wait_ge(small, 16 * 11)
                dve.wait_ge(idle_done, 1)
                nc.vector.tensor_copy(idle[:, :, :], ps_idle[:, :, :]).then_inc(dve_step, 1)
                nc.vector.tensor_tensor(b2_all[:, :, :], ps_idle[:, :, :], b2_all[:, :, :], ALU.add).then_inc(dve_step, 1)
                dve.wait_ge(dve_step, 6)
                nc.vector.tensor_reduce(total[:, :], b2_all[:, :, :].rearrange("p e d -> p d e"), AX.X, ALU.add).then_inc(dve_step, 1)
                dve.wait_ge(dve_step, 7)
                nc.vector.tensor_tensor(w["rest"][:, :, :], total[:, :].unsqueeze(1).to_broadcast([P, EXPERTS, D]),
                                        idle[:, :, :], ALU.subtract).then_inc(dve_step, 1)


def ffn(nc, w, dram, tag, out):
    with ExitStack() as ctx:
        def sb(name, shape, dt):
            return ctx.enter_context(nc.sbuf_tensor(name + tag, shape, dt))

        def pb(name, shape):
            return ctx.enter_context(nc.psum_tensor(name + tag, shape, F32))

        def sem(name):
            return ctx.enter_context(nc.semaphore(name + tag))

        x_sb = w["x"]
        xn_sb = sb("xn", [P, TILES, D], F32)
        slot_i = sb("slot_i", [P, TILES], U32)
        expert_i = sb("expert_i", [1, SORTED], I32)

        with ExitStack() as sub:
            def sb2(name, shape, dt):
                return sub.enter_context(nc.sbuf_tensor(name + tag, shape, dt))

            def sem2(name):
                return sub.enter_context(nc.semaphore(name + tag))

            stats = sb2("stats", [P, TILES, 6], F32)
            mv = sb2("mv", [P, TILES, 2], F32)
            rt = sb2("rt", [P, 7, TILES], F32)
            xnT = sb2("xnT", [P, 2, QUAD * P], F32)
            logit = sb2("logit", [P, TILES, EXPERTS], F32)
            best = sb2("best", [P, TILES], F32)
            first = sb2("first", [P, TILES, EXPERTS], F32)
            ranked = sb2("ranked", [P, TILES, EXPERTS], F32)
            firstmax = sb2("firstmax", [P, TILES], F32)
            onehot = sb2("onehot", [P, TILES, EXPERTS], F32)
            onehot_b = sb2("onehot_b", [P, TILES, EXPERTS], BF16)
            count = sb2("count", [P, EXPERTS, TILES], F32)
            upto = sb2("upto", [P, EXPERTS, TILES], F32)
            cmp = sb2("cmp", [P, EXPERTS, TILES], F32)
            ntiles = sb2("ntiles", [P, EXPERTS], F32)
            end = sb2("end", [P, EXPERTS], F32)
            base = sb2("base", [P, EXPERTS], F32)
            place = sb2("place", [P, EXPERTS, TILES], F32)
            slot_f = sb2("slot_f", [P, TILES], F32)
            passed = sb2("passed", [1, SORTED, EXPERTS], F32)
            expert_f = sb2("expert_f", [1, SORTED], F32)
            ps_t = [sub.enter_context(nc.psum_tensor(f"ps_t{p}" + tag, [P, QUAD * P], F32)) for p in range(2)]
            ps_l = sub.enter_context(nc.psum_tensor("ps_l" + tag, [P, 2, TILES * EXPERTS], F32))
            ps_r = sub.enter_context(nc.psum_tensor("ps_r" + tag, [P, 2, TILES * EXPERTS], F32))
            vstep, astep, normed, routed = sem2("vstep"), sem2("astep"), sem2("normed"), sem2("routed")
            t_full, t_out, t_used, l_full = sem2("t_full"), sem2("t_out"), sem2("t_used"), sem2("l_full")
            r_full, slots, scattered = sem2("r_full"), sem2("slots"), sem2("scattered")

            with nc.Block() as block:
                @block.vector
                def _(dve):
                    layernorm(nc, dve, None, x_sb, xn_sb, stats, mv, rt, normed, vstep, astep, "dve")
                    dve.wait_ge(l_full, 1)
                    nc.vector.tensor_tensor(logit[:, :, :], ps_l[:, 0, :].rearrange("p (t e) -> p t e", e=EXPERTS),
                                            w["br"][:, :].unsqueeze(1).to_broadcast([P, TILES, EXPERTS]), ALU.add).then_inc(routed, 1)
                    dve.wait_ge(routed, 1)
                    nc.vector.tensor_reduce(best[:, :], logit[:, :, :], AX.X, ALU.max).then_inc(routed, 1)
                    dve.wait_ge(routed, 2)
                    nc.vector.tensor_tensor(first[:, :, :], logit[:, :, :], best[:, :].unsqueeze(2).to_broadcast([P, TILES, EXPERTS]),
                                            ALU.is_ge).then_inc(routed, 1)
                    dve.wait_ge(routed, 3)
                    nc.vector.tensor_tensor(ranked[:, :, :], first[:, :, :],
                                            w["rank8"][:, :].unsqueeze(1).to_broadcast([P, TILES, EXPERTS]), ALU.mult).then_inc(routed, 1)
                    dve.wait_ge(routed, 4)
                    nc.vector.tensor_reduce(firstmax[:, :], ranked[:, :, :], AX.X, ALU.max).then_inc(routed, 1)
                    dve.wait_ge(routed, 5)
                    nc.vector.tensor_tensor(onehot[:, :, :], ranked[:, :, :], firstmax[:, :].unsqueeze(2).to_broadcast([P, TILES, EXPERTS]),
                                            ALU.is_equal).then_inc(routed, 1)
                    dve.wait_ge(routed, 6)
                    nc.vector.tensor_copy(onehot_b[:, :, :], onehot[:, :, :]).then_inc(routed, 1)
                    dve.wait_ge(r_full, 1)
                    nc.vector.tensor_copy(count[:, :, :], ps_r[:, 1, :].rearrange("p (t e) -> p e t", e=EXPERTS)).then_inc(routed, 1)
                    dve.wait_ge(routed, 8)
                    nc.vector.tensor_tensor_scan(upto[:, :, :].rearrange("p e t -> p (e t)"), w["seg"][:, :, :].rearrange("p e t -> p (e t)"),
                                                 count[:, :, :].rearrange("p e t -> p (e t)"), 0.0, ALU.mult, ALU.add).then_inc(routed, 1)
                    dve.wait_ge(routed, 9)
                    nc.vector.scalar_tensor_tensor(out=cmp[:, :, :], in0=w["iota"][:, 0:TILES].unsqueeze(1).to_broadcast([P, EXPERTS, TILES]),
                                                   scalar=float(P), in1=upto[:, :, TILES - 1:TILES].to_broadcast([P, EXPERTS, TILES]),
                                                   op0=ALU.mult, op1=ALU.is_lt).then_inc(routed, 1)
                    dve.wait_ge(routed, 10)
                    nc.vector.tensor_reduce(ntiles[:, :], cmp[:, :, :], AX.X, ALU.add).then_inc(routed, 1)
                    dve.wait_ge(routed, 11)
                    nc.vector.tensor_tensor_scan(end[:, :], w["seg"][:, 0, 1:1 + EXPERTS], ntiles[:, :], 0.0, ALU.mult, ALU.add).then_inc(routed, 1)
                    dve.wait_ge(routed, 12)
                    nc.vector.tensor_tensor(base[:, :], end[:, :], ntiles[:, :], ALU.subtract).then_inc(routed, 1)
                    nc.vector.tensor_tensor(place[:, :, :], upto[:, :, :], count[:, :, :], ALU.subtract).then_inc(routed, 1)
                    nc.vector.tensor_tensor(passed[:, :, :], end[0:1, :].unsqueeze(1).to_broadcast([1, SORTED, EXPERTS]),
                                            w["iota"][0:1, :].unsqueeze(2).to_broadcast([1, SORTED, EXPERTS]), ALU.is_le).then_inc(routed, 1)
                    dve.wait_ge(routed, 15)
                    nc.vector.tensor_reduce(expert_f[:, :], passed[:, :, :], AX.X, ALU.add).then_inc(routed, 1)
                    nc.vector.scalar_tensor_tensor(out=cmp[:, :, :], in0=base[:, :].unsqueeze(2).to_broadcast([P, EXPERTS, TILES]),
                                                   scalar=float(P), in1=place[:, :, :], op0=ALU.mult, op1=ALU.add).then_inc(routed, 1)
                    dve.wait_ge(routed, 17)
                    nc.vector.tensor_scalar(expert_i[:, :], expert_f[:, :], float(EXPERTS - 1), None, ALU.min).then_inc(routed, 1)
                    nc.vector.tensor_tensor(place[:, :, :], cmp[:, :, :], ps_r[:, 0, :].rearrange("p (t e) -> p e t", e=EXPERTS),
                                            ALU.add).then_inc(routed, 1)
                    dve.wait_ge(routed, 19)
                    nc.vector.tensor_tensor(first[:, :, :], place[:, :, :].rearrange("p e t -> p t e"), onehot[:, :, :], ALU.mult).then_inc(routed, 1)
                    dve.wait_ge(routed, 20)
                    nc.vector.tensor_reduce(slot_f[:, :], first[:, :, :], AX.X, ALU.add).then_inc(routed, 1)
                    dve.wait_ge(routed, 21)
                    nc.vector.tensor_copy(slot_i[:, :], slot_f[:, :]).then_inc(slots, 1)

                @block.scalar
                def _(act):
                    layernorm(nc, None, act, x_sb, xn_sb, stats, mv, rt, normed, vstep, astep, "act")
                    for q in range(QUADS):
                        act.wait_ge(t_full, q + 1)
                        if q >= 2:
                            act.wait_ge(t_used, q - 1)
                        nc.scalar.activation(xnT[:, q % 2, :], ps_t[q % 2][:, :], ACT.Copy).then_inc(t_out, 1)

                @block.tensor
                def _(pe):
                    def logits(q):
                        pe.wait_ge(t_out, q + 1)
                        for i in range(QUAD):
                            t = QUAD * q + i
                            last = nc.tensor.matmul(ps_l[:, 0, t * EXPERTS:(t + 1) * EXPERTS], xnT[:, q % 2, i * P:(i + 1) * P],
                                                    w["Wr"][:, :], start=True, stop=True)
                        last.then_inc(t_used, 1)

                    for q in range(QUADS):
                        pe.wait_ge(normed, q + 1)
                        if q >= 2:
                            pe.wait_ge(t_out, q - 1)
                        for i in range(QUAD):
                            last = nc.tensor.transpose(ps_t[q % 2][:, i * P:(i + 1) * P], xn_sb[:, QUAD * q + i, :], w["ident"][:, :])
                        last.then_inc(t_full, 1)
                        if q >= 1:
                            logits(q - 1)
                    pe.wait_ge(t_out, QUADS)
                    for i in range(QUAD):
                        t = TILES - QUAD + i
                        last = nc.tensor.matmul(ps_l[:, 0, t * EXPERTS:(t + 1) * EXPERTS], xnT[:, (QUADS - 1) % 2, i * P:(i + 1) * P],
                                                w["Wr"][:, :], start=True, stop=True)
                    last.then_inc(l_full, 1)
                    pe.wait_ge(routed, 7)
                    chosen = onehot_b[:, :, :].rearrange("p t e -> p (t e)")
                    nc.tensor.matmul(ps_r[:, 0, :], w["before"][:, :], chosen, start=True, stop=True)
                    nc.tensor.matmul(ps_r[:, 1, :], w["ones"][:, :], chosen, start=True, stop=True).then_inc(r_full, 1)

                @block.gpsimd
                def _(pool):
                    pool.wait_ge(slots, 1)
                    for t in range(TILES):
                        nc.gpsimd.indirect_dma_start(dram["sorted_x"], bass.IndirectOffsetOnAxis(ap=slot_i[:, t:t + 1], axis=0),
                                                     xn_sb[:, t, :], None).then_inc(scattered, 16)
                    pool.wait_ge(scattered, 16 * TILES)

        with ExitStack() as sub:
            def sb2(name, shape, dt):
                return sub.enter_context(nc.sbuf_tensor(name + tag, shape, dt))

            def pair(name):
                return [sub.enter_context(nc.semaphore(f"{name}{p}" + tag)) for p in range(2)]

            xs = sb2("xs", [P, 2, D], F32)
            xsT = sb2("xsT", [P, 2, P], F32)
            w1s = sb2("w1s", [P, 2, HID], F32)
            b1s = sb2("b1s", [P, 2, HC], F32)
            hT = sb2("hT", [P, 2, HID], F32)
            ys = sb2("ys", [P, 2, D], F32)
            ps_x = [sub.enter_context(nc.psum_tensor(f"ps_x{p}" + tag, [P, HALF], F32)) for p in range(2)]
            ps_h = [[sub.enter_context(nc.psum_tensor(f"ps_h{p}{v}" + tag, [P, HALF], F32)) for v in range(2)] for p in range(2)]
            ps_y = [sub.enter_context(nc.psum_tensor(f"ps_y{p}" + tag, [P, HALF], F32)) for p in range(2)]
            x_in, x_t, xT_out, w1_in = pair("x_in"), pair("x_t"), pair("xT_out"), pair("w1_in")
            h_full, h_act, h_dve, y_full, y_out, y_stored = (pair(n) for n in ("h_full", "h_act", "h_dve", "y_full", "y_out", "y_stored"))

            with nc.Block() as block:
                @block.sync
                def _(sp):
                    def load(i, p):
                        sp.dma_start(xs[:, p, :], dram["sorted_x"][bass.ds((2 * i + p) * P, P), :]).then_inc(x_in[p], 16)

                    def store(i, p):
                        sp.wait_ge(y_out[p], i + 1)
                        sp.dma_start(dram["sorted_y"][bass.ds((2 * i + p) * P, P), :], ys[:, p, :]).then_inc(y_stored[p], 16)

                    load(0, 0)
                    load(0, 1)

                    def both(i):
                        for p in range(2):
                            sp.wait_ge(x_t[p], i + 1)
                            load(i + 1, p)
                        for p in range(2):
                            store(i, p)

                    both(0)
                    with sp.Fori(1, PAIRS - 1) as i:
                        both(i)
                    store(PAIRS - 1, 0)
                    store(PAIRS - 1, 1)
                    for p in range(2):
                        sp.wait_ge(y_stored[p], 16 * PAIRS)

                @block.gpsimd
                def _(pool):
                    def both(i):
                        for p in range(2):
                            e = pool.value_load(expert_i[0:1, bass.ds(2 * i + p, 1)], min_val=0, max_val=EXPERTS - 1)
                            wait_unless_zero(pool, h_full[p], i)
                            nc.gpsimd.tensor_copy(w1s[:, p, :], w["W1"][:, bass.ds(e, 1), :].rearrange("p a h -> p (a h)")).then_inc(w1_in[p], 1)
                            wait_unless_zero(pool, h_dve[p], i)
                            wait_unless_zero(pool, h_act[p], i)
                            nc.gpsimd.tensor_copy(b1s[:, p, :], w["b1T"][:, bass.ds(e, 1), :].rearrange("p a c -> p (a c)")).then_inc(w1_in[p], 1)

                    both(0)
                    with pool.Fori(1, PAIRS) as i:
                        both(i)

                @block.tensor
                def _(pe):
                    def turn(i, p):
                        pe.wait_ge(x_in[p], 16 * i + 16)
                        wait_unless_zero(pe, xT_out[p], i)
                        nc.tensor.transpose(ps_x[p][:, 0:P], xs[:, p, :], w["ident"][:, :]).then_inc(x_t[p], 1)

                    def up(i, p):
                        pe.wait_ge(xT_out[p], i + 1)
                        pe.wait_ge(w1_in[p], 2 * i + 2)
                        wait_unless_zero(pe, h_act[p], i)
                        wait_unless_zero(pe, h_dve[p], i)
                        for c in range(HC):
                            last = nc.tensor.matmul(ps_h[p][c // 2][:, (c % 2) * P:(c % 2 + 1) * P], w1s[:, p, c * P:(c + 1) * P],
                                                    xsT[:, p, :], start=True, stop=True)
                        last.then_inc(h_full[p], 1)

                    def down(i, p):
                        e = pe.value_load(expert_i[0:1, bass.ds(2 * i + p, 1)], min_val=0, max_val=EXPERTS - 1)
                        pe.wait_ge(h_act[p], i + 1)
                        pe.wait_ge(h_dve[p], i + 1)
                        wait_unless_zero(pe, y_out[p], i)
                        for c in range(HC):
                            last = nc.tensor.matmul(ps_y[p][:, 0:D], hT[:, p, c * P:(c + 1) * P],
                                                    w["W2"][:, bass.ds(e, 1), c, :].rearrange("p a d -> p (a d)"),
                                                    start=(c == 0), stop=(c == HC - 1))
                        last.then_inc(y_full[p], 1)

                    turn(0, 0)
                    up(0, 0)
                    turn(0, 1)

                    def both(i):
                        up(i, 1)
                        turn(i + 1, 0)
                        down(i, 0)
                        up(i + 1, 0)
                        turn(i + 1, 1)
                        down(i, 1)

                    both(0)
                    with pe.Fori(1, PAIRS - 1) as i:
                        both(i)
                    up(PAIRS - 1, 1)
                    down(PAIRS - 1, 0)
                    down(PAIRS - 1, 1)

                @block.scalar
                def _(act):
                    def turned(i, p):
                        act.wait_ge(x_t[p], i + 1)
                        wait_unless_zero(act, h_full[p], i)
                        nc.scalar.activation(xsT[:, p, :], ps_x[p][:, 0:P], ACT.Copy).then_inc(xT_out[p], 1)

                    def relu(i, p):
                        act.wait_ge(w1_in[p], 2 * i + 2)
                        act.wait_ge(h_full[p], i + 1)
                        wait_unless_zero(act, y_full[p], i)
                        for c in range(2):
                            last = nc.scalar.activation(hT[:, p, c * P:(c + 1) * P], ps_h[p][0][:, c * P:(c + 1) * P], ACT.Relu,
                                                        bias=b1s[:, p, c:c + 1])
                        last.then_inc(h_act[p], 1)

                    turned(0, 0)
                    relu(0, 0)
                    turned(0, 1)

                    def both(i):
                        relu(i, 1)
                        turned(i + 1, 0)
                        relu(i + 1, 0)
                        turned(i + 1, 1)

                    both(0)
                    with act.Fori(1, PAIRS - 1) as i:
                        both(i)
                    relu(PAIRS - 1, 1)

                @block.vector
                def _(dve):
                    def relu(i, p):
                        dve.wait_ge(w1_in[p], 2 * i + 2)
                        dve.wait_ge(h_full[p], i + 1)
                        wait_unless_zero(dve, y_full[p], i)
                        for c in range(2, HC):
                            last = nc.vector.tensor_scalar(hT[:, p, c * P:(c + 1) * P], ps_h[p][1][:, (c - 2) * P:(c - 1) * P],
                                                           b1s[:, p, c:c + 1], 0.0, ALU.add, ALU.max)
                        last.then_inc(h_dve[p], 1)

                    def result(i, p):
                        e = dve.value_load(expert_i[0:1, bass.ds(2 * i + p, 1)], min_val=0, max_val=EXPERTS - 1)
                        dve.wait_ge(y_full[p], i + 1)
                        wait_unless_zero(dve, y_stored[p], 16 * i)
                        nc.vector.tensor_tensor(ys[:, p, :], ps_y[p][:, 0:D],
                                                w["rest"][:, bass.ds(e, 1), :].rearrange("p a d -> p (a d)"), ALU.add).then_inc(y_out[p], 1)

                    relu(0, 0)

                    def both(i):
                        relu(i, 1)
                        result(i, 0)
                        relu(i + 1, 0)
                        result(i, 1)

                    both(0)
                    with dve.Fori(1, PAIRS - 1) as i:
                        both(i)
                    relu(PAIRS - 1, 1)
                    result(PAIRS - 1, 0)
                    result(PAIRS - 1, 1)

        with ExitStack() as sub:
            gathered = [sub.enter_context(nc.semaphore(f"gathered{q}" + tag)) for q in range(QUADS)]
            added, stored = (sub.enter_context(nc.semaphore(n + tag)) for n in ("added", "stored"))
            y_sb = xn_sb

            with nc.Block() as block:
                @block.gpsimd
                def _(pool):
                    for t in range(TILES):
                        nc.gpsimd.indirect_dma_start(y_sb[:, t, :], None, dram["sorted_y"],
                                                     bass.IndirectOffsetOnAxis(ap=slot_i[:, t:t + 1], axis=0)).then_inc(gathered[t // QUAD], 16)

                @block.vector
                def _(dve):
                    for q in range(QUADS):
                        dve.wait_ge(gathered[q], 16 * QUAD)
                        tiles = slice(q * QUAD, (q + 1) * QUAD)
                        nc.vector.scalar_tensor_tensor(out=x_sb[:, tiles, :], in0=y_sb[:, tiles, :], scalar=0.5,
                                                       in1=x_sb[:, tiles, :], op0=ALU.mult, op1=ALU.add).then_inc(added, 1)

                if out is not None:
                    @block.sync
                    def _(sp):
                        for q in range(QUADS):
                            sp.wait_ge(added, q + 1)
                            b, t = q * QUAD // KT, q * QUAD % KT
                            sp.dma_start(out[b, t * P:(t + QUAD) * P, :].rearrange("(t p) d -> p t d", p=P),
                                         x_sb[:, q * QUAD:(q + 1) * QUAD, :]).then_inc(stored, 16)
                        sp.wait_ge(stored, 16 * QUADS)


def project(nc, w, dram, v_sb):
    with ExitStack() as ctx:
        def sb(name, shape, dt):
            return ctx.enter_context(nc.sbuf_tensor(name, shape, dt))

        def banks(name):
            return [ctx.enter_context(nc.psum_tensor(f"{name}{p}", [P, HALF], F32)) for p in range(2)]

        def sem(name):
            return ctx.enter_context(nc.semaphore(name))

        xn_sb = sb("xn_a", [P, TILES, D], F32)
        stats, mv, rt = sb("stats_a", [P, TILES, 6], F32), sb("mv_a", [P, TILES, 2], F32), sb("rt_a", [P, 7, TILES], F32)
        xnT = sb("xnT_a", [P, 2, HALF], F32)
        exact = sb("exact", [P, 2, 2, HALF], F32)
        rem = sb("rem", [P, 2, 2, HALF], F32)
        parts = sb("parts", [P, 2, 2, PARTS, HALF], BF16)
        ps_t, ps_q, ps_k, ps_v = banks("ps_ta"), banks("ps_q"), banks("ps_k"), banks("ps_v")
        vstep, astep, normed = sem("vstep_a"), sem("astep_a"), sem("normed_a")
        t_full, t_out, qk_full, v_full = sem("t_full_a"), sem("t_out_a"), sem("qk_full"), sem("v_full")
        high, middle, left, low, v_out = sem("high"), sem("middle"), sem("left"), sem("low"), sem("v_out")
        stored = [sem(f"parts_stored{p}") for p in range(2)]

        with nc.Block() as block:
            @block.vector
            def _(dve):
                layernorm(nc, dve, None, w["x"], xn_sb, stats, mv, rt, normed, vstep, astep, "dve")
                for q in range(QUADS):
                    p = q % 2
                    if q >= 2:
                        dve.wait_ge(middle, 2 * q - 2)
                    for j in range(2):
                        dve.wait_ge(high, 4 * q + 2 * j + 2)
                        nc.vector.tensor_tensor(rem[:, p, j, :], exact[:, p, j, :], parts[:, p, j, 0, :], ALU.subtract).then_inc(left, 1)
                    dve.wait_ge(v_full, q + 1)
                    b, t = q * QUAD // KT, q * QUAD % KT
                    nc.vector.tensor_tensor(v_sb[:, b * GPB:(b + 1) * GPB, t:t + QUAD, :].rearrange("p g t c -> p t g c"),
                                            ps_v[p][:, :].rearrange("p (t g c) -> p t g c", t=QUAD, g=GPB),
                                            w["bv"][:, :].rearrange("p (g c) -> p g c", g=GPB).unsqueeze(1).to_broadcast([P, QUAD, GPB, GH * DK]),
                                            ALU.add).then_inc(v_out, 1)
                    for j in range(2):
                        dve.wait_ge(middle, 2 * q + j + 1)
                        nc.vector.tensor_tensor(parts[:, p, j, 2, :], rem[:, p, j, :], parts[:, p, j, 1, :], ALU.subtract).then_inc(low, 1)

            @block.tensor
            def _(pe):
                for q in range(QUADS):
                    p = q % 2
                    pe.wait_ge(normed, q + 1)
                    if q >= 2:
                        pe.wait_ge(t_out, q - 1)
                    for i in range(QUAD):
                        last = nc.tensor.transpose(ps_t[p][:, i * P:(i + 1) * P], xn_sb[:, QUAD * q + i, :], w["ident"][:, :])
                    last.then_inc(t_full, 1)
                    pe.wait_ge(t_out, q + 1)
                    if q >= 2:
                        pe.wait_ge(high, 4 * q - 4)
                        pe.wait_ge(v_out, q - 1)
                    nc.tensor.matmul(ps_q[p][:, :], w["Wq"][:, :], xnT[:, p, :], start=True, stop=True).then_inc(qk_full, 1)
                    nc.tensor.matmul(ps_k[p][:, :], w["Wk"][:, :], xnT[:, p, :], start=True, stop=True).then_inc(qk_full, 1)
                    for i in range(QUAD):
                        last = nc.tensor.matmul(ps_v[p][:, i * P:(i + 1) * P], xnT[:, p, i * P:(i + 1) * P], w["Wv"][:, :], start=True, stop=True)
                    last.then_inc(v_full, 1)

            @block.scalar
            def _(act):
                layernorm(nc, None, act, w["x"], xn_sb, stats, mv, rt, normed, vstep, astep, "act")
                for q in range(QUADS):
                    p = q % 2
                    act.wait_ge(t_full, q + 1)
                    if q >= 2:
                        act.wait_ge(v_full, q - 1)
                    nc.scalar.activation(xnT[:, p, :], ps_t[p][:, :], ACT.Copy).then_inc(t_out, 1)
                    for j, (bank, bias) in enumerate(((ps_q[p], w["bq"]), (ps_k[p], w["bk"]))):
                        act.wait_ge(qk_full, 2 * q + j + 1)
                        if q >= 2:
                            act.wait_ge(left, 2 * q - 2)
                            act.wait_ge(stored[p], 16 * 2 * PARTS * (q // 2))
                        nc.scalar.activation(exact[:, p, j, :], bank[:, :], ACT.Identity, bias=bias[:, 0:1]).then_inc(high, 1)
                        nc.scalar.activation(parts[:, p, j, 0, :], bank[:, :], ACT.Identity, bias=bias[:, 0:1]).then_inc(high, 1)
                    for j in range(2):
                        act.wait_ge(left, 2 * q + j + 1)
                        nc.scalar.activation(parts[:, p, j, 1, :], rem[:, p, j, :], ACT.Copy).then_inc(middle, 1)

            @block.sync
            def _(sp):
                for q in range(QUADS):
                    p = q % 2
                    b, t = q * QUAD // KT, q * QUAD % KT * P
                    sp.wait_ge(low, 2 * q + 2)
                    for j, key in enumerate(("q_parts", "k_parts")):
                        for n in range(PARTS):
                            sp.dma_start(dram[key][b * HEADS:(b + 1) * HEADS, n * DK:(n + 1) * DK, t:t + HALF],
                                         parts[:, p, j, n, :]).then_inc(stored[p], 16)
                for p in range(2):
                    sp.wait_ge(stored[p], 16 * 2 * PARTS * (QUADS // 2))


class Body:

    def __init__(self, g, par, use, half, extra):
        self.g, self.par, self.use, self.half, self.extra = g, par, use, half, extra

    def unit(self, n):
        n += self.extra
        return n % 2, self.half + n // 2

    def units_before(self):
        return self.half + (self.extra + 1) // 2, self.half + self.extra // 2


UNITS_0 = P1_UNITS + 2
UNITS = P1_UNITS + 3


def body_of(g, pair=None):
    if g == 0:
        return Body(0, 0, 0, P1_UNITS // 2, 0)
    if pair is None:
        pair = (g - 1) // 2
    half = (P1_UNITS + UNITS_0) // 2 + UNITS * pair
    return Body(1 + 2 * pair, 1, pair, half, 0) if g % 2 else Body(2 + 2 * pair, 0, pair + 1, half, UNITS)


LEAD = 6


def plan(first=False, last=False):
    lead = [("m", 0)] if last else [("max", 0), ("m", 0)] + [("max", n) for n in range(1, LEAD)]
    steps, n = [], LEAD
    for k in range(STEPS):
        upto = LEAD + (P1_UNITS - LEAD) * (k + 1) // STEPS
        here = [] if last else [("max", m) for m in range(n, upto)]
        n = upto
        if k == 2 and not first:
            here.append(("o", 1))
        if k == KT + 2:
            here.append(("o", 0))
        steps.append(here)
    return lead, steps


def attention(nc, w, dram, v_sb, ctx_sb):
    with ExitStack() as ctx:
        def sb(name, shape, dt):
            return ctx.enter_context(nc.sbuf_tensor(name, shape, dt))

        def sem(name):
            return ctx.enter_context(nc.semaphore(name))

        def sems(name):
            return [ctx.enter_context(nc.semaphore(f"{name}{p}")) for p in range(2)]

        q1, k1 = ([sb(f"{n}{p}", [P, SEQ], BF16) for p in range(2)] for n in ("q1_", "k1_"))
        q2, k2 = ([sb(f"{n}{p}", [P, GH, SEQ], BF16) for p in range(2)] for n in ("q2_", "k2_"))
        vs = [sb(f"vs{p}", [P, KT, GH, 32], F32) for p in range(2)]
        probs = sb("probs", [P, 2, GH, HALF], F32)
        oT = sb("oT", [P, HALF], F32)
        maxima = sb("maxima", [P, GH, KT, 2], F32)
        top = sb("top", [P, GH * KT], F32)
        mpart = [sb(f"mpart{p}", [GH * KT, PARTS, P], BF16) for p in range(2)]
        mrest = sb("mrest", [GH * KT, P], F32)
        rden = sb("rden", [P, 2, QUAD, GH, 1], F32)
        ps_m = [ctx.enter_context(nc.psum_tensor(f"ps_m{p}", [P, 2, HALF], F32)) for p in range(2)]
        ps_s = [ctx.enter_context(nc.psum_tensor(f"ps_s{n}", [P, HALF], F32)) for n in range(3)]
        ps_o = ctx.enter_context(nc.psum_tensor("ps_o", [P, HALF], F32))

        in1, in2, in_m, in_v = sems("in1_"), sems("in2_"), sems("in_m"), sems("in_v")
        unit_full, unit_free = sems("unit_full"), sems("unit_free")
        scored, exped, step_done, o_out = sem("scored"), sem("exped"), sem("step_done"), sem("o_out")
        combined, split, recip, preset = sem("combined"), sem("split"), sem("recip"), sem("preset")

        LOADS1, LOADS2 = 3 * GH, PARTS + PARTS * PARTS
        SPLITS = PARTS

        with nc.Block() as block:
            @block.sync
            def _(sp):
                def load1(g, par):
                    for j in range(GH):
                        head = bass.ds(g * GH + j, 1)
                        sp.dma_start(q1[par][MROWS * j:MROWS * (j + 1), :],
                                     dram["q_parts"][head, 0:2 * DK, :].to_broadcast([2, 2 * DK, SEQ])).then_inc(in1[par], 16)
                        for n in range(2):
                            row = MROWS * j + 2 * DK * n
                            sp.dma_start(k1[par][row:row + 2 * DK, :],
                                         dram["k_parts"][head, n * DK:(n + 1) * DK, :].to_broadcast([2, DK, SEQ])).then_inc(in1[par], 16)

                def load2(g, par):
                    heads = bass.ds(g * GH, GH)
                    for n in range(PARTS):
                        rows = slice(n * PARTS * DK, (n + 1) * PARTS * DK)
                        sp.dma_start(q2[par][rows, :, :], dram["q_parts"][heads, :, :].rearrange("j r t -> r j t")).then_inc(in2[par], 16)
                        for m in range(PARTS):
                            row = (n * PARTS + m) * DK
                            sp.dma_start(k2[par][row:row + DK, :, :],
                                         dram["k_parts"][heads, n * DK:(n + 1) * DK, :].rearrange("j d t -> d j t")).then_inc(in2[par], 16)

                def body(at, more1=True, more2=True, first=False):
                    g, par = at.g, at.par
                    sp.wait_ge(split, SPLITS * g + SPLITS)
                    sp.dma_start(dram["m_rows"][par, :, :, :], mpart[par][:, :, :]).then_inc(in_m[par], 16)
                    sp.wait_ge(in_m[par], 32 * at.use + 16)
                    sp.dma_start(q2[par][ROWS:ROWS + PARTS, :, :].rearrange("r j (t q) -> r (j t) q", q=P),
                                 dram["m_rows"][par, :, :, :].rearrange("a r q -> r a q")).then_inc(in_m[par], 16)
                    if more2:
                        if not first:
                            sp.wait_ge(step_done, STEPS * g)
                        load2(g + 1, 1 - par)
                    if more1:
                        load1(g + 2, par)

                load1(0, 0)
                load1(1, 1)
                sp.wait_ge(preset, 2)
                load2(0, 0)
                body(body_of(0), first=True)
                with sp.Fori(0, GROUPS // 2 - 2) as i:
                    body(body_of(1, i))
                    body(body_of(2, i))
                body(body_of(GROUPS - 3))
                body(body_of(GROUPS - 2), more1=False)
                body(body_of(GROUPS - 1), more1=False, more2=False)
                for p in range(2):
                    sp.wait_ge(in_m[p], 32 * (GROUPS // 2))

            @block.gpsimd
            def _(pool):
                for p in range(2):
                    nc.gpsimd.memset(k2[p][64:96, :, :], 1.0).then_inc(preset, 1)
                pool.wait_ge(preset, 2)
                for p in range(2):
                    nc.gpsimd.memset(vs[p][:, :, :, :], 1.0).then_inc(preset, 1)
                pool.wait_ge(preset, 4)

                def stage(g, par, first=False):
                    if not first:
                        pool.wait_ge(step_done, STEPS * (g - 1))
                    nc.gpsimd.tensor_copy(vs[par][:, :, :, 0:DK],
                                          v_sb[:, bass.ds(g, 1), :, :].rearrange("p a t (j d) -> p (a t) j d", d=DK)).then_inc(in_v[par], 1)

                stage(0, 0, first=True)
                stage(1, 1, first=True)
                with pool.Fori(0, GROUPS // 2 - 1) as i:
                    stage(2 * i + 2, 0)
                    stage(2 * i + 3, 1)

            @block.tensor
            def _(pe):
                def maxima_unit(slot, par, n):
                    qt, kh, pr = n // 4, n // 2 % 2, n % 2
                    for j in (2 * pr, 2 * pr + 1):
                        last = nc.tensor.matmul(ps_m[slot][:, j % 2, :], q1[par][MROWS * j:MROWS * (j + 1), qt * P:(qt + 1) * P],
                                                k1[par][MROWS * j:MROWS * (j + 1), kh * HALF:(kh + 1) * HALF], start=True, stop=True)
                    last.then_inc(unit_full[slot], 1)

                def result_unit(slot):
                    for i in range(QUAD):
                        last = nc.tensor.transpose(ps_m[slot][:, 0, i * P:(i + 1) * P], oT[:, i * P:(i + 1) * P], w["ident"][:, :])
                    last.then_inc(unit_full[slot], 1)

                def do_unit(at, n, kind, which):
                    slot, used = at.unit(n)
                    pe.wait_ge(unit_free[slot], used)
                    if kind == "max":
                        if which == 0:
                            pe.wait_ge(in1[1 - at.par], 16 * LOADS1 * (at.use + at.par + 1))
                        maxima_unit(slot, 1 - at.par, which)
                    elif kind == "m":
                        pe.wait_ge(combined, at.g + 1)
                        nc.tensor.transpose(ps_m[slot][0:GH * KT, 0, 0:P], top[:, :], w["ident"][:, :]).then_inc(unit_full[slot], 1)
                    else:
                        pe.wait_ge(o_out, 2 * at.g + 1 - which)
                        result_unit(slot)

                def score(at, k, j, first):
                    g, par = at.g, at.par
                    u, kt, n = k // KT, k % KT, GH * k + j
                    if n >= 3:
                        pe.wait_ge(exped, GH * STEPS * g + n - 2)
                    elif par == 1:
                        pe.wait_ge(exped, GH * STEPS * g + n - 2)
                    elif not first and n < 2:
                        pe.wait_ge(exped, GH * STEPS * g + n - 1)
                    nc.tensor.matmul(ps_s[(n + par) % 3][:, :], k2[par][0:ROWS + PARTS, j, kt * P:(kt + 1) * P],
                                     q2[par][0:ROWS + PARTS, j, u * HALF:(u + 1) * HALF], start=True, stop=True).then_inc(scored, 1)

                def values(at, k):
                    u, kt = k // KT, k % KT
                    if kt == 0:
                        wait_unless_zero(pe, o_out, 2 * at.g + u)
                    pe.wait_ge(exped, GH * STEPS * at.g + GH * (k + 1))
                    for j in range(GH):
                        last = nc.tensor.matmul(ps_o[32 * j:32 * (j + 1), :], vs[at.par][:, kt, j, :], probs[:, k % 2, j, :],
                                                start=(kt == 0), stop=(kt == KT - 1))
                    last.then_inc(step_done, 1)

                def body(at, first=False, last=False):
                    lead, steps = plan(first, last)
                    n = 0
                    for kind, which in lead:
                        do_unit(at, n, kind, which)
                        n += 1
                    pe.wait_ge(in2[at.par], 16 * LOADS2 * (at.use + 1))
                    pe.wait_ge(in_m[at.par], 32 * (at.use + 1))
                    pe.wait_ge(in_v[at.par], at.use + 1)
                    for k in range(STEPS + 1):
                        if k < STEPS:
                            for j in range(GH):
                                score(at, k, j, first)
                            for kind, which in steps[k]:
                                do_unit(at, n, kind, which)
                                n += 1
                        if k >= 1:
                            values(at, k - 1)

                pe.wait_ge(in1[0], 16 * LOADS1)
                for n in range(P1_UNITS):
                    if n >= 2:
                        pe.wait_ge(unit_free[n % 2], n // 2)
                    maxima_unit(n % 2, 0, n)
                body(body_of(0), first=True)
                with pe.Fori(0, GROUPS // 2 - 1) as i:
                    body(body_of(1, i))
                    body(body_of(2, i))
                body(body_of(GROUPS - 1), last=True)
                slot, used = body_of(GROUPS - 1).unit(3)
                pe.wait_ge(unit_free[slot], used)
                pe.wait_ge(o_out, 2 * GROUPS)
                result_unit(slot)

            @block.scalar
            def _(act):
                def take_out(half):
                    act.wait_ge(step_done, KT * half + KT)
                    wait_unless_zero(act, recip, half)
                    nc.scalar.activation(oT[:, :], ps_o[:, :], ACT.Copy).then_inc(o_out, 1)

                def body(at, first=False):
                    for k in range(STEPS):
                        if not (first and k < 2):
                            act.wait_ge(step_done, STEPS * at.g + k - 1)
                        for j in range(GH):
                            n = GH * k + j
                            act.wait_ge(scored, GH * STEPS * at.g + n + 1)
                            nc.scalar.activation(probs[:, k % 2, j, :], ps_s[(n + at.par) % 3][:, :], ACT.Exp, scale=SCALE).then_inc(exped, 1)
                        if k == 0 and not first:
                            take_out(2 * at.g - 1)
                        if k == KT:
                            take_out(2 * at.g)

                body(body_of(0), first=True)
                with act.Fori(0, GROUPS // 2 - 1) as i:
                    body(body_of(1, i))
                    body(body_of(2, i))
                body(body_of(GROUPS - 1))
                take_out(2 * GROUPS - 1)

            @block.vector
            def _(dve):
                def maxima_unit(slot, used, n):
                    qt, kh, pr = n // 4, n // 2 % 2, n % 2
                    dve.wait_ge(unit_full[slot], used + 1)
                    nc.vector.tensor_reduce(maxima[:, 2 * pr:2 * pr + 2, qt, kh], ps_m[slot][:, :, :], AX.X, ALU.max).then_inc(unit_free[slot], 1)

                def split_unit(at, slot, used):
                    dve.wait_ge(unit_full[slot], used + 1)
                    src, part = ps_m[slot][0:GH * KT, 0, 0:P], mpart[at.par]
                    nc.vector.tensor_scalar(part[:, 0, :], src, -1.0, None, ALU.mult).then_inc(split, 1)
                    dve.wait_ge(split, SPLITS * at.g + 1)
                    nc.vector.scalar_tensor_tensor(out=mrest[:, :], in0=src, scalar=-1.0, in1=part[:, 0, :],
                                                   op0=ALU.mult, op1=ALU.subtract).then_inc(unit_free[slot], 1)
                    dve.wait_ge(unit_free[slot], used + 1)
                    nc.vector.tensor_copy(part[:, 1, :], mrest[:, :]).then_inc(split, 1)
                    dve.wait_ge(split, SPLITS * at.g + 2)
                    nc.vector.tensor_tensor(part[:, 2, :], mrest[:, :], part[:, 1, :], ALU.subtract).then_inc(split, 1)

                def result_unit(g, u, slot, used):
                    dve.wait_ge(unit_full[slot], used + 1)
                    src = ps_m[slot][:, 0, :].rearrange("p (i j c) -> p i j c", i=QUAD, j=GH)
                    nc.vector.reciprocal(rden[:, u, :, :, :], src[:, :, :, DK:DK + 1]).then_inc(recip, 1)
                    dve.wait_ge(recip, 2 * g + u + 1)
                    nc.vector.tensor_tensor(ctx_sb[:, bass.ds(g, 1), u * QUAD:(u + 1) * QUAD, :].rearrange("p a t (j d) -> p (a t) j d", d=DK),
                                            src[:, :, :, 0:DK], rden[:, u, :, :, :].to_broadcast([P, QUAD, GH, DK]),
                                            ALU.mult).then_inc(unit_free[slot], 1)

                def do_unit(at, n, kind, which):
                    slot, used = at.unit(n)
                    if kind == "max":
                        maxima_unit(slot, used, which)
                    elif kind == "m":
                        split_unit(at, slot, used)
                    else:
                        result_unit(at.g - which, which, slot, used)

                def body(at, first=False, last=False):
                    for slot, used in enumerate(at.units_before()):
                        dve.wait_ge(unit_free[slot], used)
                    nc.vector.tensor_reduce(top[:, :], maxima[:, :, :, :].rearrange("p j t h -> p (j t) h"), AX.X, ALU.max).then_inc(combined, 1)
                    dve.wait_ge(combined, at.g + 1)
                    lead, steps = plan(first, last)
                    for n, (kind, which) in enumerate(lead + [x for here in steps for x in here]):
                        do_unit(at, n, kind, which)

                for n in range(P1_UNITS):
                    maxima_unit(n % 2, n // 2, n)
                body(body_of(0), first=True)
                with dve.Fori(0, GROUPS // 2 - 1) as i:
                    body(body_of(1, i))
                    body(body_of(2, i))
                body(body_of(GROUPS - 1), last=True)
                slot, used = body_of(GROUPS - 1).unit(3)
                result_unit(GROUPS - 1, 1, slot, used)


def output_projection(nc, w, ctx_sb):
    with ExitStack() as ctx:
        def banks(name):
            return [ctx.enter_context(nc.psum_tensor(f"{name}{p}", [P, HALF], F32)) for p in range(2)]

        def sem(name):
            return ctx.enter_context(nc.semaphore(name))

        cT = ctx.enter_context(nc.sbuf_tensor("cT", [P, 2, HALF], F32))
        rows = ctx.enter_context(nc.sbuf_tensor("ctx_rows", [P, 2, QUAD, D], F32))
        in_rows = sem("in_rows")
        plus_bo = ctx.enter_context(nc.sbuf_tensor("plus_bo", [P, 2, QUAD, D], F32))
        ps_c, ps_y = banks("ps_c"), banks("ps_yo")
        c_full, c_out, y_full, biased, added = sem("c_full"), sem("c_out"), sem("y_full_o"), sem("biased"), sem("added_o")

        with nc.Block() as block:
            @block.gpsimd
            def _(pool):
                for q in range(QUADS):
                    b, t = q * QUAD // KT, q * QUAD % KT
                    if q >= 2:
                        pool.wait_ge(c_full, q - 1)
                    nc.gpsimd.tensor_copy(rows[:, q % 2, :, :].rearrange("p t (g c) -> p t g c", g=GPB),
                                          ctx_sb[:, b * GPB:(b + 1) * GPB, t:t + QUAD, :].rearrange("p g t c -> p t g c")).then_inc(in_rows, 1)

            @block.tensor
            def _(pe):
                for q in range(QUADS):
                    p = q % 2
                    pe.wait_ge(in_rows, q + 1)
                    if q >= 2:
                        pe.wait_ge(c_out, q - 1)
                    for i in range(QUAD):
                        last = nc.tensor.transpose(ps_c[p][:, i * P:(i + 1) * P], rows[:, p, i, :], w["ident"][:, :])
                    last.then_inc(c_full, 1)
                    pe.wait_ge(c_out, q + 1)
                    if q >= 2:
                        pe.wait_ge(biased, q - 1)
                    for i in range(QUAD):
                        last = nc.tensor.matmul(ps_y[p][:, i * P:(i + 1) * P], cT[:, p, i * P:(i + 1) * P], w["Wo"][:, :], start=True, stop=True)
                    last.then_inc(y_full, 1)

            @block.scalar
            def _(act):
                for q in range(QUADS):
                    act.wait_ge(c_full, q + 1)
                    if q >= 2:
                        act.wait_ge(y_full, q - 1)
                    nc.scalar.activation(cT[:, q % 2, :], ps_c[q % 2][:, :], ACT.Copy).then_inc(c_out, 1)

            @block.vector
            def _(dve):
                for q in range(QUADS):
                    p, tiles = q % 2, slice(q * QUAD, (q + 1) * QUAD)
                    dve.wait_ge(y_full, q + 1)
                    nc.vector.tensor_tensor(plus_bo[:, p, :, :], ps_y[p][:, :].rearrange("p (t d) -> p t d", d=D),
                                            w["bo"][:, :].unsqueeze(1).to_broadcast([P, QUAD, D]), ALU.add).then_inc(biased, 1)
                    dve.wait_ge(biased, q + 1)
                    nc.vector.tensor_tensor(w["x"][:, tiles, :], w["x"][:, tiles, :], plus_bo[:, p, :, :], ALU.add).then_inc(added, 1)


def layer(nc, dram, out):
    with ExitStack() as ctx:
        def sb(name, shape, dt):
            return ctx.enter_context(nc.sbuf_tensor(name, shape, dt))

        w = {
            "x": sb("x", [P, TILES, D], F32),
            "W1": sb("W1", [P, EXPERTS, HID], F32), "W2": sb("W2", [P, EXPERTS, HC, D], F32),
            "b1T": sb("b1T", [P, EXPERTS, HC], F32), "rest": sb("rest", [P, EXPERTS, D], F32),
            "Wr": sb("Wr", [P, EXPERTS], F32), "br": sb("br", [P, EXPERTS], F32),
            "Wq": sb("Wq", [P, D], F32), "Wk": sb("Wk", [P, D], F32), "Wv": sb("Wv", [P, D], F32), "Wo": sb("Wo", [P, D], F32),
            "bq": sb("bq", [P, 1], F32), "bk": sb("bk", [P, 1], F32), "bv": sb("bv", [P, D], F32), "bo": sb("bo", [P, D], F32),
            "ident": sb("ident", [P, P], F32), "before": sb("before", [P, P], BF16), "ones": sb("ones", [P, P], BF16),
            "iota": sb("iota", [P, SORTED], F32), "rank8": sb("rank8", [P, EXPERTS], F32),
            "seg": sb("seg", [P, EXPERTS, TILES], F32),
        }
        constants(nc, w, dram)
        ffn(nc, w, dram, "_1", None)
        with ExitStack() as mid:
            ctx_sb = mid.enter_context(nc.sbuf_tensor("ctx_sb", [P, GROUPS, KT, GH * DK], F32))
            v_sb = mid.enter_context(nc.sbuf_tensor("v_sb", [P, GROUPS, KT, GH * DK], F32))
            project(nc, w, dram, v_sb)
            attention(nc, w, dram, v_sb, ctx_sb)
            output_projection(nc, w, ctx_sb)
        ffn(nc, w, dram, "_2", out)


_INS = ["L0_attn_x", "L0_attn_Wq", "L0_attn_bq", "L0_attn_Wk", "L0_attn_bk", "L0_attn_Wv", "L0_attn_bv", "L0_attn_Wo", "L0_attn_bo",
        "L0_ffn_W1", "L0_ffn_b1", "L0_ffn_W2", "L0_ffn_b2", "L0_ffn_Wr", "L0_ffn_br"]


def kernel(**inputs):
    import numpy as np
    import concourse.bacc as bacc
    from concourse.bass_utils import run_bass_kernel_spmd

    nc = bacc.Bacc("TRN2", target_bir_lowering=False, num_devices=1)
    arrays, dram = {}, {}
    for name in _INS:
        arrays[name] = np.ascontiguousarray(inputs[name])
        dram[name] = nc.dram_tensor(name, arrays[name].shape, F32, kind="ExternalInput").ap()
    dram["sorted_x"] = nc.dram_tensor("sorted_x", [SORTED * P, D], F32).ap()
    dram["sorted_y"] = nc.dram_tensor("sorted_y", [SORTED * P, D], F32).ap()
    dram["q_parts"] = nc.dram_tensor("q_parts", [BATCH * HEADS, PARTS * DK, SEQ], BF16).ap()
    dram["k_parts"] = nc.dram_tensor("k_parts", [BATCH * HEADS, PARTS * DK, SEQ], BF16).ap()
    dram["m_rows"] = nc.dram_tensor("m_rows", [2, GH * KT, PARTS, P], BF16).ap()
    out = nc.dram_tensor("out", [BATCH, SEQ, D], F32, kind="ExternalOutput").ap()
    layer(nc, dram, out)
    results = run_bass_kernel_spmd(nc, [arrays], core_ids=[0])
    return results.results[0]["out"]
```

```python
import concourse.bass as bass
from concourse import mybir
from contextlib import ExitStack

F32 = mybir.dt.float32
BF16 = mybir.dt.bfloat16
I32 = mybir.dt.int32
U32 = mybir.dt.uint32
ALU = mybir.AluOpType
ACT = mybir.ActivationFunctionType
AX = mybir.AxisListType

P = 128
BATCH, SEQ, D = 4, 1024, 128
TOKENS = BATCH * SEQ
TILES = TOKENS // P
QUAD = 4
QUADS = TILES // QUAD
HEADS, DK = 16, 8
EXPERTS, HID = 8, 512
HC = HID // P
SORTED = TILES + EXPERTS
ROTATION = 4
TURNS = SORTED // ROTATION
EPS = 1e-5

GH = 4
GROUPS = BATCH * HEADS // GH
GPB = HEADS // GH
KT = SEQ // P
HALF = 512
PARTS = 3
ROWS = PARTS * PARTS * DK
FILL = 96
BUFS = 3
STEPS = 2 * KT
P1_UNITS = 32
SCALE = float(DK) ** -0.5


def wait_unless_zero(engine, semaphore, count):
    if not (isinstance(count, int) and count == 0):
        engine.wait_ge(semaphore, count)


def layernorm(nc, dve, act, x_sb, xn_sb, stats, mv, rt, done, vsem, asem, half):
    if half == "act":
        act.wait_ge(vsem, 3)
        nc.scalar.activation(rt[:, 0, :], rt[:, 1, :], ACT.Sqrt).then_inc(asem, 1)
        return
    for t in range(TILES):
        last = nc.vector.bn_stats(stats[:, t, :], x_sb[:, t, :])
    last.then_inc(vsem, 1)
    dve.wait_ge(vsem, 1)
    for t in range(TILES):
        last = nc.vector.bn_aggr(mv[:, t, :], stats[:, t, :])
    last.then_inc(vsem, 1)
    dve.wait_ge(vsem, 2)
    nc.vector.tensor_scalar(rt[:, 1, :], mv[:, :, 1], EPS, None, ALU.add).then_inc(vsem, 1)
    dve.wait_ge(asem, 1)
    nc.vector.reciprocal(rt[:, 2, :], rt[:, 0, :]).then_inc(vsem, 1)
    dve.wait_ge(vsem, 4)
    nc.vector.tensor_tensor(rt[:, 3, :], rt[:, 2, :], rt[:, 2, :], ALU.mult).then_inc(vsem, 1)
    dve.wait_ge(vsem, 5)
    nc.vector.tensor_tensor(rt[:, 4, :], rt[:, 3, :], rt[:, 1, :], ALU.mult).then_inc(vsem, 1)
    dve.wait_ge(vsem, 6)
    nc.vector.tensor_scalar(rt[:, 5, :], rt[:, 4, :], -0.5, 1.5, ALU.mult, ALU.add).then_inc(vsem, 1)
    dve.wait_ge(vsem, 7)
    nc.vector.tensor_tensor(rt[:, 6, :], rt[:, 5, :], rt[:, 2, :], ALU.mult).then_inc(vsem, 1)
    dve.wait_ge(vsem, 8)
    for t in range(TILES):
        ins = nc.vector.tensor_scalar(xn_sb[:, t, :], x_sb[:, t, :], mv[:, t, 0:1], rt[:, 6, t:t + 1],
                                      ALU.subtract, ALU.mult)
        if t % QUAD == QUAD - 1:
            ins.then_inc(done, 1)


def constants(nc, w, dram):
    with ExitStack() as ctx:
        def sb(name, shape, dt):
            return ctx.enter_context(nc.sbuf_tensor(name, shape, dt))

        def sem(name):
            return ctx.enter_context(nc.semaphore(name))

        b1_rows = sb("b1_rows", [EXPERTS * HC, P], F32)
        b2_all = sb("b2_all", [P, EXPERTS, D], F32)
        relu_b1 = sb("relu_b1", [P, EXPERTS, HC], F32)
        idle = sb("idle", [P, EXPERTS, D], F32)
        total = sb("total", [P, D], F32)
        iota_i = sb("iota_i", [P, P], I32)
        partition_i = sb("partition_i", [P, 1], I32)
        ps_b1 = ctx.enter_context(nc.psum_tensor("ps_b1", [P, HALF], F32))
        ps_idle = ctx.enter_context(nc.psum_tensor("ps_idle", [P, EXPERTS, D], F32))
        small, big, xload, b1load = sem("small"), sem("big"), sem("xload"), sem("b1load")
        pool_step, dve_step, b1_t, idle_done = sem("pool_step"), sem("dve_step"), sem("b1_t"), sem("idle_done")

        with nc.Block() as block:
            @block.sync
            def _(sp):
                sp.dma_start(b1_rows[:, :], dram["L0_ffn_b1"].rearrange("e (c p) -> (e c) p", p=P)).then_inc(b1load, 16)
                sp.dma_start(w["x"][:, :, :], dram["L0_attn_x"].rearrange("b (t p) d -> p (b t) d", p=P)).then_inc(xload, 16)
                sp.dma_start(w["W2"][:, :, :, :], dram["L0_ffn_W2"].rearrange("e (c p) d -> p e c d", p=P)).then_inc(big, 16)
                sp.dma_start(w["W1"][:, :, 0:HID], dram["L0_ffn_W1"].rearrange("e d h -> d e h")).then_inc(big, 16)
                sp.wait_ge(xload, 16)

            @block.scalar
            def _(act):
                act.dma_start(b2_all[:, :, :], dram["L0_ffn_b2"].partition_broadcast(P)).then_inc(small, 16)
                for name, key in (("Wr", "L0_ffn_Wr"), ("Wq", "L0_attn_Wq"), ("Wk", "L0_attn_Wk"),
                                  ("Wv", "L0_attn_Wv"), ("Wo", "L0_attn_Wo")):
                    act.dma_start(w[name][:, :], dram[key]).then_inc(small, 16)
                for name, key in (("br", "L0_ffn_br"), ("bv", "L0_attn_bv"), ("bo", "L0_attn_bo")):
                    act.dma_start(w[name][:, :], dram[key].partition_broadcast(P)).then_inc(small, 16)
                for name, key in (("bq", "L0_attn_bq"), ("bk", "L0_attn_bk")):
                    act.dma_start(w[name][:, :], dram[key].rearrange("(p a) -> p a", a=1)).then_inc(small, 16)
                act.wait_ge(small, 16 * 11)

            @block.gpsimd
            def _(pool):
                nc.gpsimd.memset(w["ident"][:, :], 0.0).then_inc(pool_step, 1)
                nc.gpsimd.memset(w["before"][:, :], 0.0).then_inc(pool_step, 1)
                nc.gpsimd.memset(w["ones"][:, :], 1.0).then_inc(pool_step, 1)
                nc.gpsimd.iota(iota_i[:, :], [[1, P]], base=0, channel_multiplier=0).then_inc(pool_step, 1)
                nc.gpsimd.iota(partition_i[:, :], [[0, 1]], base=0, channel_multiplier=1).then_inc(pool_step, 1)
                pool.wait_ge(pool_step, 5)
                nc.gpsimd.affine_select(out=w["ident"][:, :], in_=w["ident"][:, :], compare_op=ALU.not_equal, fill=1.0,
                                        base=0, pattern=[[-1, P]], channel_multiplier=1).then_inc(pool_step, 1)
                nc.gpsimd.affine_select(out=w["before"][:, :], in_=w["before"][:, :], compare_op=ALU.is_ge, fill=1.0,
                                        base=0, pattern=[[-1, P]], channel_multiplier=1).then_inc(pool_step, 1)

            @block.tensor
            def _(pe):
                pe.wait_ge(b1load, 16)
                pe.wait_ge(pool_step, 7)
                nc.tensor.transpose(ps_b1[:, 0:EXPERTS * HC], b1_rows[:, :],
                                    w["ident"][0:EXPERTS * HC, 0:EXPERTS * HC]).then_inc(b1_t, 1)
                pe.wait_ge(big, 32)
                pe.wait_ge(dve_step, 2)
                for e in range(EXPERTS):
                    for c in range(HC):
                        last = nc.tensor.matmul(ps_idle[:, e, :], relu_b1[:, e, c:c + 1].to_broadcast([P, P]),
                                                w["W2"][:, e, c, :], start=(c == 0), stop=(c == HC - 1))
                last.then_inc(idle_done, 1)

            @block.vector
            def _(dve):
                dve.wait_ge(b1_t, 1)
                nc.vector.tensor_copy(w["W1"][:, :, HID:], ps_b1[:, 0:EXPERTS * HC].rearrange("p (e c) -> p e c", e=EXPERTS)).then_inc(dve_step, 1)
                nc.vector.tensor_scalar(relu_b1[:, :, :].rearrange("p e c -> p (e c)"), ps_b1[:, 0:EXPERTS * HC],
                                        0.0, None, ALU.max).then_inc(dve_step, 1)
                dve.wait_ge(pool_step, 7)
                nc.vector.tensor_copy(w["iota"][:, :], iota_i[:, :])
                nc.vector.tensor_copy(w["partition"][:, :], partition_i[:, :])
                nc.vector.memset(w["seg"][:, :, :], 1.0).then_inc(dve_step, 1)
                dve.wait_ge(dve_step, 3)
                nc.vector.memset(w["seg"][:, :, 0:1], 0.0)
                nc.vector.tensor_scalar(w["rank8"][:, :], w["iota"][:, 0:EXPERTS], -1.0, float(EXPERTS), ALU.mult, ALU.add)
                dve.wait_ge(small, 16 * 11)
                dve.wait_ge(idle_done, 1)
                nc.vector.tensor_copy(idle[:, :, :], ps_idle[:, :, :]).then_inc(dve_step, 1)
                nc.vector.tensor_tensor(b2_all[:, :, :], ps_idle[:, :, :], b2_all[:, :, :], ALU.add).then_inc(dve_step, 1)
                dve.wait_ge(dve_step, 5)
                nc.vector.tensor_reduce(total[:, :], b2_all[:, :, :].rearrange("p e d -> p d e"), AX.X, ALU.add).then_inc(dve_step, 1)
                dve.wait_ge(dve_step, 6)
                nc.vector.tensor_tensor(w["rest"][:, :, :], total[:, :].unsqueeze(1).to_broadcast([P, EXPERTS, D]),
                                        idle[:, :, :], ALU.subtract).then_inc(dve_step, 1)


def ffn(nc, w, dram, tag, out):
    with ExitStack() as ctx:
        def sb(name, shape, dt):
            return ctx.enter_context(nc.sbuf_tensor(name + tag, shape, dt))

        def pb(name, shape):
            return ctx.enter_context(nc.psum_tensor(name + tag, shape, F32))

        def sem(name):
            return ctx.enter_context(nc.semaphore(name + tag))

        x_sb = w["x"]
        xn_sb = sb("xn", [P, TILES, D], F32)
        source_i = sb("source_i", [P, SORTED], U32)
        target_i = sb("target_i", [P, SORTED], U32)
        expert_i = sb("expert_i", [1, SORTED], I32)

        with ExitStack() as sub:
            def sb2(name, shape, dt):
                return sub.enter_context(nc.sbuf_tensor(name + tag, shape, dt))

            def sem2(name):
                return sub.enter_context(nc.semaphore(name + tag))

            stats = sb2("stats", [P, TILES, 6], F32)
            mv = sb2("mv", [P, TILES, 2], F32)
            rt = sb2("rt", [P, 7, TILES], F32)
            xnT = sb2("xnT", [P, 2, QUAD * P], F32)
            logit = sb2("logit", [P, TILES, EXPERTS], F32)
            best = sb2("best", [P, TILES], F32)
            first = sb2("first", [P, TILES, EXPERTS], F32)
            ranked = sb2("ranked", [P, TILES, EXPERTS], F32)
            firstmax = sb2("firstmax", [P, TILES], F32)
            onehot = sb2("onehot", [P, TILES, EXPERTS], F32)
            onehot_b = sb2("onehot_b", [P, TILES, EXPERTS], BF16)
            count = sb2("count", [P, EXPERTS, TILES], F32)
            upto = sb2("upto", [P, EXPERTS, TILES], F32)
            cmp = sb2("cmp", [P, EXPERTS, TILES], F32)
            ntiles = sb2("ntiles", [P, EXPERTS], F32)
            end = sb2("end", [P, EXPERTS], F32)
            base = sb2("base", [P, EXPERTS], F32)
            place = sb2("place", [P, EXPERTS, TILES], F32)
            slot_f = sb2("slot_f", [P, TILES], F32)
            passed = sb2("passed", [1, SORTED, EXPERTS], F32)
            expert_f = sb2("expert_f", [1, SORTED], F32)
            begun = sb2("begun", [P, TILES, SORTED], F32)
            in_tile = sb2("in_tile", [P, TILES], F32)
            tile_at = sb2("tile_at", [P, TILES], F32)
            marks = sb2("marks", [P, TILES, 3, SORTED], BF16)
            columns = sb2("columns", [P, TILES, P], BF16)
            found = sb2("found", [P, 3, SORTED], F32)
            source = sb2("source", [P, SORTED], F32)
            target = sb2("target", [P, SORTED], F32)
            ps_t = [sub.enter_context(nc.psum_tensor(f"ps_t{p}" + tag, [P, QUAD * P], F32)) for p in range(2)]
            ps_f = sub.enter_context(nc.psum_tensor("ps_f" + tag, [P, HALF], F32))
            ps_l = sub.enter_context(nc.psum_tensor("ps_l" + tag, [P, 2, TILES * EXPERTS], F32))
            ps_r = sub.enter_context(nc.psum_tensor("ps_r" + tag, [P, 2, TILES * EXPERTS], F32))
            vstep, astep, normed, routed = sem2("vstep"), sem2("astep"), sem2("normed"), sem2("routed")
            t_full, t_out, t_used, l_full = sem2("t_full"), sem2("t_out"), sem2("t_used"), sem2("l_full")
            r_full, column, f_full, stored = sem2("r_full"), sem2("column"), sem2("f_full"), sem2("xn_stored")

            with nc.Block() as block:
                @block.vector
                def _(dve):
                    layernorm(nc, dve, None, x_sb, xn_sb, stats, mv, rt, normed, vstep, astep, "dve")
                    dve.wait_ge(l_full, 1)
                    nc.vector.tensor_tensor(logit[:, :, :], ps_l[:, 0, :].rearrange("p (t e) -> p t e", e=EXPERTS),
                                            w["br"][:, :].unsqueeze(1).to_broadcast([P, TILES, EXPERTS]), ALU.add).then_inc(routed, 1)
                    dve.wait_ge(routed, 1)
                    nc.vector.tensor_reduce(best[:, :], logit[:, :, :], AX.X, ALU.max).then_inc(routed, 1)
                    dve.wait_ge(routed, 2)
                    nc.vector.tensor_tensor(first[:, :, :], logit[:, :, :], best[:, :].unsqueeze(2).to_broadcast([P, TILES, EXPERTS]),
                                            ALU.is_ge).then_inc(routed, 1)
                    dve.wait_ge(routed, 3)
                    nc.vector.tensor_tensor(ranked[:, :, :], first[:, :, :],
                                            w["rank8"][:, :].unsqueeze(1).to_broadcast([P, TILES, EXPERTS]), ALU.mult).then_inc(routed, 1)
                    dve.wait_ge(routed, 4)
                    nc.vector.tensor_reduce(firstmax[:, :], ranked[:, :, :], AX.X, ALU.max).then_inc(routed, 1)
                    dve.wait_ge(routed, 5)
                    nc.vector.tensor_tensor(onehot[:, :, :], ranked[:, :, :], firstmax[:, :].unsqueeze(2).to_broadcast([P, TILES, EXPERTS]),
                                            ALU.is_equal).then_inc(routed, 1)
                    dve.wait_ge(routed, 6)
                    nc.vector.tensor_copy(onehot_b[:, :, :], onehot[:, :, :]).then_inc(routed, 1)
                    dve.wait_ge(r_full, 1)
                    nc.vector.tensor_copy(count[:, :, :], ps_r[:, 1, :].rearrange("p (t e) -> p e t", e=EXPERTS)).then_inc(routed, 1)
                    dve.wait_ge(routed, 8)
                    nc.vector.tensor_tensor_scan(upto[:, :, :].rearrange("p e t -> p (e t)"), w["seg"][:, :, :].rearrange("p e t -> p (e t)"),
                                                 count[:, :, :].rearrange("p e t -> p (e t)"), 0.0, ALU.mult, ALU.add).then_inc(routed, 1)
                    dve.wait_ge(routed, 9)
                    nc.vector.scalar_tensor_tensor(out=cmp[:, :, :], in0=w["iota"][:, 0:TILES].unsqueeze(1).to_broadcast([P, EXPERTS, TILES]),
                                                   scalar=float(P), in1=upto[:, :, TILES - 1:TILES].to_broadcast([P, EXPERTS, TILES]),
                                                   op0=ALU.mult, op1=ALU.is_lt).then_inc(routed, 1)
                    dve.wait_ge(routed, 10)
                    nc.vector.tensor_reduce(ntiles[:, :], cmp[:, :, :], AX.X, ALU.add).then_inc(routed, 1)
                    dve.wait_ge(routed, 11)
                    nc.vector.tensor_tensor_scan(end[:, :], w["seg"][:, 0, 1:1 + EXPERTS], ntiles[:, :], 0.0, ALU.mult, ALU.add).then_inc(routed, 1)
                    dve.wait_ge(routed, 12)
                    nc.vector.tensor_tensor(base[:, :], end[:, :], ntiles[:, :], ALU.subtract).then_inc(routed, 1)
                    nc.vector.tensor_tensor(place[:, :, :], upto[:, :, :], count[:, :, :], ALU.subtract).then_inc(routed, 1)
                    nc.vector.tensor_tensor(passed[:, :, :], end[0:1, :].unsqueeze(1).to_broadcast([1, SORTED, EXPERTS]),
                                            w["iota"][0:1, 0:SORTED].unsqueeze(2).to_broadcast([1, SORTED, EXPERTS]), ALU.is_le).then_inc(routed, 1)
                    dve.wait_ge(routed, 15)
                    nc.vector.tensor_reduce(expert_f[:, :], passed[:, :, :], AX.X, ALU.add).then_inc(routed, 1)
                    nc.vector.scalar_tensor_tensor(out=cmp[:, :, :], in0=base[:, :].unsqueeze(2).to_broadcast([P, EXPERTS, TILES]),
                                                   scalar=float(P), in1=place[:, :, :], op0=ALU.mult, op1=ALU.add).then_inc(routed, 1)
                    dve.wait_ge(routed, 17)
                    nc.vector.tensor_scalar(expert_i[:, :], expert_f[:, :], float(EXPERTS - 1), None, ALU.min).then_inc(routed, 1)
                    nc.vector.tensor_tensor(place[:, :, :], cmp[:, :, :], ps_r[:, 0, :].rearrange("p (t e) -> p e t", e=EXPERTS),
                                            ALU.add).then_inc(routed, 1)
                    dve.wait_ge(routed, 19)
                    nc.vector.tensor_tensor(first[:, :, :], place[:, :, :].rearrange("p e t -> p t e"), onehot[:, :, :], ALU.mult).then_inc(routed, 1)
                    dve.wait_ge(routed, 20)
                    nc.vector.tensor_reduce(slot_f[:, :], first[:, :, :], AX.X, ALU.add).then_inc(routed, 1)
                    dve.wait_ge(routed, 21)
                    nc.vector.scalar_tensor_tensor(out=begun[:, :, :], in0=w["iota"][:, 0:SORTED].unsqueeze(1).to_broadcast([P, TILES, SORTED]),
                                                   scalar=float(P), in1=slot_f[:, :].unsqueeze(2).to_broadcast([P, TILES, SORTED]),
                                                   op0=ALU.mult, op1=ALU.is_le).then_inc(routed, 1)
                    dve.wait_ge(routed, 22)
                    nc.vector.tensor_reduce(tile_at[:, :], begun[:, :, :], AX.X, ALU.add).then_inc(routed, 1)
                    dve.wait_ge(routed, 23)
                    nc.vector.scalar_tensor_tensor(out=in_tile[:, :], in0=tile_at[:, :], scalar=-float(P), in1=slot_f[:, :],
                                                   op0=ALU.mult, op1=ALU.add).then_inc(routed, 1)
                    dve.wait_ge(routed, 24)
                    nc.vector.scalar_tensor_tensor(out=marks[:, :, 2, :], in0=w["iota"][:, 0:SORTED].unsqueeze(1).to_broadcast([P, TILES, SORTED]),
                                                   scalar=1.0, in1=tile_at[:, :].unsqueeze(2).to_broadcast([P, TILES, SORTED]),
                                                   op0=ALU.add, op1=ALU.is_equal).then_inc(routed, 1)
                    nc.vector.tensor_scalar(in_tile[:, :], in_tile[:, :], float(P), None, ALU.add).then_inc(routed, 1)
                    dve.wait_ge(routed, 26)
                    nc.vector.tensor_tensor(marks[:, :, 0, :], marks[:, :, 2, :],
                                            w["iota"][:, 0:TILES].unsqueeze(2).to_broadcast([P, TILES, SORTED]), ALU.mult)
                    nc.vector.tensor_scalar(marks[:, :, 1, :], marks[:, :, 2, :], w["partition"][:, 0:1], None, ALU.mult)
                    for q in range(QUADS):
                        tiles = slice(q * QUAD, (q + 1) * QUAD)
                        nc.vector.tensor_tensor(columns[:, tiles, :], w["iota"][:, :].unsqueeze(1).to_broadcast([P, QUAD, P]),
                                                in_tile[:, tiles].unsqueeze(2).to_broadcast([P, QUAD, P]), ALU.is_equal).then_inc(column, 1)
                    dve.wait_ge(f_full, 1)
                    nc.vector.tensor_copy(found[:, :, :], ps_f[:, 0:3 * SORTED].rearrange("p (a s) -> p a s", a=3)).then_inc(routed, 1)
                    dve.wait_ge(routed, 27)
                    nc.vector.scalar_tensor_tensor(out=source[:, :], in0=found[:, 0, :], scalar=float(P), in1=found[:, 1, :],
                                                   op0=ALU.mult, op1=ALU.add).then_inc(routed, 1)
                    dve.wait_ge(routed, 28)
                    nc.vector.tensor_copy(source_i[:, :], source[:, :])
                    nc.vector.scalar_tensor_tensor(out=target[:, :], in0=found[:, 2, :], scalar=-float(TOKENS), in1=source[:, :],
                                                   op0=ALU.mult, op1=ALU.add).then_inc(routed, 1)
                    dve.wait_ge(routed, 29)
                    nc.vector.tensor_scalar(target_i[:, :], target[:, :], float(TOKENS), None, ALU.add).then_inc(routed, 1)

                @block.scalar
                def _(act):
                    layernorm(nc, None, act, x_sb, xn_sb, stats, mv, rt, normed, vstep, astep, "act")
                    for q in range(QUADS):
                        act.wait_ge(t_full, q + 1)
                        if q >= 2:
                            act.wait_ge(t_used, q - 1)
                        nc.scalar.activation(xnT[:, q % 2, :], ps_t[q % 2][:, :], ACT.Copy).then_inc(t_out, 1)

                @block.tensor
                def _(pe):
                    def logits(q):
                        pe.wait_ge(t_out, q + 1)
                        for i in range(QUAD):
                            t = QUAD * q + i
                            last = nc.tensor.matmul(ps_l[:, 0, t * EXPERTS:(t + 1) * EXPERTS], xnT[:, q % 2, i * P:(i + 1) * P],
                                                    w["Wr"][:, :], start=True, stop=True)
                        last.then_inc(t_used, 1)

                    for q in range(QUADS):
                        pe.wait_ge(normed, q + 1)
                        if q >= 2:
                            pe.wait_ge(t_out, q - 1)
                        for i in range(QUAD):
                            last = nc.tensor.transpose(ps_t[q % 2][:, i * P:(i + 1) * P], xn_sb[:, QUAD * q + i, :], w["ident"][:, :])
                        last.then_inc(t_full, 1)
                        if q >= 1:
                            logits(q - 1)
                    pe.wait_ge(t_out, QUADS)
                    for i in range(QUAD):
                        t = TILES - QUAD + i
                        last = nc.tensor.matmul(ps_l[:, 0, t * EXPERTS:(t + 1) * EXPERTS], xnT[:, (QUADS - 1) % 2, i * P:(i + 1) * P],
                                                w["Wr"][:, :], start=True, stop=True)
                    last.then_inc(l_full, 1)
                    pe.wait_ge(routed, 7)
                    chosen = onehot_b[:, :, :].rearrange("p t e -> p (t e)")
                    nc.tensor.matmul(ps_r[:, 0, :], w["before"][:, :], chosen, start=True, stop=True)
                    nc.tensor.matmul(ps_r[:, 1, :], w["ones"][:, :], chosen, start=True, stop=True).then_inc(r_full, 1)
                    for t in range(TILES):
                        if t % QUAD == 0:
                            pe.wait_ge(column, t // QUAD + 1)
                        last = nc.tensor.matmul(ps_f[:, 0:3 * SORTED], columns[:, t, :], marks[:, t, :, :].rearrange("p a s -> p (a s)"),
                                                start=(t == 0), stop=(t == TILES - 1))
                    last.then_inc(f_full, 1)

                @block.sync
                def _(sp):
                    for q in range(QUADS):
                        sp.wait_ge(normed, q + 1)
                        sp.dma_start(dram["xn_rows"][q * QUAD * P:(q + 1) * QUAD * P, :].rearrange("(t p) d -> p t d", p=P),
                                     xn_sb[:, q * QUAD:(q + 1) * QUAD, :]).then_inc(stored, 16)
                    sp.wait_ge(stored, 16 * QUADS)

        with ExitStack() as sub:
            def sb2(name, shape, dt):
                return sub.enter_context(nc.sbuf_tensor(name + tag, shape, dt))

            def sem2(name):
                return sub.enter_context(nc.semaphore(name + tag))

            def sems2(name):
                return [sub.enter_context(nc.semaphore(f"{name}{p}" + tag)) for p in range(ROTATION)]

            def banks(name):
                return [sub.enter_context(nc.psum_tensor(f"{name}{p}" + tag, [P, HALF], F32)) for p in range(2)]

            xs = sb2("xs", [P, ROTATION, D], F32)
            xsT = sb2("xsT", [P, 2, P], F32)
            w1s = sb2("w1s", [P, ROTATION, HID + HC], F32)
            hT = sb2("hT", [P, 2, HID], F32)
            ys = sb2("ys", [P, ROTATION, D], F32)
            ps_x, ps_y, ps_h = banks("ps_x"), banks("ps_y"), (banks("ps_ha"), banks("ps_hb"))
            x_in, y_stored = sems2("x_in"), sems2("y_stored")
            x_t, xT_out, w1_in = sem2("x_t"), sem2("xT_out"), sem2("w1_in")
            h_full, h_act, h_dve, y_full, y_out = (sem2(n) for n in ("h_full", "h_act", "h_dve", "y_full", "y_out"))

            def turns(engine, turn):
                turn(0)
                with engine.Fori(1, TURNS - 1) as i:
                    turn(i)
                turn(TURNS - 1, last=True)

            def wait_tile(engine, semaphore, i, r, back=0):
                if not (isinstance(i, int) and ROTATION * i + r - back < 0):
                    engine.wait_ge(semaphore, ROTATION * i + r - back + 1)

            def expert(engine, i, r):
                return engine.value_load(expert_i[0:1, bass.ds(ROTATION * i + r, 1)], min_val=0, max_val=EXPERTS - 1)

            with nc.Block() as block:
                @block.gpsimd
                def _(pool):
                    def gather(i, r):
                        nc.gpsimd.indirect_dma_start(xs[:, r, :], None, dram["xn_rows"],
                                                     bass.IndirectOffsetOnAxis(ap=source_i[:, ROTATION * i + r:ROTATION * i + r + 1], axis=0)).then_inc(x_in[r], 16)

                    def scatter(i, r):
                        wait_tile(pool, y_out, i, r)
                        nc.gpsimd.indirect_dma_start(dram["y_rows"], bass.IndirectOffsetOnAxis(ap=target_i[:, ROTATION * i + r:ROTATION * i + r + 1], axis=0),
                                                     ys[:, r, :], None, bounds_check=TOKENS - 1, oob_is_err=False).then_inc(y_stored[r], 16)

                    for r in range(ROTATION):
                        gather(0, r)

                    def turn(i, last=False):
                        for r in range(ROTATION):
                            if not last:
                                wait_tile(pool, x_t, i, r)
                                gather(i + 1, r)
                            if r >= 2:
                                scatter(i, r - 2)
                            elif not (isinstance(i, int) and i == 0):
                                scatter(i - 1, r + 2)

                    for i in range(TURNS):
                        turn(i, last=i == TURNS - 1)
                    for r in (2, 3):
                        scatter(TURNS - 1, r)
                    for r in range(ROTATION):
                        pool.wait_ge(y_stored[r], 16 * TURNS)

                @block.tensor
                def _(pe):
                    def turned(i, r):
                        pe.wait_ge(x_in[r], 16 * i + 16)
                        wait_tile(pe, xT_out, i, r, 2)
                        nc.tensor.transpose(ps_x[r % 2][:, 0:P], xs[:, r, :], w["ident"][:, :]).then_inc(x_t, 1)

                    def up(i, r):
                        wait_tile(pe, xT_out, i, r)
                        wait_tile(pe, w1_in, i, r)
                        wait_tile(pe, h_act, i, r, 2)
                        wait_tile(pe, h_dve, i, r, 2)
                        for c in range(HC):
                            last = nc.tensor.matmul(ps_h[c // 2][r % 2][:, (c % 2) * P:(c % 2 + 1) * P], w1s[:, r, c * P:(c + 1) * P],
                                                    xsT[:, r % 2, :], start=True, stop=True)
                        last.then_inc(h_full, 1)

                    def down(i, r, e):
                        wait_tile(pe, h_act, i, r)
                        wait_tile(pe, h_dve, i, r)
                        wait_tile(pe, y_out, i, r, 2)
                        for c in range(HC):
                            last = nc.tensor.matmul(ps_y[r % 2][:, 0:D], hT[:, r % 2, c * P:(c + 1) * P],
                                                    w["W2"][:, bass.ds(e, 1), c, :].rearrange("p a d -> p (a d)"),
                                                    start=(c == 0), stop=(c == HC - 1))
                        last.then_inc(y_full, 1)

                    turned(0, 0)
                    turned(0, 1)
                    up(0, 0)

                    def turn(i, last=False):
                        for r in range(ROTATION):
                            e = expert(pe, i, r)
                            if r + 1 < ROTATION:
                                up(i, r + 1)
                            elif not last:
                                up(i + 1, 0)
                            if r + 2 < ROTATION:
                                turned(i, r + 2)
                            elif not last:
                                turned(i + 1, r + 2 - ROTATION)
                            down(i, r, e)

                    turns(pe, turn)

                @block.scalar
                def _(act):
                    def turned(i, r):
                        wait_tile(act, x_t, i, r)
                        wait_tile(act, h_full, i, r, 2)
                        nc.scalar.activation(xsT[:, r % 2, :], ps_x[r % 2][:, 0:P], ACT.Copy).then_inc(xT_out, 1)

                    def weights(i, r):
                        e = expert(act, i, r)
                        wait_tile(act, h_full, i, r, ROTATION)
                        wait_tile(act, h_dve, i, r, ROTATION)
                        wait_tile(act, h_act, i, r, ROTATION)
                        nc.scalar.activation(w1s[:, r, :], w["W1"][:, bass.ds(e, 1), :].rearrange("p a h -> p (a h)"), ACT.Copy).then_inc(w1_in, 1)

                    def relu(i, r):
                        wait_tile(act, w1_in, i, r)
                        wait_tile(act, h_full, i, r)
                        wait_tile(act, y_full, i, r, 2)
                        for c in range(2):
                            last = nc.scalar.activation(hT[:, r % 2, c * P:(c + 1) * P], ps_h[0][r % 2][:, c * P:(c + 1) * P], ACT.Relu,
                                                        bias=w1s[:, r, HID + c:HID + c + 1])
                        last.then_inc(h_act, 1)

                    for r in range(3):
                        weights(0, r)
                    turned(0, 0)
                    turned(0, 1)
                    relu(0, 0)

                    def turn(i, last=False):
                        for r in range(ROTATION):
                            if r + 2 < ROTATION:
                                turned(i, r + 2)
                            elif not last:
                                turned(i + 1, r + 2 - ROTATION)
                            if r + 1 < ROTATION:
                                relu(i, r + 1)
                            elif not last:
                                relu(i + 1, 0)
                            if r + 3 < ROTATION:
                                weights(i, r + 3)
                            elif not last:
                                weights(i + 1, r + 3 - ROTATION)

                    turns(act, turn)

                @block.vector
                def _(dve):
                    def relu(i, r):
                        wait_tile(dve, w1_in, i, r)
                        wait_tile(dve, h_full, i, r)
                        wait_tile(dve, y_full, i, r, 2)
                        for c in range(2, HC):
                            last = nc.vector.tensor_scalar(hT[:, r % 2, c * P:(c + 1) * P], ps_h[1][r % 2][:, (c - 2) * P:(c - 1) * P],
                                                           w1s[:, r, HID + c:HID + c + 1], 0.0, ALU.add, ALU.max)
                        last.then_inc(h_dve, 1)

                    def result(i, r, e):
                        wait_tile(dve, y_full, i, r)
                        wait_unless_zero(dve, y_stored[r], 16 * i)
                        nc.vector.tensor_tensor(ys[:, r, :], ps_y[r % 2][:, 0:D],
                                                w["rest"][:, bass.ds(e, 1), :].rearrange("p a d -> p (a d)"), ALU.add).then_inc(y_out, 1)

                    relu(0, 0)

                    def turn(i, last=False):
                        for r in range(ROTATION):
                            e = expert(dve, i, r)
                            if r + 1 < ROTATION:
                                relu(i, r + 1)
                            elif not last:
                                relu(i + 1, 0)
                            result(i, r, e)

                    turns(dve, turn)

        with ExitStack() as sub:
            loaded = [sub.enter_context(nc.semaphore(f"y_loaded{p}" + tag)) for p in range(QUADS)]
            added, stored = (sub.enter_context(nc.semaphore(n + tag)) for n in ("added", "stored"))
            y_sb = xn_sb

            def load(engine, q):
                engine.dma_start(y_sb[:, q * QUAD:(q + 1) * QUAD, :],
                                 dram["y_rows"][q * QUAD * P:(q + 1) * QUAD * P, :].rearrange("(t p) d -> p t d", p=P)).then_inc(loaded[q], 16)

            with nc.Block() as block:
                @block.vector
                def _(dve):
                    for q in range(QUADS):
                        dve.wait_ge(loaded[q], 16)
                        tiles = slice(q * QUAD, (q + 1) * QUAD)
                        nc.vector.scalar_tensor_tensor(out=x_sb[:, tiles, :], in0=y_sb[:, tiles, :], scalar=0.5,
                                                       in1=x_sb[:, tiles, :], op0=ALU.mult, op1=ALU.add).then_inc(added, 1)

                @block.scalar
                def _(act):
                    for q in range(1, QUADS, 2):
                        load(act, q)

                @block.sync
                def _(sp):
                    for q in range(0, QUADS, 2):
                        load(sp, q)
                    if out is not None:
                        for q in range(QUADS):
                            sp.wait_ge(added, q + 1)
                            b, t = q * QUAD // KT, q * QUAD % KT
                            sp.dma_start(out[b, t * P:(t + QUAD) * P, :].rearrange("(t p) d -> p t d", p=P),
                                         x_sb[:, q * QUAD:(q + 1) * QUAD, :]).then_inc(stored, 16)
                        sp.wait_ge(stored, 16 * QUADS)


def project(nc, w, dram, v_sb, q2, k2):
    with ExitStack() as ctx:
        def sb(name, shape, dt):
            return ctx.enter_context(nc.sbuf_tensor(name, shape, dt))

        def banks(name):
            return [ctx.enter_context(nc.psum_tensor(f"{name}{p}", [P, HALF], F32)) for p in range(2)]

        def sem(name):
            return ctx.enter_context(nc.semaphore(name))

        xn_sb = sb("xn_a", [P, TILES, D], F32)
        stats, mv, rt = sb("stats_a", [P, TILES, 6], F32), sb("mv_a", [P, TILES, 2], F32), sb("rt_a", [P, 7, TILES], F32)
        xnT = sb("xnT_a", [P, 2, HALF], F32)
        exact = sb("exact", [P, 2, 2, HALF], F32)
        rem = sb("rem", [P, 2, 2, HALF], F32)
        parts = sb("parts", [P, 2, 2, PARTS, HALF], BF16)
        ps_t, ps_q, ps_k, ps_v = banks("ps_ta"), banks("ps_q"), banks("ps_k"), banks("ps_v")
        vstep, astep, normed = sem("vstep_a"), sem("astep_a"), sem("normed_a")
        t_full, t_out, qk_full, v_full = sem("t_full_a"), sem("t_out_a"), sem("qk_full"), sem("v_full")
        high, middle, left, low, v_out = sem("high"), sem("middle"), sem("left"), sem("low"), sem("v_out")
        stored = [sem(f"parts_stored{p}") for p in range(2)]
        filled = sem("filled")

        with nc.Block() as block:
            @block.gpsimd
            def _(pool):
                for p in range(BUFS):
                    for rows, q_value, k_value in ((slice(64, FILL), 0.0, 0.0), (slice(FILL, P), 0.0, 1.0)):
                        nc.gpsimd.memset(q2[p][rows, :, :], q_value).then_inc(filled, 1)
                        nc.gpsimd.memset(k2[p][rows, :, :], k_value).then_inc(filled, 1)
                        pool.wait_ge(filled, 4 * p + (2 if rows.start == 64 else 4))

            @block.vector
            def _(dve):
                layernorm(nc, dve, None, w["x"], xn_sb, stats, mv, rt, normed, vstep, astep, "dve")
                for q in range(QUADS):
                    p = q % 2
                    if q >= 2:
                        dve.wait_ge(middle, 2 * q - 2)
                    for j in range(2):
                        dve.wait_ge(high, 4 * q + 2 * j + 2)
                        nc.vector.tensor_tensor(rem[:, p, j, :], exact[:, p, j, :], parts[:, p, j, 0, :], ALU.subtract).then_inc(left, 1)
                    dve.wait_ge(v_full, q + 1)
                    b, t = q * QUAD // KT, q * QUAD % KT
                    nc.vector.tensor_tensor(v_sb[:, b * GPB:(b + 1) * GPB, t:t + QUAD, :].rearrange("p g t c -> p t g c"),
                                            ps_v[p][:, :].rearrange("p (t g c) -> p t g c", t=QUAD, g=GPB),
                                            w["bv"][:, :].rearrange("p (g c) -> p g c", g=GPB).unsqueeze(1).to_broadcast([P, QUAD, GPB, GH * DK]),
                                            ALU.add).then_inc(v_out, 1)
                    for j in range(2):
                        dve.wait_ge(middle, 2 * q + j + 1)
                        nc.vector.tensor_tensor(parts[:, p, j, 2, :], rem[:, p, j, :], parts[:, p, j, 1, :], ALU.subtract).then_inc(low, 1)

            @block.tensor
            def _(pe):
                for q in range(QUADS):
                    p = q % 2
                    pe.wait_ge(normed, q + 1)
                    if q >= 2:
                        pe.wait_ge(t_out, q - 1)
                    for i in range(QUAD):
                        last = nc.tensor.transpose(ps_t[p][:, i * P:(i + 1) * P], xn_sb[:, QUAD * q + i, :], w["ident"][:, :])
                    last.then_inc(t_full, 1)
                    pe.wait_ge(t_out, q + 1)
                    if q >= 2:
                        pe.wait_ge(high, 4 * q - 4)
                        pe.wait_ge(v_out, q - 1)
                    nc.tensor.matmul(ps_q[p][:, :], w["Wq"][:, :], xnT[:, p, :], start=True, stop=True).then_inc(qk_full, 1)
                    nc.tensor.matmul(ps_k[p][:, :], w["Wk"][:, :], xnT[:, p, :], start=True, stop=True).then_inc(qk_full, 1)
                    for i in range(QUAD):
                        last = nc.tensor.matmul(ps_v[p][:, i * P:(i + 1) * P], xnT[:, p, i * P:(i + 1) * P], w["Wv"][:, :], start=True, stop=True)
                    last.then_inc(v_full, 1)

            @block.scalar
            def _(act):
                layernorm(nc, None, act, w["x"], xn_sb, stats, mv, rt, normed, vstep, astep, "act")
                for q in range(QUADS):
                    p = q % 2
                    act.wait_ge(t_full, q + 1)
                    if q >= 2:
                        act.wait_ge(v_full, q - 1)
                    nc.scalar.activation(xnT[:, p, :], ps_t[p][:, :], ACT.Copy).then_inc(t_out, 1)
                    for j, (bank, bias) in enumerate(((ps_q[p], w["bq"]), (ps_k[p], w["bk"]))):
                        act.wait_ge(qk_full, 2 * q + j + 1)
                        if q >= 2:
                            act.wait_ge(left, 2 * q - 2)
                            act.wait_ge(stored[p], 16 * 2 * PARTS * (q // 2))
                        nc.scalar.activation(exact[:, p, j, :], bank[:, :], ACT.Identity, bias=bias[:, 0:1]).then_inc(high, 1)
                        nc.scalar.activation(parts[:, p, j, 0, :], bank[:, :], ACT.Identity, bias=bias[:, 0:1]).then_inc(high, 1)
                    for j in range(2):
                        act.wait_ge(left, 2 * q + j + 1)
                        nc.scalar.activation(parts[:, p, j, 1, :], rem[:, p, j, :], ACT.Copy).then_inc(middle, 1)

            @block.sync
            def _(sp):
                for q in range(QUADS):
                    p = q % 2
                    b, t = q * QUAD // KT, q * QUAD % KT * P
                    sp.wait_ge(low, 2 * q + 2)
                    for j, key in enumerate(("q_parts", "k_parts")):
                        for n in range(PARTS):
                            sp.dma_start(dram[key][b * HEADS:(b + 1) * HEADS, n * DK:(n + 1) * DK, t:t + HALF],
                                         parts[:, p, j, n, :]).then_inc(stored[p], 16)
                for p in range(2):
                    sp.wait_ge(stored[p], 16 * 2 * PARTS * (QUADS // 2))


class Body:

    def __init__(self, g, buf, use):
        self.g, self.buf, self.use = g, buf, use

    def ahead(self, n):
        return Body(self.g + n, (self.buf + n) % BUFS, self.use + (self.buf + n) // BUFS)

    def unit(self, n):
        if isinstance(self.g, int) and self.g == 0:
            n += PROLOGUE
            return n % 2, n // 2
        start = PROLOGUE - 1
        if isinstance(self.g, int) and self.g == GROUPS - 1:
            n -= AHEAD
        return n % 2, UNITS // 2 * self.g + (start + n) // 2


AHEAD = 10
UNITS = P1_UNITS + 2
PROLOGUE = P1_UNITS + 1 + AHEAD


def first_pass(finish, start):
    units = [("max", 1, m) for m in range(AHEAD, P1_UNITS)] if finish else []
    begin = [("max", 2, m) for m in range(AHEAD)] if start else []
    return units + (begin[:2] + [("m", 1, 0)] if finish else []) + begin[2:]


def plan(first=False, finish=True, start=True):
    units, steps = first_pass(finish, start), []
    for k in range(STEPS):
        here = units[2 * k:2 * k + 2] if k < STEPS - 1 else units[2 * k:]
        steps.append(here + ([("o", -1, 0)] if k == 3 and not first else []))
    return steps


def bodies(engine, body):
    at = Body(0, 0, 0)
    body(at, first=True)
    loops = (GROUPS - 3) // BUFS
    with engine.Fori(0, loops) as i:
        for n in range(1, BUFS + 1):
            body(Body(BUFS * i + n, n % BUFS, i + n // BUFS))
    for g in range(1 + BUFS * loops, GROUPS):
        body(Body(g, g % BUFS, g // BUFS), finish=g + 1 < GROUPS, start=g + 2 < GROUPS)


def attention(nc, w, dram, v_sb, ctx_sb, q2, k2):
    with ExitStack() as ctx:
        def sb(name, shape, dt):
            return ctx.enter_context(nc.sbuf_tensor(name, shape, dt))

        def sem(name):
            return ctx.enter_context(nc.semaphore(name))

        def sems(name, n):
            return [ctx.enter_context(nc.semaphore(f"{name}{p}")) for p in range(n)]

        vs = [sb(f"vs{p}", [P, KT, GH, 32], F32) for p in range(BUFS)]
        probs = sb("probs", [P, 2, GH, HALF], F32)
        oT = sb("oT", [P, 2, HALF], F32)
        maxima = sb("maxima", [P, GH, KT, 2], F32)
        top = sb("top", [P, GH * KT], F32)
        mpart = [sb(f"mpart{p}", [GH * KT, PARTS, P], BF16) for p in range(BUFS)]
        mrest = sb("mrest", [GH * KT, P], F32)
        rden = sb("rden", [P, KT, GH, 1], F32)
        ps_m = [ctx.enter_context(nc.psum_tensor(f"ps_m{p}", [P, 2, HALF], F32)) for p in range(2)]
        ps_s = [ctx.enter_context(nc.psum_tensor(f"ps_s{n}", [P, HALF], F32)) for n in range(3)]
        ps_o = ctx.enter_context(nc.psum_tensor("ps_o", [P, HALF], F32))

        loaded, in_m, in_v = sems("loaded", BUFS), sems("in_m", BUFS), sems("in_v", BUFS)
        unit_full, unit_free = sems("unit_full", 2), sems("unit_free", 2)
        scored, exped, step_done, o_out = sem("scored"), sem("exped"), sem("step_done"), sem("o_out")
        combined, split, recip, padded = sem("combined"), sem("split"), sem("recip"), sem("padded")

        LOADS = PARTS + PARTS * PARTS

        with nc.Block() as block:
            @block.sync
            def _(sp):
                def load(at):
                    heads = bass.ds(at.g * GH, GH)
                    for n in range(PARTS):
                        rows = slice(n * PARTS * DK, (n + 1) * PARTS * DK)
                        sp.dma_start(q2[at.buf][rows, :, :], dram["q_parts"][heads, :, :].rearrange("j r t -> r j t")).then_inc(loaded[at.buf], 16)
                        for m in range(PARTS):
                            row = (n * PARTS + m) * DK
                            sp.dma_start(k2[at.buf][row:row + DK, :, :],
                                         dram["k_parts"][heads, n * DK:(n + 1) * DK, :].rearrange("j d t -> d j t")).then_inc(loaded[at.buf], 16)

                def take_maxima(at):
                    rows = dram["m_rows"][at.buf, :, :, :]
                    sp.wait_ge(split, PARTS * at.g + PARTS)
                    sp.dma_start(rows, mpart[at.buf][:, :, :]).then_inc(in_m[at.buf], 16)
                    sp.wait_ge(in_m[at.buf], 32 * at.use + 16)
                    sp.dma_start(q2[at.buf][FILL:FILL + PARTS, :, :].rearrange("r j (t q) -> r (j t) q", q=P),
                                 rows.rearrange("a r q -> r a q")).then_inc(in_m[at.buf], 16)

                def body(at, first=False, finish=True, start=True):
                    if start and not first:
                        sp.wait_ge(step_done, STEPS * at.g)
                        load(at.ahead(2))
                    if finish:
                        take_maxima(at.ahead(1))

                for g in range(BUFS):
                    load(Body(g, g, 0))
                take_maxima(Body(0, 0, 0))
                bodies(sp, body)
                for p in range(BUFS):
                    sp.wait_ge(in_m[p], 32 * ((GROUPS - 1 - p) // BUFS + 1))

            @block.gpsimd
            def _(pool):
                for p in range(BUFS):
                    nc.gpsimd.memset(vs[p][:, :, :, :], 1.0).then_inc(padded, 1)

                def stage(at):
                    nc.gpsimd.tensor_copy(vs[at.buf][:, :, :, 0:DK],
                                          v_sb[:, bass.ds(at.g, 1), :, :].rearrange("p a t (j d) -> p (a t) j d", d=DK)).then_inc(in_v[at.buf], 1)

                def body(at, first=False, finish=True, start=True):
                    if start and not first:
                        pool.wait_ge(step_done, STEPS * at.g)
                        stage(at.ahead(2))

                for g in range(BUFS):
                    pool.wait_ge(padded, g + 1)
                    stage(Body(g, g, 0))
                bodies(pool, body)

            @block.tensor
            def _(pe):
                def maxima_unit(slot, buf, n):
                    qt, kh, pr = n // 4, n // 2 % 2, n % 2
                    for j in (2 * pr, 2 * pr + 1):
                        last = nc.tensor.matmul(ps_m[slot][:, j % 2, :], q2[buf][0:FILL, j, qt * P:(qt + 1) * P],
                                                k2[buf][0:FILL, j, kh * HALF:(kh + 1) * HALF], start=True, stop=True)
                    last.then_inc(unit_full[slot], 1)

                def turn_maxima(at, slot):
                    pe.wait_ge(combined, at.g + 1)
                    nc.tensor.transpose(ps_m[slot][0:GH * KT, 0, 0:P], top[:, :], w["ident"][:, :]).then_inc(unit_full[slot], 1)

                def turn_results(at, slot):
                    pe.wait_ge(o_out, 2 * at.g + 2)
                    for i in range(KT):
                        last = nc.tensor.transpose(ps_m[slot][:, i // QUAD, i % QUAD * P:(i % QUAD + 1) * P],
                                                   oT[:, i // QUAD, i % QUAD * P:(i % QUAD + 1) * P], w["ident"][:, :])
                    last.then_inc(unit_full[slot], 1)

                def do_unit(at, n, kind, ahead, which):
                    slot, used = at.unit(n)
                    of = at.ahead(ahead) if ahead > 0 else Body(at.g + ahead, None, None)
                    pe.wait_ge(unit_free[slot], used)
                    if kind == "max":
                        if which == 0:
                            pe.wait_ge(loaded[of.buf], 16 * LOADS * (of.use + 1))
                        maxima_unit(slot, of.buf, which)
                    elif kind == "m":
                        turn_maxima(of, slot)
                    else:
                        turn_results(of, slot)

                def score(at, k, j):
                    u, kt, n = k // KT, k % KT, GH * k + j
                    if not (isinstance(at.g, int) and GH * STEPS * at.g + n < 3):
                        pe.wait_ge(exped, GH * STEPS * at.g + n - 2)
                    nc.tensor.matmul(ps_s[(n + at.buf) % 3][:, :], k2[at.buf][:, j, kt * P:(kt + 1) * P],
                                     q2[at.buf][:, j, u * HALF:(u + 1) * HALF], start=True, stop=True).then_inc(scored, 1)

                def values(at, k):
                    u, kt = k // KT, k % KT
                    if kt == 0:
                        wait_unless_zero(pe, o_out, 2 * at.g + u)
                    pe.wait_ge(exped, GH * STEPS * at.g + GH * (k + 1))
                    for j in range(GH):
                        last = nc.tensor.matmul(ps_o[32 * j:32 * (j + 1), :], vs[at.buf][:, kt, j, :], probs[:, k % 2, j, :],
                                                start=(kt == 0), stop=(kt == KT - 1))
                    last.then_inc(step_done, 1)

                def body(at, first=False, finish=True, start=True):
                    n = 0
                    pe.wait_ge(in_m[at.buf], 32 * (at.use + 1))
                    pe.wait_ge(in_v[at.buf], at.use + 1)
                    for k, units in enumerate(plan(first, finish, start)):
                        for j in range(GH):
                            score(at, k, j)
                            for kind, ahead, which in units[j:j + 1]:
                                do_unit(at, n, kind, ahead, which)
                                n += 1
                        if k >= 1:
                            values(at, k - 1)
                    values(at, STEPS - 1)

                pe.wait_ge(loaded[0], 16 * LOADS)
                for n in range(P1_UNITS):
                    if n >= 2:
                        pe.wait_ge(unit_free[n % 2], n // 2)
                    maxima_unit(n % 2, 0, n)
                pe.wait_ge(unit_free[P1_UNITS % 2], P1_UNITS // 2)
                turn_maxima(Body(0, 0, 0), P1_UNITS % 2)
                pe.wait_ge(loaded[1], 16 * LOADS)
                for m in range(AHEAD):
                    n = P1_UNITS + 1 + m
                    pe.wait_ge(unit_free[n % 2], n // 2)
                    maxima_unit(n % 2, 1, m)
                bodies(pe, body)
                slot, used = Body(GROUPS - 1, None, None).unit(1)
                pe.wait_ge(unit_free[slot], used)
                turn_results(Body(GROUPS - 1, None, None), slot)

            @block.scalar
            def _(act):
                def take_out(g, u):
                    act.wait_ge(step_done, STEPS * g + KT * (u + 1))
                    if u == 0:
                        wait_unless_zero(act, recip, g)
                    nc.scalar.activation(oT[:, u, :], ps_o[:, :], ACT.Copy).then_inc(o_out, 1)

                def body(at, first=False, finish=True, start=True):
                    for k in range(STEPS):
                        if not (first and k < 2):
                            act.wait_ge(step_done, STEPS * at.g + k - 1)
                        for j in range(GH):
                            n = GH * k + j
                            act.wait_ge(scored, GH * STEPS * at.g + n + 1)
                            nc.scalar.activation(probs[:, k % 2, j, :], ps_s[(n + at.buf) % 3][:, :], ACT.Exp, scale=SCALE).then_inc(exped, 1)
                            if j == 0 and k == 1 and not first:
                                take_out(at.g - 1, 1)
                            if j == 0 and k == KT + 1:
                                take_out(at.g, 0)

                bodies(act, body)
                take_out(GROUPS - 1, 1)

            @block.vector
            def _(dve):
                def maxima_unit(slot, used, n):
                    qt, kh, pr = n // 4, n // 2 % 2, n % 2
                    dve.wait_ge(unit_full[slot], used + 1)
                    nc.vector.tensor_reduce(maxima[:, 2 * pr:2 * pr + 2, qt, kh], ps_m[slot][:, :, :], AX.X, ALU.max).then_inc(unit_free[slot], 1)

                def combine(at, slot, used):
                    dve.wait_ge(unit_free[slot], used)
                    dve.wait_ge(unit_free[1 - slot], used + slot)
                    nc.vector.tensor_reduce(top[:, :], maxima[:, :, :, :].rearrange("p j t h -> p (j t) h"), AX.X, ALU.max).then_inc(combined, 1)
                    dve.wait_ge(combined, at.g + 1)

                def split_unit(at, slot, used):
                    dve.wait_ge(unit_full[slot], used + 1)
                    src, part = ps_m[slot][0:GH * KT, 0, 0:P], mpart[at.buf]
                    nc.vector.tensor_scalar(part[:, 0, :], src, -1.0, None, ALU.mult).then_inc(split, 1)
                    dve.wait_ge(split, PARTS * at.g + 1)
                    nc.vector.scalar_tensor_tensor(out=mrest[:, :], in0=src, scalar=-1.0, in1=part[:, 0, :],
                                                   op0=ALU.mult, op1=ALU.subtract).then_inc(unit_free[slot], 1)
                    dve.wait_ge(unit_free[slot], used + 1)
                    nc.vector.tensor_copy(part[:, 1, :], mrest[:, :]).then_inc(split, 1)
                    dve.wait_ge(split, PARTS * at.g + 2)
                    nc.vector.tensor_tensor(part[:, 2, :], mrest[:, :], part[:, 1, :], ALU.subtract).then_inc(split, 1)

                def result_unit(g, slot, used):
                    dve.wait_ge(unit_full[slot], used + 1)
                    src = ps_m[slot][:, :, :].rearrange("p u (i j c) -> p (u i) j c", i=QUAD, j=GH)
                    nc.vector.reciprocal(rden[:, :, :, :], src[:, :, :, DK:DK + 1]).then_inc(recip, 1)
                    dve.wait_ge(recip, g + 1)
                    nc.vector.tensor_tensor(ctx_sb[:, bass.ds(g, 1), :, :].rearrange("p a t (j d) -> p (a t) j d", d=DK),
                                            src[:, :, :, 0:DK], rden[:, :, :, :].to_broadcast([P, KT, GH, DK]),
                                            ALU.mult).then_inc(unit_free[slot], 1)

                def do_unit(at, n, kind, ahead, which):
                    slot, used = at.unit(n)
                    if kind == "max":
                        maxima_unit(slot, used, which)
                        if which == P1_UNITS - 1:
                            combine(at.ahead(ahead), *at.unit(n + 1))
                    elif kind == "m":
                        split_unit(at.ahead(ahead), slot, used)
                    else:
                        result_unit(at.g - 1, slot, used)

                def body(at, first=False, finish=True, start=True):
                    units = [unit for units in plan(first, finish, start) for unit in units]
                    for n, (kind, ahead, which) in enumerate(units):
                        do_unit(at, n, kind, ahead, which)

                for n in range(P1_UNITS):
                    maxima_unit(n % 2, n // 2, n)
                combine(Body(0, 0, 0), P1_UNITS % 2, P1_UNITS // 2)
                split_unit(Body(0, 0, 0), P1_UNITS % 2, P1_UNITS // 2)
                for m in range(AHEAD):
                    n = P1_UNITS + 1 + m
                    maxima_unit(n % 2, n // 2, m)
                bodies(dve, body)
                slot, used = Body(GROUPS - 1, None, None).unit(0)
                dve.wait_ge(unit_free[slot], used + 1)
                slot, used = Body(GROUPS - 1, None, None).unit(1)
                result_unit(GROUPS - 1, slot, used)


def output_projection(nc, w, ctx_sb):
    with ExitStack() as ctx:
        def banks(name):
            return [ctx.enter_context(nc.psum_tensor(f"{name}{p}", [P, HALF], F32)) for p in range(2)]

        def sem(name):
            return ctx.enter_context(nc.semaphore(name))

        cT = ctx.enter_context(nc.sbuf_tensor("cT", [P, 2, HALF], F32))
        rows = ctx.enter_context(nc.sbuf_tensor("ctx_rows", [P, 2, QUAD, D], F32))
        in_rows = sem("in_rows")
        plus_bo = ctx.enter_context(nc.sbuf_tensor("plus_bo", [P, 2, QUAD, D], F32))
        ps_c, ps_y = banks("ps_c"), banks("ps_yo")
        c_full, c_out, y_full, biased, added = sem("c_full"), sem("c_out"), sem("y_full_o"), sem("biased"), sem("added_o")

        with nc.Block() as block:
            @block.gpsimd
            def _(pool):
                for q in range(QUADS):
                    b, t = q * QUAD // KT, q * QUAD % KT
                    if q >= 2:
                        pool.wait_ge(c_full, q - 1)
                    nc.gpsimd.tensor_copy(rows[:, q % 2, :, :].rearrange("p t (g c) -> p t g c", g=GPB),
                                          ctx_sb[:, b * GPB:(b + 1) * GPB, t:t + QUAD, :].rearrange("p g t c -> p t g c")).then_inc(in_rows, 1)

            @block.tensor
            def _(pe):
                for q in range(QUADS):
                    p = q % 2
                    pe.wait_ge(in_rows, q + 1)
                    if q >= 2:
                        pe.wait_ge(c_out, q - 1)
                    for i in range(QUAD):
                        last = nc.tensor.transpose(ps_c[p][:, i * P:(i + 1) * P], rows[:, p, i, :], w["ident"][:, :])
                    last.then_inc(c_full, 1)
                    pe.wait_ge(c_out, q + 1)
                    if q >= 2:
                        pe.wait_ge(biased, q - 1)
                    for i in range(QUAD):
                        last = nc.tensor.matmul(ps_y[p][:, i * P:(i + 1) * P], cT[:, p, i * P:(i + 1) * P], w["Wo"][:, :], start=True, stop=True)
                    last.then_inc(y_full, 1)

            @block.scalar
            def _(act):
                for q in range(QUADS):
                    act.wait_ge(c_full, q + 1)
                    if q >= 2:
                        act.wait_ge(y_full, q - 1)
                    nc.scalar.activation(cT[:, q % 2, :], ps_c[q % 2][:, :], ACT.Copy).then_inc(c_out, 1)

            @block.vector
            def _(dve):
                for q in range(QUADS):
                    p, tiles = q % 2, slice(q * QUAD, (q + 1) * QUAD)
                    dve.wait_ge(y_full, q + 1)
                    nc.vector.tensor_tensor(plus_bo[:, p, :, :], ps_y[p][:, :].rearrange("p (t d) -> p t d", d=D),
                                            w["bo"][:, :].unsqueeze(1).to_broadcast([P, QUAD, D]), ALU.add).then_inc(biased, 1)
                    dve.wait_ge(biased, q + 1)
                    nc.vector.tensor_tensor(w["x"][:, tiles, :], w["x"][:, tiles, :], plus_bo[:, p, :, :], ALU.add).then_inc(added, 1)


def layer(nc, dram, out):
    with ExitStack() as ctx:
        def sb(name, shape, dt):
            return ctx.enter_context(nc.sbuf_tensor(name, shape, dt))

        w = {
            "x": sb("x", [P, TILES, D], F32),
            "W1": sb("W1", [P, EXPERTS, HID + HC], F32), "W2": sb("W2", [P, EXPERTS, HC, D], F32),
            "rest": sb("rest", [P, EXPERTS, D], F32),
            "Wr": sb("Wr", [P, EXPERTS], F32), "br": sb("br", [P, EXPERTS], F32),
            "Wq": sb("Wq", [P, D], F32), "Wk": sb("Wk", [P, D], F32), "Wv": sb("Wv", [P, D], F32), "Wo": sb("Wo", [P, D], F32),
            "bq": sb("bq", [P, 1], F32), "bk": sb("bk", [P, 1], F32), "bv": sb("bv", [P, D], F32), "bo": sb("bo", [P, D], F32),
            "ident": sb("ident", [P, P], F32), "before": sb("before", [P, P], BF16), "ones": sb("ones", [P, P], BF16),
            "iota": sb("iota", [P, P], F32), "partition": sb("partition", [P, 1], F32), "rank8": sb("rank8", [P, EXPERTS], F32),
            "seg": sb("seg", [P, EXPERTS, TILES], F32),
        }
        constants(nc, w, dram)
        ffn(nc, w, dram, "_1", None)
        with ExitStack() as mid:
            ctx_sb = mid.enter_context(nc.sbuf_tensor("ctx_sb", [P, GROUPS, KT, GH * DK], F32))
            v_sb = mid.enter_context(nc.sbuf_tensor("v_sb", [P, GROUPS, KT, GH * DK], F32))
            q2, k2 = ([mid.enter_context(nc.sbuf_tensor(f"{n}{p}", [P, GH, SEQ], BF16)) for p in range(BUFS)]
                      for n in ("q2_", "k2_"))
            project(nc, w, dram, v_sb, q2, k2)
            attention(nc, w, dram, v_sb, ctx_sb, q2, k2)
            output_projection(nc, w, ctx_sb)
        ffn(nc, w, dram, "_2", out)


_INS = ["L0_attn_x", "L0_attn_Wq", "L0_attn_bq", "L0_attn_Wk", "L0_attn_bk", "L0_attn_Wv", "L0_attn_bv", "L0_attn_Wo", "L0_attn_bo",
        "L0_ffn_W1", "L0_ffn_b1", "L0_ffn_W2", "L0_ffn_b2", "L0_ffn_Wr", "L0_ffn_br"]


def kernel(**inputs):
    import numpy as np
    import concourse.bacc as bacc
    from concourse.bass_utils import run_bass_kernel_spmd

    nc = bacc.Bacc("TRN2", target_bir_lowering=False, num_devices=1)
    arrays, dram = {}, {}
    for name in _INS:
        arrays[name] = np.ascontiguousarray(inputs[name])
        dram[name] = nc.dram_tensor(name, arrays[name].shape, F32, kind="ExternalInput").ap()
    dram["xn_rows"] = nc.dram_tensor("xn_rows", [TOKENS, D], F32).ap()
    dram["y_rows"] = nc.dram_tensor("y_rows", [TOKENS, D], F32).ap()
    dram["q_parts"] = nc.dram_tensor("q_parts", [BATCH * HEADS, PARTS * DK, SEQ], BF16).ap()
    dram["k_parts"] = nc.dram_tensor("k_parts", [BATCH * HEADS, PARTS * DK, SEQ], BF16).ap()
    dram["m_rows"] = nc.dram_tensor("m_rows", [BUFS, GH * KT, PARTS, P], BF16).ap()
    out = nc.dram_tensor("out", [BATCH, SEQ, D], F32, kind="ExternalOutput").ap()
    layer(nc, dram, out)
    results = run_bass_kernel_spmd(nc, [arrays], core_ids=[0])
    return results.results[0]["out"]
```

```python
import concourse.bass as bass
from concourse import mybir
from contextlib import ExitStack

F32 = mybir.dt.float32
BF16 = mybir.dt.bfloat16
I32 = mybir.dt.int32
U32 = mybir.dt.uint32
ALU = mybir.AluOpType
ACT = mybir.ActivationFunctionType
AX = mybir.AxisListType

P = 128
BATCH, SEQ, D = 4, 1024, 128
TOKENS = BATCH * SEQ
TILES = TOKENS // P
QUAD = 4
QUADS = TILES // QUAD
HEADS, DK = 16, 8
EXPERTS, HID = 8, 512
HC = HID // P
SORTED = TILES + EXPERTS - 1
ROTATION = 6
W_ROTATION = 3
GATHERED = 5
TURNS = -(-SORTED // ROTATION)
LAST_TURN = SORTED - ROTATION * (TURNS - 1)
EPS = 1e-5

GH = 4
GROUPS = BATCH * HEADS // GH
GPB = HEADS // GH
KT = SEQ // P
HALF = 512
PARTS = 3
FILL = 96
BUFS = 3
STEPS = 2 * KT
P1_UNITS = 32
SCALE = float(DK) ** -0.5


def wait_unless_zero(engine, semaphore, count):
    if not (isinstance(count, int) and count == 0):
        engine.wait_ge(semaphore, count)


def layernorm(nc, dve, act, x_sb, xn_sb, stats, mv, rt, done, vsem, asem, half, arrive=None, span=(0, TILES), before=0,
              counted=False):
    tiles, steps = range(*span), 8 * before
    every = slice(*span)
    if half == "act":
        act.wait_ge(vsem, steps + 3)
        nc.scalar.activation(rt[:, 0, every], rt[:, 1, every], ACT.Sqrt).then_inc(asem, 1)
        return
    if not counted:
        for t in tiles:
            if arrive is not None and t % QUAD == 0:
                arrive(t // QUAD)
            last = nc.vector.bn_stats(stats[:, t, :], x_sb[:, t, :])
        last.then_inc(vsem, 1)
    dve.wait_ge(vsem, steps + 1)
    for t in tiles:
        last = nc.vector.bn_aggr(mv[:, t, :], stats[:, t, :])
    last.then_inc(vsem, 1)
    dve.wait_ge(vsem, steps + 2)
    nc.vector.tensor_scalar(rt[:, 1, every], mv[:, every, 1], EPS, None, ALU.add).then_inc(vsem, 1)
    dve.wait_ge(asem, before + 1)
    nc.vector.reciprocal(rt[:, 2, every], rt[:, 0, every]).then_inc(vsem, 1)
    dve.wait_ge(vsem, steps + 4)
    nc.vector.tensor_tensor(rt[:, 3, every], rt[:, 2, every], rt[:, 2, every], ALU.mult).then_inc(vsem, 1)
    dve.wait_ge(vsem, steps + 5)
    nc.vector.tensor_tensor(rt[:, 4, every], rt[:, 3, every], rt[:, 1, every], ALU.mult).then_inc(vsem, 1)
    dve.wait_ge(vsem, steps + 6)
    nc.vector.tensor_scalar(rt[:, 5, every], rt[:, 4, every], -0.5, 1.5, ALU.mult, ALU.add).then_inc(vsem, 1)
    dve.wait_ge(vsem, steps + 7)
    nc.vector.tensor_tensor(rt[:, 6, every], rt[:, 5, every], rt[:, 2, every], ALU.mult).then_inc(vsem, 1)
    dve.wait_ge(vsem, steps + 8)
    for t in tiles:
        ins = nc.vector.tensor_scalar(xn_sb[:, t, :], x_sb[:, t, :], mv[:, t, 0:1], rt[:, 6, t:t + 1],
                                      ALU.subtract, ALU.mult)
        if t % QUAD == QUAD - 1:
            ins.then_inc(done, 1)


class Setup:

    def __init__(self, nc, ctx, w, dram, q2, k2, vs):
        def sb(name, shape, dt):
            return ctx.enter_context(nc.sbuf_tensor(name, shape, dt))

        def sem(name):
            return ctx.enter_context(nc.semaphore(name))

        self.nc, self.w, self.dram = nc, w, dram
        self.q2, self.k2, self.vs = q2, k2, vs
        self.b1_rows = sb("b1_rows", [EXPERTS * HC, P], F32)
        self.b2_all = sb("b2_all", [P, EXPERTS, D], F32)
        self.relu_b1 = sb("relu_b1", [P, EXPERTS, HC], F32)
        self.idle = sb("idle", [P, EXPERTS, D], F32)
        self.total = sb("total", [P, D], F32)
        self.iota_i = sb("iota_i", [P, P], I32)
        self.partition_i = sb("partition_i", [P, 1], I32)
        self.small, self.w1_load, self.w2_load, self.b1_load = sem("small"), sem("w1_load"), sem("w2_load"), sem("b1_load")
        self.x_load = [sem(f"x_load{q}") for q in range(QUADS)]
        self.made, self.dve_step, self.b1_t, self.idle_done, self.filled = (
            sem("made"), sem("dve_step"), sem("b1_t"), sem("idle_done"), sem("filled"))

    def sync_loads(self, sp):
        dram, w = self.dram, self.w
        sp.dma_start(self.b1_rows[:, :], dram["L0_ffn_b1"].rearrange("e (c p) -> (e c) p", p=P)).then_inc(self.b1_load, 16)
        for q in range(QUADS):
            b, t = q * QUAD // KT, q * QUAD % KT
            sp.dma_start(w["x"][:, q * QUAD:(q + 1) * QUAD, :],
                         dram["L0_attn_x"][b, t * P:(t + QUAD) * P, :].rearrange("(t p) d -> p t d", p=P)).then_inc(self.x_load[q], 16)
        sp.dma_start(w["W2"][:, :, :, :], dram["L0_ffn_W2"].rearrange("e (c p) d -> p e c d", p=P)).then_inc(self.w2_load, 16)
        sp.dma_start(w["W1"][:, :, 0:HID], dram["L0_ffn_W1"].rearrange("e d h -> d e h")).then_inc(self.w1_load, 16)

    def scalar_loads(self, act):
        dram, w = self.dram, self.w
        for name, key in (("Wr", "L0_ffn_Wr"), ("Wq", "L0_attn_Wq"), ("Wk", "L0_attn_Wk"),
                          ("Wv", "L0_attn_Wv"), ("Wo", "L0_attn_Wo")):
            act.dma_start(w[name][:, 0:dram[key].shape[1]], dram[key]).then_inc(self.small, 16)
        for name, key in (("br", "L0_ffn_br"), ("bv", "L0_attn_bv"), ("bo", "L0_attn_bo")):
            act.dma_start(w[name][:, :], dram[key].partition_broadcast(P)).then_inc(self.small, 16)
        for name, key in (("bq", "L0_attn_bq"), ("bk", "L0_attn_bk")):
            act.dma_start(w[name][:, :], dram[key].rearrange("(p a) -> p a", a=1)).then_inc(self.small, 16)
        act.dma_start(self.b2_all[:, :, :], dram["L0_ffn_b2"].partition_broadcast(P)).then_inc(self.small, 16)

    def small_loaded(self, engine):
        engine.wait_ge(self.small, 16 * 11)

    def gpsimd_masks(self, pool):
        nc, w = self.nc, self.w
        nc.gpsimd.memset(w["Wr"][:, EXPERTS:], 0.0)
        nc.gpsimd.memset(w["ident"][:, :], 0.0).then_inc(self.made, 1)
        nc.gpsimd.memset(w["before"][:, :], 0.0).then_inc(self.made, 1)
        nc.gpsimd.memset(w["ones"][:, :], 1.0).then_inc(self.made, 1)
        nc.gpsimd.iota(self.iota_i[:, :], [[1, P]], base=0, channel_multiplier=0).then_inc(self.made, 1)
        nc.gpsimd.iota(self.partition_i[:, :], [[0, 1]], base=0, channel_multiplier=1).then_inc(self.made, 1)
        pool.wait_ge(self.made, 5)
        nc.gpsimd.affine_select(out=w["ident"][:, :], in_=w["ident"][:, :], compare_op=ALU.not_equal, fill=1.0,
                                base=0, pattern=[[-1, P]], channel_multiplier=1).then_inc(self.made, 1)
        nc.gpsimd.affine_select(out=w["before"][:, :], in_=w["before"][:, :], compare_op=ALU.is_ge, fill=1.0,
                                base=0, pattern=[[-1, P]], channel_multiplier=1).then_inc(self.made, 1)

    def gpsimd_fill(self, pool):
        pool.wait_ge(self.made, 7)
        for p in range(BUFS):
            if p:
                pool.wait_ge(self.filled, 5 * p)
            for rows, q_value, k_value in ((slice(64, FILL), 0.0, 0.0), (slice(FILL, P), 0.0, 1.0)):
                self.nc.gpsimd.memset(self.q2[p][rows, :, :], q_value).then_inc(self.filled, 1)
                self.nc.gpsimd.memset(self.k2[p][rows, :, :], k_value).then_inc(self.filled, 1)
                pool.wait_ge(self.filled, 5 * p + (2 if rows.start == 64 else 4))
            self.nc.gpsimd.memset(self.vs[p][:, :, :, :], 1.0).then_inc(self.filled, 1)

    def tensor_biases(self, pe):
        pe.wait_ge(self.b1_load, 16)
        pe.wait_ge(self.made, 7)
        self.nc.tensor.transpose(self.ps_b1[:, 0:EXPERTS * HC], self.b1_rows[:, :],
                                 self.w["ident"][0:EXPERTS * HC, 0:EXPERTS * HC]).then_inc(self.b1_t, 1)
        self.small_loaded(pe)

    def tensor_idle(self, pe):
        pe.wait_ge(self.w2_load, 16)
        pe.wait_ge(self.dve_step, 2)
        for e in range(EXPERTS):
            for c in range(HC):
                last = self.nc.tensor.matmul(self.ps_idle[:, e, :], self.relu_b1[:, e, c:c + 1].to_broadcast([P, P]),
                                             self.w["W2"][:, e, c, :], start=(c == 0), stop=(c == HC - 1))
        last.then_inc(self.idle_done, 1)

    def vector_constants(self, dve):
        nc, w = self.nc, self.w
        dve.wait_ge(self.b1_t, 1)
        nc.vector.tensor_copy(w["W1"][:, :, HID:], self.ps_b1[:, 0:EXPERTS * HC].rearrange("p (e c) -> p e c", e=EXPERTS)).then_inc(self.dve_step, 1)
        nc.vector.tensor_scalar(self.relu_b1[:, :, :].rearrange("p e c -> p (e c)"), self.ps_b1[:, 0:EXPERTS * HC],
                                0.0, None, ALU.max).then_inc(self.dve_step, 1)
        dve.wait_ge(self.made, 7)
        nc.vector.tensor_copy(w["iota"][:, :], self.iota_i[:, :])
        nc.vector.tensor_copy(w["iota_b"][:, :], self.iota_i[:, :])
        nc.vector.tensor_copy(w["partition"][:, :], self.partition_i[:, :])
        nc.vector.memset(w["seg"][:, :, :], 1.0).then_inc(self.dve_step, 1)
        dve.wait_ge(self.dve_step, 3)
        nc.vector.memset(w["seg"][:, :, 0:1], 0.0)
        nc.vector.tensor_scalar(w["rank8"][:, :], w["iota"][:, 0:EXPERTS], -1.0, float(EXPERTS), ALU.mult, ALU.add).then_inc(self.dve_step, 1)
        dve.wait_ge(self.dve_step, 4)

    def vector_idle(self, dve):
        dve.wait_ge(self.idle_done, 1)
        self.nc.vector.tensor_copy(self.idle[:, :, :], self.ps_idle[:, :, :]).then_inc(self.dve_step, 1)

    def vector_rest(self, dve):
        nc, w = self.nc, self.w
        dve.wait_ge(self.dve_step, 5)
        nc.vector.tensor_tensor(self.b2_all[:, :, :], self.idle[:, :, :], self.b2_all[:, :, :], ALU.add).then_inc(self.dve_step, 1)
        dve.wait_ge(self.dve_step, 6)
        nc.vector.tensor_reduce(self.total[:, :], self.b2_all[:, :, :].rearrange("p e d -> p d e"), AX.X, ALU.add).then_inc(self.dve_step, 1)
        dve.wait_ge(self.dve_step, 7)
        nc.vector.tensor_tensor(w["rest"][:, :, :], self.total[:, :].unsqueeze(1).to_broadcast([P, EXPERTS, D]),
                                self.idle[:, :, :], ALU.subtract).then_inc(self.dve_step, 1)
        dve.wait_ge(self.dve_step, 8)


def ffn(nc, w, dram, tag, xn_sb, out, operands=None, ready=0):
    with ExitStack() as ctx:
        def sb(name, shape, dt):
            return ctx.enter_context(nc.sbuf_tensor(name + tag, shape, dt))

        def pb(name, shape):
            return ctx.enter_context(nc.psum_tensor(name + tag, shape, F32))

        def sem(name):
            return ctx.enter_context(nc.semaphore(name + tag))

        x_sb = w["x"]
        source_i = sb("source_i", [P, SORTED], U32)
        target_i = sb("target_i", [P, SORTED], U32)
        setup = Setup(nc, ctx, w, dram, *operands) if operands else None
        expert_i = sb("expert_i", [1, SORTED], I32)

        with ExitStack() as sub:
            def sb2(name, shape, dt):
                return sub.enter_context(nc.sbuf_tensor(name + tag, shape, dt))

            def sem2(name):
                return sub.enter_context(nc.semaphore(name + tag))

            stats = sb2("stats", [P, TILES, 6], F32)
            mv = sb2("mv", [P, TILES, 2], F32)
            rt = sb2("rt", [P, 7, TILES], F32)
            xnT = sb2("xnT", [P, QUADS, QUAD * P], F32)
            logitT = sb2("logitT", [P, 2, QUAD * P], F32)
            logit = sb2("logit", [P, TILES, EXPERTS], F32)
            best = sb2("best", [P, TILES], F32)
            first = sb2("first", [P, TILES, EXPERTS], F32)
            ranked = sb2("ranked", [P, TILES, EXPERTS], F32)
            firstmax = sb2("firstmax", [P, TILES], F32)
            onehot = sb2("onehot", [P, TILES, EXPERTS], BF16)
            count = sb2("count", [P, EXPERTS, TILES], F32)
            upto = sb2("upto", [P, EXPERTS, TILES], F32)
            cmp = sb2("cmp", [P, EXPERTS, TILES], F32)
            ntiles = sb2("ntiles", [P, EXPERTS], F32)
            end = sb2("end", [P, EXPERTS], F32)
            base = sb2("base", [P, EXPERTS], F32)
            place = sb2("place", [P, EXPERTS, TILES], F32)
            slot_f = sb2("slot_f", [P, TILES], F32)
            passed = sb2("passed", [1, SORTED, EXPERTS], F32)
            expert_f = sb2("expert_f", [1, SORTED], F32)
            tile_i = sb2("tile_i", [P, TILES], I32)
            rounded, excess = sb2("rounded", [P, TILES], F32), sb2("excess", [P, TILES], F32)
            tile_at, in_tile = sb2("tile_at", [P, TILES], F32), sb2("in_tile", [P, TILES], F32)
            marks = sb2("marks", [P, TILES, 3, SORTED], BF16)
            columns = sb2("columns", [P, TILES, P], BF16)
            found = sb2("found", [P, 3, SORTED], F32)
            source = sb2("source", [P, SORTED], F32)
            target = sb2("target", [P, SORTED], F32)
            ps_t = [sub.enter_context(nc.psum_tensor(f"ps_t{p}" + tag, [P, QUAD * P], F32)) for p in range(2)]
            ps_f = sub.enter_context(nc.psum_tensor("ps_f" + tag, [P, HALF], F32))
            ps_lT = sub.enter_context(nc.psum_tensor("ps_lT" + tag, [P, QUAD * P], F32))
            ps_l = sub.enter_context(nc.psum_tensor("ps_l" + tag, [P, EXPERTS, D], F32))
            ps_r = sub.enter_context(nc.psum_tensor("ps_r" + tag, [P, 2, TILES * EXPERTS], F32))
            vstep, astep, normed, routed = sem2("vstep"), sem2("astep"), sem2("normed"), sem2("routed")
            t_full, t_out, lT_full, lT_out, l_full = (sem2(n) for n in ("t_full", "t_out", "lT_full", "lT_out", "l_full"))
            r_full, column, f_full, stored = sem2("r_full"), sem2("column"), sem2("f_full"), sem2("xn_stored")

            if setup:
                setup.ps_b1, setup.ps_idle = ps_f, ps_l

            with nc.Block() as block:
                @block.vector
                def _(dve):
                    if setup:
                        setup.vector_constants(dve)
                    layernorm(nc, dve, None, x_sb, xn_sb, stats, mv, rt, normed, vstep, astep, "dve",
                              (lambda q: dve.wait_ge(setup.x_load[q], 16)) if setup else None, span=(QUAD * ready, TILES))
                    if setup:
                        setup.small_loaded(dve)
                    for h in range(2):
                        dve.wait_ge(l_full, h + 1)
                        last = nc.vector.tensor_tensor(
                            logit[:, h * TILES // 2:(h + 1) * TILES // 2, :].rearrange("p (j i) e -> p j i e", i=QUAD),
                            ps_l[:, h * QUAD:(h + 1) * QUAD, :].rearrange("p i (j e) -> p j i e", j=QUAD)[:, :, :, 0:EXPERTS],
                            w["br"][:, :].unsqueeze(1).unsqueeze(1).to_broadcast([P, QUAD, QUAD, EXPERTS]), ALU.add)
                    last.then_inc(routed, 1)
                    dve.wait_ge(routed, 1)
                    nc.vector.tensor_reduce(best[:, :], logit[:, :, :], AX.X, ALU.max).then_inc(routed, 1)
                    dve.wait_ge(routed, 2)
                    nc.vector.tensor_tensor(first[:, :, :], logit[:, :, :], best[:, :].unsqueeze(2).to_broadcast([P, TILES, EXPERTS]),
                                            ALU.is_ge).then_inc(routed, 1)
                    dve.wait_ge(routed, 3)
                    nc.vector.tensor_tensor(ranked[:, :, :], first[:, :, :],
                                            w["rank8"][:, :].unsqueeze(1).to_broadcast([P, TILES, EXPERTS]), ALU.mult).then_inc(routed, 1)
                    dve.wait_ge(routed, 4)
                    nc.vector.tensor_reduce(firstmax[:, :], ranked[:, :, :], AX.X, ALU.max).then_inc(routed, 1)
                    dve.wait_ge(routed, 5)
                    nc.vector.tensor_tensor(onehot[:, :, :], ranked[:, :, :], firstmax[:, :].unsqueeze(2).to_broadcast([P, TILES, EXPERTS]),
                                            ALU.is_equal).then_inc(routed, 1)
                    dve.wait_ge(r_full, 1)
                    nc.vector.tensor_copy(count[:, :, :], ps_r[:, 1, :].rearrange("p (t e) -> p e t", e=EXPERTS)).then_inc(routed, 1)
                    dve.wait_ge(routed, 7)
                    nc.vector.tensor_tensor_scan(upto[:, :, :].rearrange("p e t -> p (e t)"), w["seg"][:, :, :].rearrange("p e t -> p (e t)"),
                                                 count[:, :, :].rearrange("p e t -> p (e t)"), 0.0, ALU.mult, ALU.add).then_inc(routed, 1)
                    dve.wait_ge(routed, 8)
                    nc.vector.scalar_tensor_tensor(out=cmp[:, :, :], in0=w["iota"][:, 0:TILES].unsqueeze(1).to_broadcast([P, EXPERTS, TILES]),
                                                   scalar=float(P), in1=upto[:, :, TILES - 1:TILES].to_broadcast([P, EXPERTS, TILES]),
                                                   op0=ALU.mult, op1=ALU.is_lt).then_inc(routed, 1)
                    dve.wait_ge(routed, 9)
                    nc.vector.tensor_reduce(ntiles[:, :], cmp[:, :, :], AX.X, ALU.add).then_inc(routed, 1)
                    dve.wait_ge(routed, 10)
                    nc.vector.tensor_tensor_scan(end[:, :], w["seg"][:, 0, 1:1 + EXPERTS], ntiles[:, :], 0.0, ALU.mult, ALU.add).then_inc(routed, 1)
                    dve.wait_ge(routed, 11)
                    nc.vector.tensor_tensor(base[:, :], end[:, :], ntiles[:, :], ALU.subtract).then_inc(routed, 1)
                    nc.vector.tensor_tensor(place[:, :, :], upto[:, :, :], count[:, :, :], ALU.subtract).then_inc(routed, 1)
                    nc.vector.tensor_tensor(passed[:, :, :], end[0:1, :].unsqueeze(1).to_broadcast([1, SORTED, EXPERTS]),
                                            w["iota"][0:1, 0:SORTED].unsqueeze(2).to_broadcast([1, SORTED, EXPERTS]), ALU.is_le).then_inc(routed, 1)
                    dve.wait_ge(routed, 14)
                    nc.vector.tensor_reduce(expert_f[:, :], passed[:, :, :], AX.X, ALU.add).then_inc(routed, 1)
                    nc.vector.scalar_tensor_tensor(out=cmp[:, :, :], in0=base[:, :].unsqueeze(2).to_broadcast([P, EXPERTS, TILES]),
                                                   scalar=float(P), in1=place[:, :, :], op0=ALU.mult, op1=ALU.add).then_inc(routed, 1)
                    dve.wait_ge(routed, 16)
                    nc.vector.tensor_scalar(expert_i[:, :], expert_f[:, :], float(EXPERTS - 1), None, ALU.min).then_inc(routed, 1)
                    nc.vector.tensor_tensor(place[:, :, :], cmp[:, :, :], ps_r[:, 0, :].rearrange("p (t e) -> p e t", e=EXPERTS),
                                            ALU.add).then_inc(routed, 1)
                    dve.wait_ge(routed, 18)
                    nc.vector.tensor_tensor(first[:, :, :], place[:, :, :].rearrange("p e t -> p t e"), onehot[:, :, :], ALU.mult).then_inc(routed, 1)
                    dve.wait_ge(routed, 19)
                    nc.vector.tensor_reduce(slot_f[:, :], first[:, :, :], AX.X, ALU.add).then_inc(routed, 1)
                    dve.wait_ge(routed, 20)
                    nc.vector.tensor_scalar(tile_i[:, :], slot_f[:, :], 1.0 / P, None, ALU.mult).then_inc(routed, 1)
                    dve.wait_ge(routed, 21)
                    nc.vector.tensor_copy(rounded[:, :], tile_i[:, :]).then_inc(routed, 1)
                    dve.wait_ge(routed, 22)
                    nc.vector.scalar_tensor_tensor(out=excess[:, :], in0=rounded[:, :], scalar=float(P), in1=slot_f[:, :],
                                                   op0=ALU.mult, op1=ALU.is_gt).then_inc(routed, 1)
                    dve.wait_ge(routed, 23)
                    nc.vector.tensor_tensor(tile_at[:, :], rounded[:, :], excess[:, :], ALU.subtract).then_inc(routed, 1)
                    dve.wait_ge(routed, 24)
                    nc.vector.scalar_tensor_tensor(out=in_tile[:, :], in0=tile_at[:, :], scalar=-float(P), in1=slot_f[:, :],
                                                   op0=ALU.mult, op1=ALU.add).then_inc(routed, 1)
                    nc.vector.tensor_tensor(marks[:, :, 2, :], w["iota_b"][:, 0:SORTED].unsqueeze(1).to_broadcast([P, TILES, SORTED]),
                                            tile_at[:, :].unsqueeze(2).to_broadcast([P, TILES, SORTED]), ALU.is_equal).then_inc(routed, 1)
                    dve.wait_ge(routed, 26)
                    nc.vector.tensor_tensor(marks[:, :, 0, :], marks[:, :, 2, :],
                                            w["iota_b"][:, 0:TILES].unsqueeze(2).to_broadcast([P, TILES, SORTED]), ALU.mult)
                    nc.vector.tensor_scalar(marks[:, :, 1, :], marks[:, :, 2, :], w["partition"][:, 0:1], None, ALU.mult)
                    for t in range(TILES):
                        last = nc.vector.tensor_scalar(columns[:, t, :], w["iota_b"][:, :], in_tile[:, t:t + 1], None, ALU.is_equal)
                        if t % QUAD == QUAD - 1:
                            last.then_inc(column, 1)
                    if setup:
                        setup.vector_idle(dve)
                    dve.wait_ge(f_full, 1)
                    nc.vector.tensor_copy(found[:, :, :], ps_f[:, 0:3 * SORTED].rearrange("p (a s) -> p a s", a=3)).then_inc(routed, 1)
                    dve.wait_ge(routed, 27)
                    nc.vector.scalar_tensor_tensor(out=source[:, :], in0=found[:, 0, :], scalar=float(P), in1=found[:, 1, :],
                                                   op0=ALU.mult, op1=ALU.add).then_inc(routed, 1)
                    dve.wait_ge(routed, 28)
                    nc.vector.tensor_copy(source_i[:, :], source[:, :])
                    nc.vector.scalar_tensor_tensor(out=target[:, :], in0=found[:, 2, :], scalar=-float(TOKENS), in1=source[:, :],
                                                   op0=ALU.mult, op1=ALU.add).then_inc(routed, 1)
                    dve.wait_ge(routed, 29)
                    nc.vector.tensor_scalar(target_i[:, :], target[:, :], float(TOKENS), None, ALU.add).then_inc(routed, 1)

                if setup:
                    @block.gpsimd
                    def _(pool):
                        setup.gpsimd_masks(pool)
                        setup.gpsimd_fill(pool)

                @block.scalar
                def _(act):
                    if setup:
                        setup.scalar_loads(act)
                    for q in range(QUADS):
                        if q == min(ready, 1):
                            layernorm(nc, None, act, x_sb, xn_sb, stats, mv, rt, normed, vstep, astep, "act", span=(QUAD * ready, TILES))
                        act.wait_ge(t_full, q + 1)
                        nc.scalar.activation(xnT[:, q, :], ps_t[q % 2][:, :], ACT.Copy).then_inc(t_out, 1)
                        if q in (QUAD, QUADS - 1):
                            h = q // (QUAD + 1)
                            act.wait_ge(lT_full, h + 1)
                            nc.scalar.activation(logitT[:, h, :], ps_lT[:, :], ACT.Copy).then_inc(lT_out, 1)

                @block.tensor
                def _(pe):
                    def turn(q):
                        if q >= ready:
                            pe.wait_ge(normed, q + 1 - ready)
                        if q >= 2:
                            pe.wait_ge(t_out, q - 1)
                        for i in range(QUAD):
                            last = nc.tensor.transpose(ps_t[q % 2][:, i * P:(i + 1) * P], xn_sb[:, QUAD * q + i, :], w["ident"][:, :])
                        last.then_inc(t_full, 1)

                    def logits(h):
                        pe.wait_ge(t_out, QUAD * (h + 1))
                        wait_unless_zero(pe, lT_out, h)
                        for j in range(QUAD):
                            last = nc.tensor.matmul(ps_lT[32 * j:32 * (j + 1), :], w["Wr"][:, :], xnT[:, QUAD * h + j, :], start=True, stop=True)
                        last.then_inc(lT_full, 1)

                    def turn_logits(h):
                        pe.wait_ge(lT_out, h + 1)
                        for i in range(QUAD):
                            last = nc.tensor.transpose(ps_l[:, QUAD * h + i, :], logitT[:, h, i * P:(i + 1) * P], w["ident"][:, :])
                        last.then_inc(l_full, 1)

                    if setup:
                        setup.tensor_biases(pe)
                    for q in range(QUAD + 1):
                        turn(q)
                    logits(0)
                    turn(QUAD + 1)
                    turn_logits(0)
                    for q in range(QUAD + 2, QUADS):
                        turn(q)
                    logits(1)
                    turn_logits(1)
                    pe.wait_ge(routed, 6)
                    chosen = onehot[:, :, :].rearrange("p t e -> p (t e)")
                    nc.tensor.matmul(ps_r[:, 0, :], w["before"][:, :], chosen, start=True, stop=True)
                    nc.tensor.matmul(ps_r[:, 1, :], w["ones"][:, :], chosen, start=True, stop=True).then_inc(r_full, 1)
                    if setup:
                        setup.tensor_idle(pe)
                    for t in range(TILES):
                        if t % QUAD == 0:
                            pe.wait_ge(column, t // QUAD + 1)
                        last = nc.tensor.matmul(ps_f[:, 0:3 * SORTED], columns[:, t, :], marks[:, t, :, :].rearrange("p a s -> p (a s)"),
                                                start=(t == 0), stop=(t == TILES - 1))
                    last.then_inc(f_full, 1)

                @block.sync
                def _(sp):
                    def token_rows(q, half):
                        return dram["token_rows"][q * QUAD * P:(q + 1) * QUAD * P, half * D:(half + 1) * D].rearrange("(t p) d -> p t d", p=P)

                    if setup:
                        setup.sync_loads(sp)
                    for q in range(QUADS):
                        if setup:
                            sp.wait_ge(setup.x_load[q], 16)
                        sp.dma_start(token_rows(q, 1), x_sb[:, q * QUAD:(q + 1) * QUAD, :]).then_inc(stored, 16)
                    for q in range(QUADS):
                        if q >= ready:
                            sp.wait_ge(normed, q + 1 - ready)
                        sp.dma_start(token_rows(q, 0), xn_sb[:, q * QUAD:(q + 1) * QUAD, :]).then_inc(stored, 16)
                    sp.wait_ge(stored, 2 * 16 * QUADS)
                    if setup:
                        sp.wait_ge(setup.w1_load, 16)

        with ExitStack() as sub:
            def sb2(name, shape, dt):
                return sub.enter_context(nc.sbuf_tensor(name + tag, shape, dt))

            def sem2(name):
                return sub.enter_context(nc.semaphore(name + tag))

            def sems2(name):
                return [sub.enter_context(nc.semaphore(f"{name}{p}" + tag)) for p in range(ROTATION)]

            def banks(name):
                return [sub.enter_context(nc.psum_tensor(f"{name}{p}" + tag, [P, HALF], F32)) for p in range(2)]

            xs = sb2("xs", [P, ROTATION, 2 * D], F32)
            xsT = sb2("xsT", [P, 2, P], F32)
            w1s = sb2("w1s", [P, W_ROTATION, HID + HC], F32)
            hT = sb2("hT", [P, 2, HID], F32)
            y_sum = sb2("y_sum", [P, 2, D], F32)
            ys = sb2("ys", [P, ROTATION, D], F32)
            target = (dram["x_rows"] if out is None else out.rearrange("b s d -> (b s) d"))
            summed = sem2("summed")
            ps_x, ps_y, ps_h = banks("ps_x"), banks("ps_y"), (banks("ps_ha"), banks("ps_hb"))
            x_in, y_stored = sems2("x_in"), sems2("y_stored")
            x_t, xT_out, w1_in = sem2("x_t"), sem2("xT_out"), sem2("w1_in")
            h_full, h_act, h_dve, y_full, y_out = (sem2(n) for n in ("h_full", "h_act", "h_dve", "y_full", "y_out"))

            def turns(engine, turn):
                turn(0)
                with engine.Fori(1, TURNS - 1) as i:
                    turn(i)
                turn(TURNS - 1, last=True)

            def wait_tile(engine, semaphore, i, r, back=0):
                if not (isinstance(i, int) and ROTATION * i + r - back < 0):
                    engine.wait_ge(semaphore, ROTATION * i + r - back + 1)

            def expert(engine, i, r):
                return engine.value_load(expert_i[0:1, bass.ds(ROTATION * i + r, 1)], min_val=0, max_val=EXPERTS - 1)

            with nc.Block() as block:
                @block.gpsimd
                def _(pool):
                    def gather(i, r):
                        nc.gpsimd.indirect_dma_start(xs[:, r, :], None, dram["token_rows"],
                                                     bass.IndirectOffsetOnAxis(ap=source_i[:, ROTATION * i + r:ROTATION * i + r + 1], axis=0)).then_inc(x_in[r], 16)

                    def scatter(i, r):
                        wait_tile(pool, y_out, i, r)
                        nc.gpsimd.indirect_dma_start(target, bass.IndirectOffsetOnAxis(ap=target_i[:, ROTATION * i + r:ROTATION * i + r + 1], axis=0),
                                                     ys[:, r, :], None, bounds_check=TOKENS - 1, oob_is_err=False).then_inc(y_stored[r], 16)

                    for t in range(GATHERED):
                        gather(0, t)
                    for t in range(SORTED):
                        ahead = t + GATHERED
                        if ahead < SORTED:
                            if ahead >= ROTATION:
                                wait_tile(pool, y_out, 0, ahead - ROTATION)
                            gather(ahead // ROTATION, ahead % ROTATION)
                        if t >= ROTATION - GATHERED:
                            done = t - (ROTATION - GATHERED)
                            scatter(done // ROTATION, done % ROTATION)
                    for t in range(SORTED - (ROTATION - GATHERED), SORTED):
                        scatter(t // ROTATION, t % ROTATION)
                    for r in range(ROTATION):
                        pool.wait_ge(y_stored[r], 16 * (TURNS if r < LAST_TURN else TURNS - 1))

                @block.tensor
                def _(pe):
                    def turned(i, r):
                        pe.wait_ge(x_in[r], 16 * i + 16)
                        wait_tile(pe, xT_out, i, r, 2)
                        nc.tensor.transpose(ps_x[r % 2][:, 0:P], xs[:, r, 0:D], w["ident"][:, :]).then_inc(x_t, 1)

                    def up(i, r):
                        wait_tile(pe, xT_out, i, r)
                        wait_tile(pe, w1_in, i, r)
                        wait_tile(pe, h_act, i, r, 2)
                        wait_tile(pe, h_dve, i, r, 2)
                        for c in range(HC):
                            last = nc.tensor.matmul(ps_h[c // 2][r % 2][:, (c % 2) * P:(c % 2 + 1) * P], w1s[:, r % W_ROTATION, c * P:(c + 1) * P],
                                                    xsT[:, r % 2, :], start=True, stop=True)
                        last.then_inc(h_full, 1)

                    def down(i, r, e):
                        wait_tile(pe, h_act, i, r)
                        wait_tile(pe, h_dve, i, r)
                        wait_tile(pe, summed, i, r, 2)
                        for c in range(HC):
                            last = nc.tensor.matmul(ps_y[r % 2][:, 0:D], hT[:, r % 2, c * P:(c + 1) * P],
                                                    w["W2"][:, bass.ds(e, 1), c, :].rearrange("p a d -> p (a d)"),
                                                    start=(c == 0), stop=(c == HC - 1))
                        last.then_inc(y_full, 1)

                    turned(0, 0)
                    turned(0, 1)
                    up(0, 0)

                    def turn(i, last=False):
                        tiles = LAST_TURN if last else ROTATION
                        for r in range(tiles):
                            e = expert(pe, i, r)
                            if r + 1 < tiles:
                                up(i, r + 1)
                            elif not last:
                                up(i + 1, 0)
                            if r + 2 < tiles:
                                turned(i, r + 2)
                            elif not last:
                                turned(i + 1, r + 2 - ROTATION)
                            down(i, r, e)

                    turns(pe, turn)

                @block.scalar
                def _(act):
                    def turned(i, r):
                        wait_tile(act, x_t, i, r)
                        wait_tile(act, h_full, i, r, 2)
                        nc.scalar.activation(xsT[:, r % 2, :], ps_x[r % 2][:, 0:P], ACT.Copy).then_inc(xT_out, 1)

                    def weights(i, r):
                        e = expert(act, i, r)
                        wait_tile(act, h_full, i, r, W_ROTATION)
                        wait_tile(act, h_dve, i, r, W_ROTATION)
                        wait_tile(act, h_act, i, r, W_ROTATION)
                        nc.scalar.activation(w1s[:, r % W_ROTATION, :], w["W1"][:, bass.ds(e, 1), :].rearrange("p a h -> p (a h)"), ACT.Copy).then_inc(w1_in, 1)

                    def relu(i, r):
                        wait_tile(act, w1_in, i, r)
                        wait_tile(act, h_full, i, r)
                        wait_tile(act, y_full, i, r, 2)
                        for c in range(2):
                            last = nc.scalar.activation(hT[:, r % 2, c * P:(c + 1) * P], ps_h[0][r % 2][:, c * P:(c + 1) * P], ACT.Relu,
                                                        bias=w1s[:, r % W_ROTATION, HID + c:HID + c + 1])
                        last.then_inc(h_act, 1)

                    for r in range(3):
                        weights(0, r)
                    turned(0, 0)
                    turned(0, 1)
                    relu(0, 0)

                    def turn(i, last=False):
                        tiles = LAST_TURN if last else ROTATION
                        for r in range(tiles):
                            if r + 2 < tiles:
                                turned(i, r + 2)
                            elif not last:
                                turned(i + 1, r + 2 - ROTATION)
                            if r + 1 < tiles:
                                relu(i, r + 1)
                            elif not last:
                                relu(i + 1, 0)
                            if r + 3 < tiles:
                                weights(i, r + 3)
                            elif not last:
                                weights(i + 1, r + 3 - ROTATION)

                    turns(act, turn)

                @block.vector
                def _(dve):
                    def relu(i, r):
                        wait_tile(dve, w1_in, i, r)
                        wait_tile(dve, h_full, i, r)
                        wait_tile(dve, y_full, i, r, 2)
                        for c in range(2, HC):
                            last = nc.vector.tensor_scalar(hT[:, r % 2, c * P:(c + 1) * P], ps_h[1][r % 2][:, (c - 2) * P:(c - 1) * P],
                                                           w1s[:, r % W_ROTATION, HID + c:HID + c + 1], 0.0, ALU.add, ALU.max)
                        last.then_inc(h_dve, 1)

                    def result(i, r, e):
                        wait_tile(dve, y_full, i, r)
                        wait_unless_zero(dve, y_stored[r], 16 * i)
                        nc.vector.tensor_tensor(y_sum[:, r % 2, :], ps_y[r % 2][:, 0:D],
                                                w["rest"][:, bass.ds(e, 1), :].rearrange("p a d -> p (a d)"), ALU.add).then_inc(summed, 1)
                        wait_tile(dve, summed, i, r)
                        nc.vector.scalar_tensor_tensor(out=ys[:, r, :], in0=y_sum[:, r % 2, :], scalar=0.5, in1=xs[:, r, D:],
                                                       op0=ALU.mult, op1=ALU.add).then_inc(y_out, 1)

                    if setup:
                        setup.vector_rest(dve)
                    relu(0, 0)

                    def turn(i, last=False):
                        tiles = LAST_TURN if last else ROTATION
                        for r in range(tiles):
                            e = expert(dve, i, r)
                            if r + 1 < tiles:
                                relu(i, r + 1)
                            elif not last:
                                relu(i + 1, 0)
                            result(i, r, e)

                    turns(dve, turn)


class Body:

    def __init__(self, g, buf, use):
        self.g, self.buf, self.use = g, buf, use

    def ahead(self, n):
        return Body(self.g + n, (self.buf + n) % BUFS, self.use + (self.buf + n) // BUFS)

    def unit(self, n):
        if isinstance(self.g, int) and self.g == 0:
            n += PROLOGUE
            return n % 2, n // 2
        start = PROLOGUE - 1
        if isinstance(self.g, int) and self.g == GROUPS - 1:
            n -= AHEAD - 2 * MERGED_14
        return n % 2, UNITS // 2 * self.g + (start + n) // 2


AHEAD = 8
UNITS = P1_UNITS + 2
PROLOGUE = P1_UNITS + 1 + AHEAD


MERGED = 6
MERGED_14 = 2


def plan(first=False, finish=True, start=True):
    steps, own = [], (P1_UNITS - AHEAD) // 2
    if start:
        quads, begin = range(0), 0
    elif finish:
        quads, begin = range(MERGED_14), STEPS - 2 * MERGED_14
    else:
        quads, begin = range(MERGED_14, MERGED), 4
    merged = [(kind, 0, q) for q in quads for kind in ("c", "y")]
    for k in range(STEPS):
        if k < own:
            here = [("max", 1, AHEAD + 2 * k + m) for m in range(2)] if finish else []
        else:
            here = [("max", 2, 2 * (k - own) + m) for m in range(2)] if start else []
        here += [("o", -1, 0)] if k == 5 and not first else []
        here += [("m", 1, 0)] if k == own and finish else []
        steps.append(here + merged[max(k - begin, 0):max(k - begin + 1, 0)])
    return steps


def last_units():
    return [("o", 0, 0)] + [(kind, 0, q) for q in range(MERGED, QUADS) for kind in ("c", "y")]


def place(what, of):
    for g in range(GROUPS - 4, GROUPS):
        units = [unit for units in plan(finish=g + 1 < GROUPS, start=g + 2 < GROUPS) for unit in units]
        if g == GROUPS - 1:
            units += last_units()
        for n, (kind, ahead, which) in enumerate(units):
            if (kind, g + ahead if kind == "o" else which) == (what, of):
                return Body(g, g % BUFS, g // BUFS).unit(n)
    raise ValueError((what, of))


def bodies(engine, body):
    at = Body(0, 0, 0)
    body(at, first=True)
    loops = (GROUPS - 3) // BUFS
    with engine.Fori(0, loops) as i:
        for n in range(1, BUFS + 1):
            body(Body(BUFS * i + n, n % BUFS, i + n // BUFS))
    for g in range(1 + BUFS * loops, GROUPS):
        body(Body(g, g % BUFS, g // BUFS), finish=g + 1 < GROUPS, start=g + 2 < GROUPS)


FIRST = 2
EARLY = 2
BETWEEN = 6


def prologue():
    project = ("query", "key", "value")
    items = []
    for q in range(EARLY):
        ahead = [] if q in (FIRST - 1, EARLY - 1) else [("turn", q + 1)]
        items += ([("turn", q)] if q in (0, FIRST) else []) + ahead + [(kind, q) for kind in project]
    for n in range(PROLOGUE):
        items.append(("unit", n))
        q, place = EARLY + n // BETWEEN, n % BETWEEN
        if q < QUADS and place < 4:
            items.append((("turn",) + project)[place:place + 1] + (q,))
    return items


def attention(nc, w, dram, q2, k2, vs, v_sb, ctx_sb):
    with ExitStack() as ctx:
        def sb(name, shape, dt):
            return ctx.enter_context(nc.sbuf_tensor(name, shape, dt))

        def sem(name):
            return ctx.enter_context(nc.semaphore(name))

        def sems(name, n):
            return [ctx.enter_context(nc.semaphore(f"{name}{p}")) for p in range(n)]

        probs = sb("probs", [P, 2, GH, HALF], F32)
        exact, rem = probs[:, :, 0:2, :], probs[:, :, 2:4, :]
        xn_sb = ctx_sb[:, :, :, :].rearrange("p g t c -> p (g t c)").rearrange("p (t d) -> p t d", d=D)
        stats, mv, rt = sb("stats_a", [P, TILES, 6], F32), sb("mv_a", [P, TILES, 2], F32), sb("rt_a", [P, 7, TILES], F32)
        xnT = sb("xnT_a", [P, 2, HALF], F32)
        parts = sb("parts", [P, 2, 2, PARTS, HALF], BF16)
        rows, plus_bo = (sb(name, [P, 2, QUAD, D], F32) for name in ("ctx_rows", "plus_bo"))
        cT = xnT
        xn_next = v_sb[:, :, :, :].rearrange("p g t c -> p (g t c)").rearrange("p (t d) -> p t d", d=D)
        oT = sb("oT", [P, 2, HALF], F32)
        maxima = sb("maxima", [P, GH, KT, 2], F32)
        top = sb("top", [P, GH * KT], F32)
        mpart = [sb(f"mpart{p}", [GH * KT, PARTS, P], BF16) for p in range(BUFS)]
        mrest = sb("mrest", [GH * KT, P], F32)
        rden = sb("rden", [P, KT, GH, 1], F32)
        ps_m = [ctx.enter_context(nc.psum_tensor(f"ps_m{p}", [P, 2, HALF], F32)) for p in range(2)]
        ps_s = [ctx.enter_context(nc.psum_tensor(f"ps_s{n}", [P, HALF], F32)) for n in range(3)]
        ps_o = ctx.enter_context(nc.psum_tensor("ps_o", [P, HALF], F32))
        ps_t, ps_q, ps_k, ps_v = ps_s[0], ps_s[1], ps_s[2], ps_o

        loaded, in_m, in_v = sems("loaded", BUFS), sems("in_m", BUFS), sems("in_v", BUFS)
        unit_full, unit_free = sems("unit_full", 2), sems("unit_free", 2)
        scored, exped, step_done, o_out = sem("scored"), sem("exped"), sem("step_done"), sem("o_out")
        in_rows, residual, vstep_2, astep_2, normed_2 = (sem(n) for n in ("in_rows", "residual", "vstep_2a", "astep_2a", "normed_2a"))
        combined, split, recip = sem("combined"), sem("split"), sem("recip")

        vstep, astep, normed = sem("vstep_a"), sem("astep_a"), sem("normed_a")
        t_full, t_out, qk_full, high = sem("t_full_a"), sem("t_out_a"), sem("qk_full"), sem("high")
        v_full, v_out, parts_stored = sem("v_full"), sem("v_out"), sems("parts_stored", 2)
        x_loaded, left, middle, low = (sems(n, QUADS) for n in ("x_loaded_a", "left", "middle", "low"))

        LOADS = PARTS + PARTS * PARTS

        def gather_rows(engine, copy, q):
            b, t = q * QUAD // KT, q * QUAD % KT
            if q >= 2:
                slot, used = place("c", q - 2)
                engine.wait_ge(unit_full[slot], used + 1)
            copy(rows[:, q % 2, :, :].rearrange("p t (g c) -> p t g c", g=GPB),
                 ctx_sb[:, b * GPB:(b + 1) * GPB, t:t + QUAD, :].rearrange("p g t c -> p t g c")).then_inc(in_rows, 1)

        def remainders(engine, nc_engine, q):
            p = q % 2
            if q >= 2:
                engine.wait_ge(low[q - 2], 2)
            for j in range(2):
                engine.wait_ge(high, 4 * q + 2 * j + 2)
                nc_engine.tensor_tensor(rem[:, p, j, :], exact[:, p, j, :], parts[:, p, j, 0, :], ALU.subtract).then_inc(left[q], 1)

        def third_parts(engine, nc_engine, q):
            p = q % 2
            for j in range(2):
                engine.wait_ge(middle[q], j + 1)
                nc_engine.tensor_tensor(parts[:, p, j, 2, :], rem[:, p, j, :], parts[:, p, j, 1, :], ALU.subtract).then_inc(low[q], 1)

        with nc.Block() as block:
            @block.sync
            def _(sp):
                def load(at):
                    heads = bass.ds(at.g * GH, GH)
                    for n in range(PARTS):
                        rows = slice(n * PARTS * DK, (n + 1) * PARTS * DK)
                        sp.dma_start(q2[at.buf][rows, :, :], dram["q_parts"][heads, :, :].rearrange("j r t -> r j t")).then_inc(loaded[at.buf], 16)
                        for m in range(PARTS):
                            row = (n * PARTS + m) * DK
                            sp.dma_start(k2[at.buf][row:row + DK, :, :],
                                         dram["k_parts"][heads, n * DK:(n + 1) * DK, :].rearrange("j d t -> d j t")).then_inc(loaded[at.buf], 16)

                def take_maxima(at):
                    rows = dram["m_rows"][at.buf, :, :, :]
                    sp.wait_ge(split, PARTS * at.g + PARTS)
                    sp.dma_start(rows, mpart[at.buf][:, :, :]).then_inc(in_m[at.buf], 16)
                    sp.wait_ge(in_m[at.buf], 32 * at.use + 16)
                    sp.dma_start(q2[at.buf][FILL:FILL + PARTS, :, :].rearrange("r j (t q) -> r (j t) q", q=P),
                                 rows.rearrange("a r q -> r a q")).then_inc(in_m[at.buf], 16)

                def body(at, first=False, finish=True, start=True):
                    if start and not first:
                        sp.wait_ge(step_done, STEPS * at.g)
                        load(at.ahead(2))
                    if finish:
                        take_maxima(at.ahead(1))

                def store(q):
                    b, t = q * QUAD // KT, q * QUAD % KT * P
                    sp.wait_ge(low[q], 2)
                    for j, key in enumerate(("q_parts", "k_parts")):
                        for n in range(PARTS):
                            sp.dma_start(dram[key][b * HEADS:(b + 1) * HEADS, n * DK:(n + 1) * DK, t:t + HALF],
                                         parts[:, q % 2, j, n, :]).then_inc(parts_stored[q % 2], 16)

                for q in range(QUADS):
                    sp.dma_start(w["x"][:, q * QUAD:(q + 1) * QUAD, :],
                                 dram["x_rows"][q * QUAD * P:(q + 1) * QUAD * P, :].rearrange("(t p) d -> p t d", p=P)).then_inc(x_loaded[q], 16)
                for q in range(2):
                    store(q)
                for p in range(2):
                    sp.wait_ge(parts_stored[p], 16 * 2 * PARTS)
                load(Body(0, 0, 0))
                store(2)
                load(Body(1, 1, 0))
                store(3)
                load(Body(2, 2, 0))
                for q in range(4, QUADS - 1):
                    store(q)
                take_maxima(Body(0, 0, 0))
                store(QUADS - 1)
                for p in range(2):
                    sp.wait_ge(parts_stored[p], 16 * 2 * PARTS * (QUADS // 2))
                bodies(sp, body)
                for p in range(BUFS):
                    sp.wait_ge(in_m[p], 32 * ((GROUPS - 1 - p) // BUFS + 1))

            @block.gpsimd
            def _(pool):
                def stage(at):
                    nc.gpsimd.tensor_copy(vs[at.buf][:, :, :, 0:DK],
                                          v_sb[:, bass.ds(at.g, 1), :, :].rearrange("p a t (j d) -> p (a t) j d", d=DK)).then_inc(in_v[at.buf], 1)

                def body(at, first=False, finish=True, start=True):
                    if start and not first:
                        pool.wait_ge(step_done, STEPS * at.g)
                        stage(at.ahead(2))

                pool.wait_ge(v_out, 2)
                for g in range(BUFS):
                    stage(Body(g, g, 0))
                for q in range(FIRST, QUADS):
                    remainders(pool, nc.gpsimd, q)
                    third_parts(pool, nc.gpsimd, q)
                pool.wait_ge(v_out, QUADS)
                bodies(pool, body)
                slot, used = place("o", 3 * GPB - 1)
                pool.wait_ge(unit_free[slot], used + 1)
                for q in range(MERGED):
                    gather_rows(pool, nc.gpsimd.tensor_copy, q)

            @block.tensor
            def _(pe):
                def maxima_unit(slot, buf, n):
                    qt, kh, pr = n // 4, n // 2 % 2, n % 2
                    for j in (2 * pr, 2 * pr + 1):
                        last = nc.tensor.matmul(ps_m[slot][:, j % 2, :], q2[buf][0:FILL, j, qt * P:(qt + 1) * P],
                                                k2[buf][0:FILL, j, kh * HALF:(kh + 1) * HALF], start=True, stop=True)
                    last.then_inc(unit_full[slot], 1)

                def turn_maxima(at, slot):
                    pe.wait_ge(combined, at.g + 1)
                    nc.tensor.transpose(ps_m[slot][0:GH * KT, 0, 0:P], top[:, :], w["ident"][:, :]).then_inc(unit_full[slot], 1)

                def turn_results(at, slot):
                    pe.wait_ge(o_out, 2 * at.g + 2)
                    for i in range(KT):
                        last = nc.tensor.transpose(ps_m[slot][:, i // QUAD, i % QUAD * P:(i % QUAD + 1) * P],
                                                   oT[:, i // QUAD, i % QUAD * P:(i % QUAD + 1) * P], w["ident"][:, :])
                    last.then_inc(unit_full[slot], 1)

                def do_unit(at, n, kind, ahead, which):
                    slot, used = at.unit(n)
                    of = at.ahead(ahead) if ahead > 0 else Body(at.g + ahead, None, None)
                    pe.wait_ge(unit_free[slot], used)
                    if kind == "max":
                        if which == 0:
                            pe.wait_ge(loaded[of.buf], 16 * LOADS * (of.use + 1))
                        maxima_unit(slot, of.buf, which)
                    elif kind == "m":
                        turn_maxima(of, slot)
                    elif kind == "o":
                        turn_results(of, slot)
                    elif kind == "c":
                        pe.wait_ge(in_rows, which + 1)
                        for i in range(QUAD):
                            last = nc.tensor.transpose(ps_m[slot][:, 0, i * P:(i + 1) * P], rows[:, which % 2, i, :], w["ident"][:, :])
                        last.then_inc(unit_full[slot], 1)
                    else:
                        turned, before = at.unit(n - 1)
                        pe.wait_ge(unit_free[turned], before + 1)
                        for i in range(QUAD):
                            last = nc.tensor.matmul(ps_m[slot][:, 0, i * P:(i + 1) * P], cT[:, which % 2, i * P:(i + 1) * P], w["Wo"][:, :],
                                                    start=True, stop=True)
                        last.then_inc(unit_full[slot], 1)

                def score(at, k, j):
                    u, kt, n = k // KT, k % KT, GH * k + j
                    if not (isinstance(at.g, int) and GH * STEPS * at.g + n < 3):
                        pe.wait_ge(exped, GH * STEPS * at.g + n - 2)
                    nc.tensor.matmul(ps_s[(n + at.buf) % 3][:, :], k2[at.buf][:, j, kt * P:(kt + 1) * P],
                                     q2[at.buf][:, j, u * HALF:(u + 1) * HALF], start=True, stop=True).then_inc(scored, 1)

                def values(at, k):
                    u, kt = k // KT, k % KT
                    if kt == 0:
                        wait_unless_zero(pe, o_out, 2 * at.g + u)
                    pe.wait_ge(exped, GH * STEPS * at.g + GH * (k + 1))
                    for j in range(GH):
                        last = nc.tensor.matmul(ps_o[32 * j:32 * (j + 1), :], vs[at.buf][:, kt, j, :], probs[:, k % 2, j, :],
                                                start=(kt == 0), stop=(kt == KT - 1))
                    last.then_inc(step_done, 1)

                def body(at, first=False, finish=True, start=True):
                    n = 0
                    pe.wait_ge(in_m[at.buf], 32 * (at.use + 1))
                    pe.wait_ge(in_v[at.buf], at.use + 1)
                    for k, units in enumerate(plan(first, finish, start)):
                        for j in range(GH):
                            score(at, k, j)
                            for unit in {0: units[0:1], 2: units[1:2]}.get(j, ()):
                                do_unit(at, n, *unit)
                                n += 1
                        if k >= 1:
                            values(at, k - 1)
                        elif not first:
                            values(Body(at.g - 1, (at.buf - 1) % BUFS, None), STEPS - 1)
                        for unit in units[2:]:
                            do_unit(at, n, *unit)
                            n += 1

                def turn(q):
                    pe.wait_ge(normed, q + 1)
                    wait_unless_zero(pe, t_out, q)
                    for i in range(QUAD):
                        last = nc.tensor.transpose(ps_t[:, i * P:(i + 1) * P], xn_sb[:, QUAD * q + i, :], w["ident"][:, :])
                    last.then_inc(t_full, 1)

                def project(kind, q):
                    p = q % 2
                    if kind == "query":
                        pe.wait_ge(t_out, q + 1)
                        wait_unless_zero(pe, high, 4 * q)
                    if kind == "value":
                        wait_unless_zero(pe, v_out, q)
                        for i in range(QUAD):
                            last = nc.tensor.matmul(ps_v[:, i * P:(i + 1) * P], xnT[:, p, i * P:(i + 1) * P], w["Wv"][:, :], start=True, stop=True)
                        last.then_inc(v_full, 1)
                    else:
                        bank, weights = (ps_q, w["Wq"]) if kind == "query" else (ps_k, w["Wk"])
                        nc.tensor.matmul(bank[:, :], weights[:, :], xnT[:, p, :], start=True, stop=True).then_inc(qk_full, 1)

                def first_unit(n):
                    if n >= 2:
                        pe.wait_ge(unit_free[n % 2], n // 2)
                    if n in (0, P1_UNITS + 1):
                        pe.wait_ge(loaded[min(n, 1)], 16 * LOADS)
                    if n < P1_UNITS:
                        maxima_unit(n % 2, 0, n)
                    elif n == P1_UNITS:
                        turn_maxima(Body(0, 0, 0), n % 2)
                    else:
                        maxima_unit(n % 2, 1, n - P1_UNITS - 1)

                for kind, n in prologue():
                    if kind == "unit":
                        first_unit(n)
                    elif kind == "turn":
                        turn(n)
                    else:
                        project(kind, n)
                pe.wait_ge(high, 4 * QUADS)
                pe.wait_ge(v_out, QUADS)
                bodies(pe, body)
                values(Body(GROUPS - 1, (GROUPS - 1) % BUFS, None), STEPS - 1)
                for n, unit in enumerate(last_units(), 1 + 2 * (MERGED - MERGED_14)):
                    do_unit(Body(GROUPS - 1, None, None), n, *unit)

            @block.scalar
            def _(act):
                def take_out(g, u):
                    act.wait_ge(step_done, STEPS * g + KT * (u + 1))
                    if u == 0:
                        wait_unless_zero(act, recip, g)
                    nc.scalar.activation(oT[:, u, :], ps_o[:, :], ACT.Copy).then_inc(o_out, 1)

                def body(at, first=False, finish=True, start=True):
                    for k in range(STEPS):
                        if not (first and k < 2):
                            act.wait_ge(step_done, STEPS * at.g + k - 1)
                        for j in range(GH):
                            n = GH * k + j
                            act.wait_ge(scored, GH * STEPS * at.g + n + 1)
                            nc.scalar.activation(probs[:, k % 2, j, :], ps_s[(n + at.buf) % 3][:, :], ACT.Exp, scale=SCALE).then_inc(exped, 1)
                            if j == 0 and k == 1 and not first:
                                take_out(at.g - 1, 1)
                            if j == 0 and k == KT + 1:
                                take_out(at.g, 0)
                        if k == STEPS - 3 and not finish:
                            layernorm(nc, None, act, w["x"], xn_next, stats, mv, rt, normed_2, vstep_2, astep_2, "act", span=(0, MERGED * QUAD))

                def turned(q):
                    act.wait_ge(t_full, q + 1)
                    if q >= 2:
                        act.wait_ge(v_full, q - 1)
                    nc.scalar.activation(xnT[:, q % 2, :], ps_t[:, :], ACT.Copy).then_inc(t_out, 1)

                def first_parts(q):
                    p = q % 2
                    if q >= 2:
                        act.wait_ge(left[q - 2], 2)
                        act.wait_ge(parts_stored[p], 16 * 2 * PARTS * (q // 2))
                    for j, (bank, bias) in enumerate(((ps_q, w["bq"]), (ps_k, w["bk"]))):
                        act.wait_ge(qk_full, 2 * q + j + 1)
                        nc.scalar.activation(exact[:, p, j, :], bank[:, :], ACT.Identity, bias=bias[:, 0:1]).then_inc(high, 1)
                        nc.scalar.activation(parts[:, p, j, 0, :], bank[:, :], ACT.Identity, bias=bias[:, 0:1]).then_inc(high, 1)

                def second_parts(q):
                    for j in range(2):
                        act.wait_ge(left[q], j + 1)
                        nc.scalar.activation(parts[:, q % 2, j, 1, :], rem[:, q % 2, j, :], ACT.Copy).then_inc(middle[q], 1)

                layernorm(nc, None, act, w["x"], xn_sb, stats, mv, rt, normed, vstep, astep, "act", span=(0, FIRST * QUAD))
                for kind, q in prologue():
                    if kind == "turn":
                        if q == FIRST:
                            layernorm(nc, None, act, w["x"], xn_sb, stats, mv, rt, normed, vstep, astep, "act",
                                      span=(FIRST * QUAD, TILES), before=1)
                        turned(q)
                    elif kind == "key":
                        first_parts(q)
                        second_parts(q)
                for q in (QUADS - 2, QUADS - 1):
                    act.wait_ge(low[q], 2)
                bodies(act, body)
                take_out(GROUPS - 1, 1)
                slot, used = place("o", GROUPS - 1)
                act.wait_ge(unit_free[slot], used + 1)
                for q in range(MERGED, QUADS):
                    gather_rows(act, nc.scalar.copy, q)

            @block.vector
            def _(dve):
                def maxima_unit(slot, used, n):
                    qt, kh, pr = n // 4, n // 2 % 2, n % 2
                    dve.wait_ge(unit_full[slot], used + 1)
                    nc.vector.tensor_reduce(maxima[:, 2 * pr:2 * pr + 2, qt, kh], ps_m[slot][:, :, :], AX.X, ALU.max).then_inc(unit_free[slot], 1)

                def combine(at, slot, used):
                    dve.wait_ge(unit_free[slot], used)
                    dve.wait_ge(unit_free[1 - slot], used + slot)
                    nc.vector.tensor_reduce(top[:, :], maxima[:, :, :, :].rearrange("p j t h -> p (j t) h"), AX.X, ALU.max).then_inc(combined, 1)
                    dve.wait_ge(combined, at.g + 1)

                def split_unit(at, slot, used):
                    dve.wait_ge(unit_full[slot], used + 1)
                    src, part = ps_m[slot][0:GH * KT, 0, 0:P], mpart[at.buf]
                    nc.vector.tensor_scalar(part[:, 0, :], src, -1.0, None, ALU.mult).then_inc(split, 1)
                    dve.wait_ge(split, PARTS * at.g + 1)
                    nc.vector.scalar_tensor_tensor(out=mrest[:, :], in0=src, scalar=-1.0, in1=part[:, 0, :],
                                                   op0=ALU.mult, op1=ALU.subtract).then_inc(unit_free[slot], 1)
                    dve.wait_ge(unit_free[slot], used + 1)
                    nc.vector.tensor_copy(part[:, 1, :], mrest[:, :]).then_inc(split, 1)
                    dve.wait_ge(split, PARTS * at.g + 2)
                    nc.vector.tensor_tensor(part[:, 2, :], mrest[:, :], part[:, 1, :], ALU.subtract).then_inc(split, 1)

                def result_unit(g, slot, used):
                    dve.wait_ge(unit_full[slot], used + 1)
                    src = ps_m[slot][:, :, :].rearrange("p u (i j c) -> p (u i) j c", i=QUAD, j=GH)
                    nc.vector.reciprocal(rden[:, :, :, :], src[:, :, :, DK:DK + 1]).then_inc(recip, 1)
                    dve.wait_ge(recip, g + 1)
                    nc.vector.tensor_tensor(ctx_sb[:, bass.ds(g, 1), :, :].rearrange("p a t (j d) -> p (a t) j d", d=DK),
                                            src[:, :, :, 0:DK], rden[:, :, :, :].to_broadcast([P, KT, GH, DK]),
                                            ALU.mult).then_inc(unit_free[slot], 1)

                def do_unit(at, n, kind, ahead, which):
                    slot, used = at.unit(n)
                    if kind == "max":
                        maxima_unit(slot, used, which)
                        if which == P1_UNITS - 1:
                            combine(at.ahead(ahead), *at.unit(n + 1))
                    elif kind == "m":
                        split_unit(at.ahead(ahead), slot, used)
                    elif kind == "o":
                        result_unit(at.g + ahead, slot, used)
                    elif kind == "c":
                        dve.wait_ge(unit_full[slot], used + 1)
                        nc.vector.tensor_copy(cT[:, which % 2, :], ps_m[slot][:, 0, :]).then_inc(unit_free[slot], 1)
                    else:
                        add_output(which, slot, used)

                def add_output(q, slot, used):
                    p, tiles = q % 2, slice(q * QUAD, (q + 1) * QUAD)
                    dve.wait_ge(unit_full[slot], used + 1)
                    nc.vector.tensor_tensor(plus_bo[:, p, :, :], ps_m[slot][:, 0, :].rearrange("p (t d) -> p t d", d=D),
                                            w["bo"][:, :].unsqueeze(1).to_broadcast([P, QUAD, D]), ALU.add).then_inc(unit_free[slot], 1)
                    dve.wait_ge(unit_free[slot], used + 1)
                    nc.vector.tensor_tensor(w["x"][:, tiles, :], w["x"][:, tiles, :], plus_bo[:, p, :, :], ALU.add).then_inc(residual, 1)
                    if q < MERGED:
                        dve.wait_ge(residual, q + 1)
                        for t in range(q * QUAD, (q + 1) * QUAD):
                            last = nc.vector.bn_stats(stats[:, t, :], w["x"][:, t, :])
                        if q == MERGED - 1:
                            last.then_inc(vstep_2, 1)

                def body(at, first=False, finish=True, start=True):
                    units = [unit for units in plan(first, finish, start) for unit in units]
                    for n, (kind, ahead, which) in enumerate(units):
                        do_unit(at, n, kind, ahead, which)

                def arrive(q):
                    for work in between.get(q, ()):
                        work()
                    dve.wait_ge(x_loaded[q], 16)

                def values(q):
                    dve.wait_ge(v_full, q + 1)
                    b, t = q * QUAD // KT, q * QUAD % KT
                    nc.vector.tensor_tensor(v_sb[:, b * GPB:(b + 1) * GPB, t:t + QUAD, :].rearrange("p g t c -> p t g c"),
                                            ps_v[:, :].rearrange("p (t g c) -> p t g c", t=QUAD, g=GPB),
                                            w["bv"][:, :].rearrange("p (g c) -> p g c", g=GPB).unsqueeze(1).to_broadcast([P, QUAD, GPB, GH * DK]),
                                            ALU.add).then_inc(v_out, 1)

                between = {4: [lambda: remainders(dve, nc.vector, 0)],
                           5: [lambda: values(0), lambda: third_parts(dve, nc.vector, 0)],
                           6: [lambda: remainders(dve, nc.vector, 1), lambda: values(1)],
                           7: [lambda: third_parts(dve, nc.vector, 1)]}
                layernorm(nc, dve, None, w["x"], xn_sb, stats, mv, rt, normed, vstep, astep, "dve", arrive, span=(0, FIRST * QUAD))
                layernorm(nc, dve, None, w["x"], xn_sb, stats, mv, rt, normed, vstep, astep, "dve", arrive,
                          span=(FIRST * QUAD, TILES), before=1)
                late = []
                for kind, n in prologue():
                    if kind == "value":
                        if FIRST <= n < EARLY:
                            values(n)
                        elif n >= EARLY:
                            late.append(n)
                    elif kind == "unit":
                        if n < P1_UNITS:
                            maxima_unit(n % 2, n // 2, n)
                        elif n == P1_UNITS:
                            combine(Body(0, 0, 0), n % 2, n // 2)
                            split_unit(Body(0, 0, 0), n % 2, n // 2)
                        else:
                            maxima_unit(n % 2, n // 2, n - P1_UNITS - 1)
                        while late:
                            values(late.pop())
                bodies(dve, body)
                layernorm(nc, dve, None, w["x"], xn_next, stats, mv, rt, normed_2, vstep_2, astep_2, "dve", span=(0, MERGED * QUAD), counted=True)
                for n, unit in enumerate(last_units(), 1 + 2 * (MERGED - MERGED_14)):
                    do_unit(Body(GROUPS - 1, None, None), n, *unit)


def layer(nc, dram, out):
    with ExitStack() as ctx:
        def sb(name, shape, dt):
            return ctx.enter_context(nc.sbuf_tensor(name, shape, dt))

        w = {
            "x": sb("x", [P, TILES, D], F32),
            "W1": sb("W1", [P, EXPERTS, HID + HC], F32), "W2": sb("W2", [P, EXPERTS, HC, D], F32),
            "rest": sb("rest", [P, EXPERTS, D], F32),
            "Wr": sb("Wr", [P, 32], F32), "br": sb("br", [P, EXPERTS], F32),
            "Wq": sb("Wq", [P, D], F32), "Wk": sb("Wk", [P, D], F32), "Wv": sb("Wv", [P, D], F32), "Wo": sb("Wo", [P, D], F32),
            "bq": sb("bq", [P, 1], F32), "bk": sb("bk", [P, 1], F32), "bv": sb("bv", [P, D], F32), "bo": sb("bo", [P, D], F32),
            "ident": sb("ident", [P, P], F32), "before": sb("before", [P, P], BF16), "ones": sb("ones", [P, P], BF16),
            "iota": sb("iota", [P, P], F32), "iota_b": sb("iota_b", [P, P], BF16), "partition": sb("partition", [P, 1], F32), "rank8": sb("rank8", [P, EXPERTS], F32),
            "seg": sb("seg", [P, EXPERTS, TILES], F32),
        }
        q2, k2 = ([sb(f"{n}{p}", [P, GH, SEQ], BF16) for p in range(BUFS)] for n in ("q2_", "k2_"))
        vs = [sb(f"vs{p}", [P, KT, GH, 32], F32) for p in range(BUFS)]
        v_sb = sb("v_sb", [P, GROUPS, KT, GH * DK], F32)
        xn_sb = v_sb[:, :, :, :].rearrange("p g t c -> p (g t c)").rearrange("p (t d) -> p t d", d=D)
        ffn(nc, w, dram, "_1", xn_sb, None, operands=(q2, k2, vs))
        with nc.sbuf_tensor("ctx_sb", [P, GROUPS, KT, GH * DK], F32) as ctx_sb:
            attention(nc, w, dram, q2, k2, vs, v_sb, ctx_sb)
        ffn(nc, w, dram, "_2", xn_sb, out, ready=MERGED)


_INS = ["L0_attn_x", "L0_attn_Wq", "L0_attn_bq", "L0_attn_Wk", "L0_attn_bk", "L0_attn_Wv", "L0_attn_bv", "L0_attn_Wo", "L0_attn_bo",
        "L0_ffn_W1", "L0_ffn_b1", "L0_ffn_W2", "L0_ffn_b2", "L0_ffn_Wr", "L0_ffn_br"]


def kernel(**inputs):
    import numpy as np
    import concourse.bacc as bacc
    from concourse.bass_utils import run_bass_kernel_spmd

    nc = bacc.Bacc("TRN2", target_bir_lowering=False, num_devices=1)
    arrays, dram = {}, {}
    for name in _INS:
        arrays[name] = np.ascontiguousarray(inputs[name])
        dram[name] = nc.dram_tensor(name, arrays[name].shape, F32, kind="ExternalInput").ap()
    dram["token_rows"] = nc.dram_tensor("token_rows", [TOKENS, 2 * D], F32).ap()
    dram["x_rows"] = nc.dram_tensor("x_rows", [TOKENS, D], F32).ap()
    dram["q_parts"] = nc.dram_tensor("q_parts", [BATCH * HEADS, PARTS * DK, SEQ], BF16).ap()
    dram["k_parts"] = nc.dram_tensor("k_parts", [BATCH * HEADS, PARTS * DK, SEQ], BF16).ap()
    dram["m_rows"] = nc.dram_tensor("m_rows", [BUFS, GH * KT, PARTS, P], BF16).ap()
    out = nc.dram_tensor("out", [BATCH, SEQ, D], F32, kind="ExternalOutput").ap()
    layer(nc, dram, out)
    results = run_bass_kernel_spmd(nc, [arrays], core_ids=[0])
    return results.results[0]["out"]
```
